# Optimizing a Trainium2 kernel written in Bass

```python
import numpy as np
import jax
import jax.numpy as jnp

def _softmax(x, axis=-1):
    return jax.nn.softmax(x, axis=axis)

def _gelu(x):
    return jax.nn.gelu(x, approximate=True)

def _silu(x):
    return jax.nn.silu(x)

def _sigmoid(x):
    return jax.nn.sigmoid(x)

def _layernorm(x, axis=-1, eps=1e-05):
    m = jnp.mean(x, axis=axis, keepdims=True)
    v = jnp.var(x, axis=axis, keepdims=True)
    return (x - m) / jnp.sqrt(v + eps)

def _scatter_add(tgt, idx, src, axis=0):
    return tgt.at[idx].add(src)

def _segment_sum(src, seg, n):
    return jax.ops.segment_sum(src, seg, n)
kernel_name = 'mk_macaron_d2_jaxref_r4_461364'

def setup_inputs(seed: int=0):
    np.random.seed(seed)
    _w = jnp.asarray

    def _L0_attn_setup():
        import jax, jax.numpy as jnp
        import numpy as np
        HIDDEN = 512
        HEADS = 16
        HEAD_DIM = HIDDEN // HEADS
        SCALE = 1.0 / float(np.sqrt(HEAD_DIM))
        B, S = (2, 512)
        key = jax.random.key(seed)
        ks = jax.random.split(key, 5)
        return {'x': jax.random.normal(ks[0], (B, S, HIDDEN), dtype=jnp.float32), 'q_w': jax.random.normal(ks[1], (HIDDEN, HIDDEN), dtype=jnp.float32) * HIDDEN ** (-0.5), 'k_w': jax.random.normal(ks[2], (HEAD_DIM, HIDDEN), dtype=jnp.float32) * HIDDEN ** (-0.5), 'v_w': jax.random.normal(ks[3], (HEAD_DIM, HIDDEN), dtype=jnp.float32) * HIDDEN ** (-0.5), 'o_w': jax.random.normal(ks[4], (HIDDEN, HIDDEN), dtype=jnp.float32) * HIDDEN ** (-0.5)}
    _L0_attn_in = _L0_attn_setup()

    def _L0_ffn_setup():
        import jax, jax.numpy as jnp
        import numpy as np
        TOP_K = 2
        key = jax.random.key(seed)
        ks = jax.random.split(key, 4)
        G, S, F, E, H = (4, 512, 512, 8, 512)
        return {'x': jax.random.normal(ks[0], (G, S, F), dtype=jnp.float32), 'router_logits': jax.random.normal(ks[1], (F, E), dtype=jnp.float32) * 0.02, 'gating_einsum': jax.random.normal(ks[2], (E, 2, H, F), dtype=jnp.float32) * 0.02, 'linear': jax.random.normal(ks[3], (E, H, F), dtype=jnp.float32) * 0.02, 'per_expert_scale': jnp.ones((E,), dtype=jnp.float32), 'router_scale': jnp.ones((F,), dtype=jnp.float32)}
    _L0_ffn_in = _L0_ffn_setup()

    def _L1_attn_setup():
        import jax, jax.numpy as jnp
        import numpy as np
        B, S, D = (4, 1024, 512)
        IDENTITY_WEIGHT = 0.5
        ROT_DIM = D // 2

        def _layernorm(x, gamma, beta, eps=1e-05):
            mu = jnp.mean(x, axis=-1, keepdims=True)
            var = jnp.var(x, axis=-1, keepdims=True)
            return (x - mu) * jax.lax.rsqrt(var + eps) * gamma + beta

        def _rotary(t, rot_dim, theta=10000.0):
            seq = t.shape[-2]
            inv_freq = 1.0 / theta ** (jnp.arange(0, rot_dim, 2, dtype=jnp.float32) / rot_dim)
            freqs = jnp.arange(seq, dtype=jnp.float32)[:, None] * inv_freq[None, :]
            freqs = jnp.repeat(freqs, 2, axis=-1)
            cos, sin = (jnp.cos(freqs), jnp.sin(freqs))
            t_rot, t_pass = (t[..., :rot_dim], t[..., rot_dim:])
            x1, x2 = (t_rot[..., 0::2], t_rot[..., 1::2])
            rot_half = jnp.stack([-x2, x1], axis=-1).reshape(t_rot.shape)
            return jnp.concatenate([t_rot * cos + rot_half * sin, t_pass], axis=-1)

        def _cos_sim(x):
            return x / jnp.linalg.norm(x, axis=-1, keepdims=True)
        key = jax.random.key(seed)
        ks = jax.random.split(key, 3)
        scale = 0.02
        return {'X': jax.random.normal(ks[0], (B, S, D), jnp.float32), 'W_in': jax.random.normal(ks[1], (D, 3 * D), jnp.float32) * scale, 'b_in': jnp.zeros((3 * D,), jnp.float32), 'W_out': jax.random.normal(ks[2], (D, D), jnp.float32) * scale, 'b_out': jnp.zeros((D,), jnp.float32), 'gamma': jnp.ones((D,), jnp.float32), 'beta': jnp.zeros((D,), jnp.float32)}
    _L1_attn_in = _L1_attn_setup()

    def _L1_ffn_setup():
        import jax, jax.numpy as jnp
        import numpy as np
        HIDDEN = 512
        INTER = 1408
        B, S = (2, 512)

        def _ternary(key, shape):
            return jax.random.randint(key, shape, -1, 2).astype(jnp.float32)
        key = jax.random.key(seed)
        ks = jax.random.split(key, 7)
        x = jax.random.normal(ks[0], (B, S, HIDDEN), dtype=jnp.float32)
        gate_w = _ternary(ks[1], (INTER, HIDDEN))
        up_w = _ternary(ks[2], (INTER, HIDDEN))
        down_w = _ternary(ks[3], (HIDDEN, INTER))
        gate_s = jax.random.uniform(ks[4], (INTER,), minval=0.01, maxval=0.1, dtype=jnp.float32)
        up_s = jax.random.uniform(ks[5], (INTER,), minval=0.01, maxval=0.1, dtype=jnp.float32)
        down_s = jax.random.uniform(ks[6], (HIDDEN,), minval=0.01, maxval=0.1, dtype=jnp.float32)
        return {'x': x, 'gate_w': gate_w, 'up_w': up_w, 'down_w': down_w, 'gate_s': gate_s, 'up_s': up_s, 'down_s': down_s}
    _L1_ffn_in = _L1_ffn_setup()
    _d = {'L0_attn_x': _L0_attn_in['x'], 'L0_attn_q_w': _L0_attn_in['q_w'], 'L0_attn_k_w': _L0_attn_in['k_w'], 'L0_attn_v_w': _L0_attn_in['v_w'], 'L0_attn_o_w': _L0_attn_in['o_w'], 'L0_ffn_router_logits': _L0_ffn_in['router_logits'], 'L0_ffn_gating_einsum': _L0_ffn_in['gating_einsum'], 'L0_ffn_linear': _L0_ffn_in['linear'], 'L0_ffn_per_expert_scale': _L0_ffn_in['per_expert_scale'], 'L0_ffn_router_scale': _L0_ffn_in['router_scale'], 'L1_attn_W_in': _L1_attn_in['W_in'], 'L1_attn_b_in': _L1_attn_in['b_in'], 'L1_attn_W_out': _L1_attn_in['W_out'], 'L1_attn_b_out': _L1_attn_in['b_out'], 'L1_attn_gamma': _L1_attn_in['gamma'], 'L1_attn_beta': _L1_attn_in['beta'], 'L1_ffn_gate_w': _L1_ffn_in['gate_w'], 'L1_ffn_up_w': _L1_ffn_in['up_w'], 'L1_ffn_down_w': _L1_ffn_in['down_w'], 'L1_ffn_gate_s': _L1_ffn_in['gate_s'], 'L1_ffn_up_s': _L1_ffn_in['up_s'], 'L1_ffn_down_s': _L1_ffn_in['down_s']}
    _x0 = _d['L0_attn_x']
    _d['L0_attn_x'] = jax.random.normal(jax.random.fold_in(jax.random.key(seed), 1), (2, 2048, 512), dtype=_x0.dtype)
    del _x0
    return _d

def reference(L0_attn_x, L0_attn_q_w, L0_attn_k_w, L0_attn_v_w, L0_attn_o_w, L0_ffn_router_logits, L0_ffn_gating_einsum, L0_ffn_linear, L0_ffn_per_expert_scale, L0_ffn_router_scale, L1_attn_W_in, L1_attn_b_in, L1_attn_W_out, L1_attn_b_out, L1_attn_gamma, L1_attn_beta, L1_ffn_gate_w, L1_ffn_up_w, L1_ffn_down_w, L1_ffn_gate_s, L1_ffn_up_s, L1_ffn_down_s):

    def _L0_attn_ref(x, q_w, k_w, v_w, o_w):
        import jax, jax.numpy as jnp
        import numpy as np
        HIDDEN = 512
        HEADS = 16
        HEAD_DIM = HIDDEN // HEADS
        SCALE = 1.0 / float(np.sqrt(HEAD_DIM))
        B, S = (2, 512)
        b, s, _ = x.shape
        q = (x @ q_w.T).reshape(b, s, HEADS, HEAD_DIM).transpose(0, 2, 1, 3)
        k = x @ k_w.T
        v = x @ v_w.T
        scores = jnp.einsum('bhqd,bkd->bhqk', q, k) * SCALE
        attn = jax.nn.softmax(scores.astype(jnp.float32), axis=-1).astype(q.dtype)
        out = jnp.einsum('bhqk,bkd->bhqd', attn, v)
        out = out.transpose(0, 2, 1, 3).reshape(b, s, HIDDEN)
        return out @ o_w.T

    def _L0_ffn_ref(x, router_logits, gating_einsum, linear, per_expert_scale, router_scale):
        import jax, jax.numpy as jnp
        import numpy as np
        TOP_K = 2
        G, S, F = x.shape
        E = router_logits.shape[-1]
        H = linear.shape[1]
        k = TOP_K
        dtype = x.dtype
        var = jnp.mean(jnp.square(x.astype(jnp.float32)), axis=-1, keepdims=True)
        router_input = x * jax.lax.rsqrt(var + 1e-06).astype(dtype)
        root_size = jax.lax.rsqrt(jnp.array(F, dtype=dtype))
        router_input = router_input * root_size * router_scale.astype(dtype)
        logits = jnp.einsum('gsd,de->gse', router_input, router_logits.astype(dtype))
        logits32 = logits.astype(jnp.float32)
        probs = jax.nn.softmax(logits32, axis=-1)
        _, choices = jax.lax.approx_max_k(logits32, k=k)
        indicator = jax.nn.one_hot(choices, E, dtype=probs.dtype).sum(axis=-2)
        renorm = jnp.sum(indicator * probs, axis=-1, keepdims=True)
        renorm = jnp.where(renorm > 0.0, renorm, 1.0)
        weights = probs / renorm
        x_flat = x.reshape((-1, F))
        batch_size = G * S
        choices_flat = choices.ravel()
        xs_order = choices_flat.argsort()
        xs_reverse_argsort = xs_order.argsort()
        xs_indices = jnp.repeat(jnp.arange(batch_size), k)[xs_order]
        sorted_xs = x_flat[xs_indices, :]
        choices_oh = jax.nn.one_hot(choices, num_classes=E, dtype=jnp.int32)
        tokens_per_expert = jnp.sum(choices_oh, axis=(0, 1, 2))
        combine_weights = (choices_oh.astype(jnp.float32) * jnp.expand_dims(weights, axis=2)).sum(axis=-1).astype(weights.dtype)
        w_gate = jnp.transpose(gating_einsum, (0, 3, 1, 2)).reshape(E, F, 2 * H)
        gate_out = jax.lax.ragged_dot(sorted_xs, w_gate.astype(dtype), group_sizes=tokens_per_expert)
        gate_out = gate_out.reshape(gate_out.shape[0], 2, H)
        activation = jax.nn.gelu(gate_out[:, 0, :]) * gate_out[:, 1, :]
        expert_outputs = jax.lax.ragged_dot(activation, linear.astype(dtype), group_sizes=tokens_per_expert)
        expert_indices = jnp.repeat(jnp.arange(E), tokens_per_expert, total_repeat_length=expert_outputs.shape[0])
        expert_outputs = expert_outputs * per_expert_scale.astype(expert_outputs.dtype)[expert_indices, None]
        out = expert_outputs[xs_reverse_argsort].reshape((G, S, k, -1))
        out = jnp.einsum('blkd,blk->bld', out, combine_weights, preferred_element_type=out.dtype)
        return out

    def _L1_attn_ref(X, W_in, b_in, W_out, b_out, gamma, beta):
        import jax, jax.numpy as jnp
        import numpy as np
        B, S, D = (4, 1024, 512)
        IDENTITY_WEIGHT = 0.5
        ROT_DIM = D // 2

        def _layernorm(x, gamma, beta, eps=1e-05):
            mu = jnp.mean(x, axis=-1, keepdims=True)
            var = jnp.var(x, axis=-1, keepdims=True)
            return (x - mu) * jax.lax.rsqrt(var + eps) * gamma + beta

        def _rotary(t, rot_dim, theta=10000.0):
            seq = t.shape[-2]
            inv_freq = 1.0 / theta ** (jnp.arange(0, rot_dim, 2, dtype=jnp.float32) / rot_dim)
            freqs = jnp.arange(seq, dtype=jnp.float32)[:, None] * inv_freq[None, :]
            freqs = jnp.repeat(freqs, 2, axis=-1)
            cos, sin = (jnp.cos(freqs), jnp.sin(freqs))
            t_rot, t_pass = (t[..., :rot_dim], t[..., rot_dim:])
            x1, x2 = (t_rot[..., 0::2], t_rot[..., 1::2])
            rot_half = jnp.stack([-x2, x1], axis=-1).reshape(t_rot.shape)
            return jnp.concatenate([t_rot * cos + rot_half * sin, t_pass], axis=-1)

        def _cos_sim(x):
            return x / jnp.linalg.norm(x, axis=-1, keepdims=True)
        Xn = _layernorm(X, gamma, beta)
        QKV = Xn @ W_in + b_in
        Q, K, V = jnp.split(QKV, 3, axis=-1)
        K = _rotary(K, ROT_DIM)
        V = _rotary(V, ROT_DIM)
        A = jnp.sum(_cos_sim(K) * _cos_sim(V), axis=-2)
        A = (1.0 - IDENTITY_WEIGHT) * A + IDENTITY_WEIGHT
        Y = A[:, None, :] * Q
        Y = Y @ W_out + b_out
        return Y + X

    def _L1_ffn_ref(x, gate_w, up_w, down_w, gate_s, up_s, down_s):
        import jax, jax.numpy as jnp
        import numpy as np
        HIDDEN = 512
        INTER = 1408
        B, S = (2, 512)

        def _ternary(key, shape):
            return jax.random.randint(key, shape, -1, 2).astype(jnp.float32)
        b, s, h = x.shape
        xf = x.reshape(b * s, h)
        g = jnp.einsum('th,ih->ti', xf, gate_w) * gate_s
        u = jnp.einsum('th,ih->ti', xf, up_w) * up_s
        hdn = jax.nn.silu(g) * u
        out = jnp.einsum('ti,hi->th', hdn, down_w) * down_s
        return out.reshape(b, s, -1)
    x = L0_attn_x
    x = x + 0.5 * _L0_ffn_ref(_layernorm(x, axis=-1), L0_ffn_router_logits, L0_ffn_gating_einsum, L0_ffn_linear, L0_ffn_per_expert_scale, L0_ffn_router_scale)
    x = x + _L0_attn_ref(_layernorm(x, axis=-1), L0_attn_q_w, L0_attn_k_w, L0_attn_v_w, L0_attn_o_w)
    x = x + 0.5 * _L0_ffn_ref(_layernorm(x, axis=-1), L0_ffn_router_logits, L0_ffn_gating_einsum, L0_ffn_linear, L0_ffn_per_expert_scale, L0_ffn_router_scale)
    x = x + 0.5 * _L1_ffn_ref(_layernorm(x, axis=-1), L1_ffn_gate_w, L1_ffn_up_w, L1_ffn_down_w, L1_ffn_gate_s, L1_ffn_up_s, L1_ffn_down_s)
    x = x + _L1_attn_ref(_layernorm(x, axis=-1), L1_attn_W_in, L1_attn_b_in, L1_attn_W_out, L1_attn_b_out, L1_attn_gamma, L1_attn_beta)
    x = x + 0.5 * _L1_ffn_ref(_layernorm(x, axis=-1), L1_ffn_gate_w, L1_ffn_up_w, L1_ffn_down_w, L1_ffn_gate_s, L1_ffn_up_s, L1_ffn_down_s)
    return x

_drawn_inputs = setup_inputs


def setup_inputs(seed=0):
    import zlib

    import numpy as np

    out = dict(_drawn_inputs(seed))
    spreads = {'L0_ffn_per_expert_scale': (1.0, 0.6),
     'L0_ffn_router_scale': (1.0, 0.6),
     'L1_attn_b_in': (0.0, 0.614),
     'L1_attn_b_out': (0.0, 0.1),
     'L1_attn_gamma': (1.0, 0.6),
     'L1_attn_beta': (0.0, 0.8)}
    factors = {}
    for name, (base, spread) in spreads.items():
        noise = np.random.default_rng([zlib.crc32(name.encode()), seed]).standard_normal(out[name].shape)
        drawn = base * np.exp(spread * noise) if base else spread * noise
        out[name] = jnp.asarray(drawn.astype(out[name].dtype))
    for name, factor in factors.items():
        out[name] = (out[name] * factor).astype(out[name].dtype)
    return out
```

```python
from contextlib import ExitStack

import concourse.bass as bass
from concourse import mybir

F32 = mybir.dt.float32
F32R = mybir.dt.float32r
I32 = mybir.dt.int32
U32 = mybir.dt.uint32
ALU = mybir.AluOpType
ACT = mybir.ActivationFunctionType
AX = mybir.AxisListType

P = 128
B, S, D = 2, 2048, 512
T = B * S
NT = T // P
DC = D // P
E, H = 8, 512
TOPK = 2
SLOT_TILES = T * TOPK // P + E
SLOTS = SLOT_TILES * P
LEVELS = T // P
HEADS, HD = 16, 32
INTER = 1408
IC = INTER // P
ROT = D // 2
LN_EPS = 1e-5
RMS_EPS = 1e-6
WPIECES = 6
WPIECE = 2 * H


class Memory:

    def __init__(self, nc, ctx, stage):
        self.nc, self.ctx, self.stage = nc, ctx, stage
        self.sems_held = []
        ctx.callback(self.zero_sems)

    def sb(self, name, shape, dt=F32):
        return self.ctx.enter_context(self.nc.sbuf_tensor(f"{self.stage}_{name}", shape, dt))

    def ps(self, name, shape, dt=F32):
        return self.ctx.enter_context(self.nc.psum_tensor(f"{self.stage}_{name}_ps", shape, dt))

    def sem(self, name):
        handle = self.nc.alloc_semaphore(f"{self.stage}_{name}_sem")
        self.sems_held.append(handle)
        return handle

    def zero_sems(self):
        if self.sems_held:
            self.nc.clear_and_free_semaphores(self.sems_held)
            self.nc.all_engine_barrier()

    def sems(self, name, n):
        return [self.sem(f"{name}{k}") for k in range(n)]


def looped(eng, n, unroll, step):
    rounds = n // unroll
    with eng.Fori(0, rounds - 1) as i:
        for k in range(unroll):
            step(i * unroll + k, k, i, False)
    for k in range(unroll):
        step((rounds - 1) * unroll + k, k, rounds - 1, True)


def spread(ap, n, axis=2):
    wide = ap.unsqueeze(axis)
    shape = list(wide.shape)
    shape[axis] = n
    return wide.to_broadcast(shape)


def setup_stage(nc, const):
    with ExitStack() as ctx:
        mem = Memory(nc, ctx, "setup")
        filled, picked = mem.sem("filled"), mem.sem("picked")
        block = ctx.enter_context(nc.Block())

        @block.gpsimd
        def _(pool):
            pool.memset(const["ident"][:], 0.0).then_inc(filled, 1)
            pool.memset(const["before"][:], 1.0).then_inc(filled, 1)
            pool.memset(const["ones"][:], 1.0).then_inc(filled, 1)
            pool.memset(const["eps"][:], LN_EPS).then_inc(filled, 1)
            pool.wait_ge(filled, 4)
            pool.affine_select(out=const["ident"][:], in_=const["ident"][:], compare_op=ALU.not_equal, fill=1.0,
                               base=0, pattern=[[-1, P]], channel_multiplier=1).then_inc(picked, 1)
            pool.affine_select(out=const["before"][:], in_=const["before"][:], compare_op=ALU.is_gt, fill=0.0,
                               base=0, pattern=[[1, P]], channel_multiplier=-1).then_inc(picked, 1)
            pool.wait_ge(picked, 2)


def routing_stage(nc, stage, const, x, scale, logits_w, expert_scale, xs, plan, clear):
    with ExitStack() as ctx:
        mem = Memory(nc, ctx, stage)
        xb = mem.sb("xb", [P, 2, D])
        y = mem.sb("y", [P, NT, D])
        yb = mem.sb("yb", [P, 2, D])
        yT = mem.sb("yT", [P, 2, D])
        bn = mem.sb("bn", [P, 2, 6])
        mv = mem.sb("mv", [P, 2, 2])
        var = mem.sb("var", [P, NT])
        sd = mem.sb("sd", [P, NT])
        rstd = mem.sb("rstd", [P, NT])
        wl = mem.sb("wl", [P, DC, E])
        rs = mem.sb("rs", [P, DC])
        wr = mem.sb("wr", [P, DC, E])
        esc = mem.sb("esc", [P, E])
        zero = mem.sb("zero", [P, 4 * D])
        small = {n: mem.sb(n, [P, NT]) for n in
                 ("ms", "msd", "rr", "top1", "top2", "at1", "at2", "gap", "egap", "den", "w1", "w2", "s1", "s2", "c1", "c2", "p1", "p2")}
        wide = {n: mem.sb(n, [P, NT, E]) for n in
                ("lg", "eq", "cand", "oh1", "oh2", "left", "both", "tot", "sumA", "sumB", "pos", "tmp", "tmp2")}
        iota_e = mem.sb("iota_e", [P, E])
        iota_e8 = mem.sb("iota_e8", [P, E])
        levels = mem.sb("levels", [P, E, LEVELS])
        over = mem.sb("over", [P, E, LEVELS])
        tiles = mem.sb("tiles", [P, E])
        endA = mem.sb("endA", [P, E])
        endB = mem.sb("endB", [P, E])
        base = mem.sb("base", [P, E])
        jota = mem.sb("jota", [1, SLOT_TILES, E])
        flip = mem.sb("flip", [1, E])
        upto = mem.sb("upto", [1, E])
        past = mem.sb("past", [1, SLOT_TILES, E])
        past2 = mem.sb("past2", [1, SLOT_TILES, E])
        tabf = mem.sb("tabf", [1, 2, SLOT_TILES])
        relf = mem.sb("relf", [1, E])
        tr = mem.ps("tr", [P, 2, D])
        lg_ps = mem.ps("lg", [P, NT, E])
        pre_ps = mem.ps("pre", [P, NT, E])
        tot_ps = mem.ps("tot", [P, NT, E])

        x_in = mem.sems("x_in", 2)
        w_in, wr_rdy, zeroed, cleared, iotas = (mem.sem(n) for n in ("w_in", "wr_rdy", "zeroed", "cleared", "iotas"))
        bn_rdy, mv_rdy, sd_rdy, rstd_rdy, y_rdy, tr_rdy, yT_rdy, lg_rdy = (
            mem.sem(n) for n in ("bn_rdy", "mv_rdy", "sd_rdy", "rstd_rdy", "y_rdy", "tr_rdy", "yT_rdy", "lg_rdy"))
        step_done, msd_rdy, gap_rdy, egap_rdy, both_rdy, counted, pos_rdy, scattered = (
            mem.sem(n) for n in ("step_done", "msd_rdy", "gap_rdy", "egap_rdy", "both_rdy", "counted", "pos_rdy", "scattered"))
        kept = mem.sem("kept")
        block = ctx.enter_context(nc.Block())

        @block.sync
        def _(sp):
            def load(t, k):
                sp.dma_start(xb[:, k, :], x[bass.ds(t * P, P), :]).then_inc(x_in[k], 16)

            load(0, 0)
            load(1, 1)
            sp.dma_start(wl[:], logits_w).then_inc(w_in, 16)
            sp.dma_start(rs[:], scale).then_inc(w_in, 16)
            sp.dma_start(esc[:], expert_scale.partition_broadcast(P)).then_inc(w_in, 16)

            def step(t, k, i, last):
                if not last:
                    sp.wait_ge(y_rdy, t + 1)
                    load(t + 2, k)

            looped(sp, NT, 2, step)

        @block.gpsimd
        def _(pool):
            pool.memset(zero[:], 0.0).then_inc(zeroed, 1)
            pool.iota(iota_e[:], [[1, E]], base=0, channel_multiplier=0, allow_small_or_imprecise_dtypes=True).then_inc(iotas, 1)
            pool.iota(iota_e8[:], [[1, E]], base=E, channel_multiplier=0, allow_small_or_imprecise_dtypes=True).then_inc(iotas, 1)
            pool.iota(levels[:], [[0, E], [P, LEVELS]], base=0, channel_multiplier=0, allow_small_or_imprecise_dtypes=True).then_inc(iotas, 1)
            pool.iota(jota[:], [[1, SLOT_TILES], [0, E]], base=0, channel_multiplier=0, allow_small_or_imprecise_dtypes=True).then_inc(iotas, 1)
            for e in range(E):
                pool.memset(flip[:, e:e + 1], 0.0 if e == E - 1 else (-1.0) ** e).then_inc(iotas, 1)
                pool.memset(upto[:, e:e + 1], 0.0 if e == E - 1 else 1.0).then_inc(iotas, 1)
            pool.wait_ge(kept, NT + 2)
            pool.wait_ge(pos_rdy, 1)
            if clear:
                pool.wait_ge(cleared, 16 * (SLOT_TILES // 4))
            for t in range(NT):
                for k in range(TOPK):
                    pool.indirect_dma_start(
                        xs, bass.IndirectOffsetOnAxis(ap=plan["slot"][:, k, t:t + 1], axis=0), y[:, t, :], None,
                    ).then_inc(scattered, 16)
            pool.wait_ge(scattered, 16 * NT * TOPK)

        @block.scalar
        def _(act):
            if clear:
                act.wait_ge(zeroed, 1)
                for n in range(SLOT_TILES // 4):
                    act.dma_start(xs[n * 4 * P:(n + 1) * 4 * P, :].rearrange("(p r) d -> p (r d)", r=4),
                                  zero[:]).then_inc(cleared, 16)

            def deviation(t, k):
                act.wait_ge(mv_rdy, t + 1)
                act.activation(sd[:, bass.ds(t, 1)], mv[:, k, 1:2], ACT.Sqrt, bias=const["eps"][:]).then_inc(sd_rdy, 1)

            def step(t, k, i, last):
                if not (last and k == 1):
                    deviation(t + 1, 1 - k)
                act.wait_ge(tr_rdy, t + 1)
                act.activation(yT[:, k, :], tr[:, k, :], ACT.Copy).then_inc(yT_rdy, 1)
                act.activation(y[:, bass.ds(t, 1), :], yb[:, k, :].unsqueeze(1), ACT.Copy).then_inc(kept, 1)

            deviation(0, 0)
            act.sem_inc(kept, 2)
            looped(act, NT, 2, step)
            act.wait_ge(step_done, 3)
            act.activation(small["msd"][:], small["ms"][:], ACT.Sqrt).then_inc(msd_rdy, 1)
            act.wait_ge(gap_rdy, 1)
            act.activation(small["egap"][:], small["gap"][:], ACT.Exp).then_inc(egap_rdy, 1)

        @block.tensor
        def _(pe):
            pe.sem_inc(yT_rdy, 2)
            pe.wait_ge(wr_rdy, DC)

            def step(t, k, i, last):
                pe.wait_ge(y_rdy, t + 1)
                pe.wait_ge(yT_rdy, t + 1)
                for c in range(DC):
                    ins = pe.transpose(tr[:, k, c * P:(c + 1) * P], yb[:, k, c * P:(c + 1) * P], const["ident"][:])
                ins.then_inc(tr_rdy, 1)
                pe.wait_ge(yT_rdy, t + 3)
                for c in range(DC):
                    ins = pe.matmul(lg_ps[:, bass.ds(t, 1), :], yT[:, k, c * P:(c + 1) * P], wr[:, c, :],
                                    start=(c == 0), stop=(c == DC - 1), skip_group_check=True)
                ins.then_inc(lg_rdy, 1)

            looped(pe, NT, 2, step)
            pe.wait_ge(both_rdy, 1)
            pe.matmul(pre_ps[:], const["before"][:], wide["both"][:], start=True, stop=True)
            pe.matmul(tot_ps[:], const["ones"][:], wide["both"][:], start=True, stop=True).then_inc(counted, 1)

        @block.vector
        def _(dve):
            steps = [0]

            def then(ins):
                steps[0] += 1
                ins.then_inc(step_done, 1)
                dve.wait_ge(step_done, steps[0])

            dve.wait_ge(w_in, 48)
            for c in range(DC):
                dve.tensor_scalar(wr[:, c, :], wl[:, c, :], rs[:, c:c + 1], float(D) ** -0.5, ALU.mult, ALU.mult).then_inc(wr_rdy, 1)

            def stats(t, k, i):
                dve.wait_ge(x_in[k], 16 * (i + 1))
                dve.bn_stats(bn[:, k, :], xb[:, k, :]).then_inc(bn_rdy, 1)

            def moments(t, k):
                dve.bn_aggr(mv[:, k, :], bn[:, k, :]).then_inc(mv_rdy, 1)
                dve.wait_ge(mv_rdy, t + 1)
                dve.tensor_copy(var[:, bass.ds(t, 1)], mv[:, k, 1:2])

            stats(0, 0, 0)
            dve.wait_ge(bn_rdy, 1)
            moments(0, 0)

            def step(t, k, i, last):
                ahead = not (last and k == 1)
                if ahead:
                    stats(t + 1, 1 - k, i + k)
                    dve.wait_ge(bn_rdy, t + 2)
                dve.wait_ge(sd_rdy, t + 1)
                dve.reciprocal(rstd[:, bass.ds(t, 1)], sd[:, bass.ds(t, 1)]).then_inc(rstd_rdy, 1)
                if ahead:
                    moments(t + 1, 1 - k)
                dve.wait_ge(rstd_rdy, t + 1)
                dve.wait_ge(kept, t + 1)
                dve.tensor_scalar(yb[:, k, :], xb[:, k, :], mv[:, k, 0:1], rstd[:, bass.ds(t, 1)],
                                  ALU.subtract, ALU.mult).then_inc(y_rdy, 1)

            looped(dve, NT, 2, step)
            then(dve.tensor_tensor(small["ms"][:], rstd[:], rstd[:], ALU.mult))
            then(dve.tensor_tensor(small["ms"][:], small["ms"][:], var[:], ALU.mult))
            then(dve.tensor_scalar(small["ms"][:], small["ms"][:], RMS_EPS, None, ALU.add))
            dve.wait_ge(msd_rdy, 1)
            then(dve.reciprocal(small["rr"][:], small["msd"][:]))
            dve.wait_ge(lg_rdy, NT)
            dve.wait_ge(iotas, 4 + 2 * E)
            lg = wide["lg"]
            then(dve.tensor_tensor(lg[:], lg_ps[:], spread(small["rr"][:], E), ALU.mult))

            def best(values, top, at, onehot):
                then(dve.tensor_reduce(top[:], values[:], AX.X, ALU.max))
                then(dve.tensor_tensor(wide["eq"][:], values[:], spread(top[:], E), ALU.is_equal))
                then(dve.tensor_scalar(wide["cand"][:], wide["eq"][:], -float(E), None, ALU.mult))
                then(dve.tensor_tensor(wide["cand"][:], wide["cand"][:], spread(iota_e8[:], NT, 1), ALU.add))
                then(dve.tensor_reduce(at[:], wide["cand"][:], AX.X, ALU.min))
                then(dve.tensor_tensor(onehot[:], spread(at[:], E), spread(iota_e[:], NT, 1), ALU.is_equal))

            best(lg, small["top1"], small["at1"], wide["oh1"])
            then(dve.scalar_tensor_tensor(wide["left"][:], wide["oh1"][:], -3e38, lg[:], ALU.mult, ALU.add))
            best(wide["left"], small["top2"], small["at2"], wide["oh2"])
            dve.tensor_tensor(small["gap"][:], small["top2"][:], small["top1"][:], ALU.subtract).then_inc(gap_rdy, 1)
            dve.tensor_tensor(wide["both"][:], wide["oh1"][:], wide["oh2"][:], ALU.add).then_inc(both_rdy, 1)
            dve.wait_ge(egap_rdy, 1)
            then(dve.tensor_scalar(small["den"][:], small["egap"][:], 1.0, None, ALU.add))
            then(dve.reciprocal(small["w1"][:], small["den"][:]))
            then(dve.tensor_tensor(small["w2"][:], small["w1"][:], small["egap"][:], ALU.mult))
            for k, (oh, s, w) in enumerate((("oh1", "s1", "w1"), ("oh2", "s2", "w2"))):
                then(dve.tensor_tensor(wide["tmp"][:], wide[oh][:], spread(esc[:], NT, 1), ALU.mult))
                then(dve.tensor_reduce(small[s][:], wide["tmp"][:], AX.X, ALU.add))
                then(dve.scalar_tensor_tensor(plan["weight"][:, k, :], small[s][:], 0.5, small[w][:], ALU.mult, ALU.mult))
            dve.wait_ge(counted, 1)
            then(dve.tensor_copy(wide["tot"][:], tot_ps[:]))
            now, nxt = wide["tot"], wide["sumA"]
            for sh in (1, 2, 4, 8, 16):
                then(dve.tensor_copy(nxt[:, 0:sh, :], now[:, 0:sh, :]))
                then(dve.tensor_tensor(nxt[:, sh:NT, :], now[:, sh:NT, :], now[:, 0:NT - sh, :], ALU.add))
                now, nxt = nxt, (wide["sumB"] if nxt is wide["sumA"] else wide["sumA"])
            then(dve.tensor_tensor(over[:], spread(now[:, NT - 1, :], LEVELS), levels[:], ALU.is_gt))
            then(dve.tensor_reduce(tiles[:], over[:], AX.X, ALU.add))
            then(dve.tensor_scalar(tiles[:], tiles[:], 1.0, None, ALU.max))
            end, nend = tiles, endA
            for sh in (1, 2, 4):
                then(dve.tensor_copy(nend[:, 0:sh], end[:, 0:sh]))
                then(dve.tensor_tensor(nend[:, sh:E], end[:, sh:E], end[:, 0:E - sh], ALU.add))
                end, nend = nend, (endB if nend is endA else endA)
            then(dve.tensor_tensor(base[:], end[:], tiles[:], ALU.subtract))
            then(dve.tensor_scalar(base[:], base[:], float(P), None, ALU.mult))
            then(dve.tensor_tensor(wide["pos"][:], now[:], wide["tot"][:], ALU.subtract))
            then(dve.tensor_tensor(wide["pos"][:], wide["pos"][:], pre_ps[:], ALU.add))
            then(dve.tensor_tensor(wide["pos"][:], wide["pos"][:], spread(base[:], NT, 1), ALU.add))
            for k, (oh, p) in enumerate((("oh1", "p1"), ("oh2", "p2"))):
                then(dve.tensor_tensor(wide["tmp2"][:], wide[oh][:], wide["pos"][:], ALU.mult))
                then(dve.tensor_reduce(small[p][:], wide["tmp2"][:], AX.X, ALU.add))
                then(dve.tensor_copy(plan["slot"][:, k, :], small[p][:]))
            dve.sem_inc(pos_rdy, 1)
            then(dve.tensor_tensor(past[:], jota[:], spread(end[0:1, :], SLOT_TILES, 1), ALU.is_ge))
            then(dve.tensor_tensor(past2[:], past[:], spread(upto[:], SLOT_TILES, 1), ALU.mult))
            then(dve.tensor_reduce(tabf[:, 0, :], past2[:], AX.X, ALU.add))
            then(dve.tensor_scalar(tabf[:, 0, :], tabf[:, 0, :], 1.0, None, ALU.add))
            then(dve.tensor_tensor(past2[:], past[:], spread(flip[:], SLOT_TILES, 1), ALU.mult))
            then(dve.tensor_reduce(tabf[:, 1, :], past2[:], AX.X, ALU.add))
            then(dve.tensor_scalar(tabf[:, 1, :], tabf[:, 1, :], float(WPIECES * WPIECE), None, ALU.mult))
            then(dve.tensor_copy(plan["tile"][:], tabf[:]))
            then(dve.memset(relf[:], 1.0))
            then(dve.tensor_scalar(relf[:, 2:E], end[0:1, 0:E - 2], 1.0, None, ALU.add))
            then(dve.tensor_copy(plan["release"][:], relf[:]))


def expert_stage(nc, stage, const, xs, ys, w_experts, plan):
    with ExitStack() as ctx:
        mem = Memory(nc, ctx, stage)
        w_hi = mem.sb("w_hi", [P, 2 * WPIECES * WPIECE], F32R)
        w_lo = mem.sb("w_lo", [P, 2 * WPIECES * WPIECE], F32R)
        raw = mem.sb("raw", [P, 2, WPIECE])
        xb = mem.sb("xb", [P, 2, D])
        x_hi = mem.sb("x_hi", [P, 2, D], F32R)
        x_lo = mem.sb("x_lo", [P, 2, D], F32R)
        gl = mem.sb("gl", [P, 2, H])
        ac = mem.sb("ac", [P, 2, H])
        a_hi = mem.sb("a_hi", [P, 2, H], F32R)
        a_lo = mem.sb("a_lo", [P, 2, H], F32R)
        ob = mem.sb("ob", [P, 2, D])
        tr = mem.ps("tr", [P, 2, D])
        gu = mem.ps("gu", [P, 2, H])
        at = mem.ps("at", [P, 2, H])
        dn = mem.ps("dn", [P, 2, D])

        raw_in, raw_free, w_rdy, hi_w = mem.sems("raw_in", 2), mem.sem("raw_free"), mem.sem("w_rdy"), mem.sem("hi_w")
        x_in, st = mem.sems("x_in", 2), mem.sems("st", 2)
        tr_rdy, xhi_rdy, xlo_rdy, gu_rdy, gl_rdy, ac_rdy, at_rdy, ahi_rdy, alo_rdy, dn_rdy, ob_rdy = (
            mem.sem(n) for n in ("tr_rdy", "xhi_rdy", "xlo_rdy", "gu_rdy", "gl_rdy", "ac_rdy", "at_rdy", "ahi_rdy",
                                 "alo_rdy", "dn_rdy", "ob_rdy"))
        block = ctx.enter_context(nc.Block())
        NTL = SLOT_TILES

        @block.gpsimd
        def _(pool):
            def load(e, n, s):
                pool.dma_start(raw[:, s, :], w_experts[bass.ds(e, 1), :, n, :].rearrange("a p m -> (a p) m")).then_inc(raw_in[s], 16)

            def split(e, par, i):
                pool.wait_ge(dn_rdy, pool.value_load(plan["release"][0:1, bass.ds(e, 1)], min_val=1, max_val=SLOT_TILES + 1))
                for n in range(WPIECES):
                    s = n % 2
                    g = e * WPIECES + n
                    pool.wait_ge(raw_in[s], 16 * (e * (WPIECES // 2) + n // 2 + 1))
                    o = (par * WPIECES + n) * WPIECE
                    pool.tensor_tensor(w_hi[:, o:o + WPIECE], raw[:, s, :], const["ones"][:, 0:1].to_broadcast([P, WPIECE]), ALU.mult).then_inc(hi_w, 1)
                    pool.wait_ge(hi_w, g + 1)
                    ins = pool.tensor_tensor(w_lo[:, o:o + WPIECE], raw[:, s, :], w_hi[:, o:o + WPIECE].bitcast(F32), ALU.subtract)
                    ins.then_inc(w_rdy, 1)
                    pool.wait_ge(w_rdy, g + 1)
                    if n + 2 < WPIECES:
                        load(e, n + 2, s)
                    else:
                        yield n + 2 - WPIECES, s

            load(0, 0, 0)
            load(0, 1, 1)
            with pool.Fori(0, E // 2 - 1) as i:
                for par in range(2):
                    for n, s in split(i * 2 + par, par, i):
                        load(i * 2 + par + 1, n, s)
            for n, s in split(E - 2, 0, E // 2 - 1):
                load(E - 1, n, s)
            for n, s in split(E - 1, 1, E // 2 - 1):
                pass

        @block.sync
        def _(sp):
            def load(j, k):
                sp.dma_start(xb[:, k, :], xs[bass.ds(j * P, P), :]).then_inc(x_in[k], 16)

            sp.sem_inc(st[0], 16)
            sp.sem_inc(st[1], 16)
            load(0, 0)
            load(1, 1)

            def step(j, k, i, last):
                if not last:
                    sp.wait_ge(tr_rdy, j + 1)
                    load(j + 2, k)
                sp.wait_ge(ob_rdy, j + 1)
                sp.dma_start(ys[bass.ds(j * P, P), :], ob[:, k, :]).then_inc(st[k], 16)

            looped(sp, NTL, 2, step)
            for k in range(2):
                sp.wait_ge(st[k], 16 * (NTL // 2 + 1))

        @block.tensor
        def _(pe):
            def turn_rows(j, k, i):
                pe.wait_ge(x_in[k], 16 * (i + 1))
                pe.wait_ge(xlo_rdy, j + 1)
                for c in range(DC):
                    ins = pe.transpose(tr[:, k, c * P:(c + 1) * P], xb[:, k, c * P:(c + 1) * P], const["ident"][:])
                ins.then_inc(tr_rdy, 1)

            def up(j, k):
                need = pe.value_load(plan["tile"][0:1, 0, bass.ds(j, 1)], min_val=1, max_val=E)
                off = pe.value_load(plan["tile"][0:1, 1, bass.ds(j, 1)], min_val=0, max_val=WPIECES * WPIECE)
                pe.wait_ge(w_rdy, need * WPIECES)
                pe.wait_ge(xlo_rdy, j + 3)
                pe.wait_ge(ac_rdy, j + 1)
                for c in range(DC):
                    xh, xl = x_hi[:, k, c * P:(c + 1) * P], x_lo[:, k, c * P:(c + 1) * P]
                    for n, (a, w) in enumerate(((xh, w_hi), (xh, w_lo), (xl, w_hi))):
                        for q in range(2):
                            ins = pe.matmul(gu[:, q, :], a, w[:, bass.ds(off + (c * WPIECE + q * H), H)],
                                            start=(c == 0 and n == 0), stop=(c == DC - 1 and n == 2))
                ins.then_inc(gu_rdy, 1)
                return off

            def turn_act(j, k):
                pe.wait_ge(ac_rdy, j + 2)
                pe.wait_ge(alo_rdy, j + 1)
                for c in range(DC):
                    ins = pe.transpose(at[:, k, c * P:(c + 1) * P], ac[:, k, c * P:(c + 1) * P], const["ident"][:])
                ins.then_inc(at_rdy, 1)

            def down(j, k):
                off = pe.value_load(plan["tile"][0:1, 1, bass.ds(j, 1)], min_val=0, max_val=WPIECES * WPIECE)
                pe.wait_ge(alo_rdy, j + 3)
                for c in range(DC):
                    ah, al = a_hi[:, k, c * P:(c + 1) * P], a_lo[:, k, c * P:(c + 1) * P]
                    for n, (a, w) in enumerate(((ah, w_hi), (ah, w_lo), (al, w_hi))):
                        ins = pe.matmul(dn[:, k, :], a, w[:, bass.ds(off + (DC * WPIECE + c * D), D)],
                                        start=(c == 0 and n == 0), stop=(c == DC - 1 and n == 2))
                ins.then_inc(dn_rdy, 1)

            pe.sem_inc(xlo_rdy, 2)
            pe.sem_inc(alo_rdy, 2)
            pe.sem_inc(ac_rdy, 1)
            pe.sem_inc(dn_rdy, 1)
            turn_rows(0, 0, 0)
            turn_rows(1, 1, 0)
            up(0, 0)
            with pe.Fori(0, NTL // 2 - 1) as i:
                for k in range(2):
                    j = i * 2 + k + 1
                    turn_act(j - 1, k)
                    up(j, 1 - k)
                    turn_rows(j + 1, k, i + 1)
                    down(j - 1, k)
            j = NTL - 1
            turn_act(j - 1, 0)
            up(j, 1)
            down(j - 1, 0)
            turn_act(j, 1)
            down(j, 1)

        @block.scalar
        def _(act):
            def x_part(j, k):
                act.wait_ge(tr_rdy, j + 1)
                act.activation(x_hi[:, k, :], tr[:, k, :], ACT.Copy).then_inc(xhi_rdy, 1)

            def gelu(j, k):
                act.wait_ge(gu_rdy, j + 1)
                act.activation(gl[:, k, :], gu[:, 0, :], ACT.Gelu_apprx_tanh).then_inc(gl_rdy, 1)

            def a_part(j, k):
                act.wait_ge(at_rdy, j + 1)
                act.activation(a_hi[:, k, :], at[:, k, :], ACT.Copy).then_inc(ahi_rdy, 1)

            def out(j, k, i):
                act.wait_ge(dn_rdy, j + 2)
                act.wait_ge(st[k], 16 * (i + 1))
                act.activation(ob[:, k, :], dn[:, k, :], ACT.Copy).then_inc(ob_rdy, 1)

            x_part(0, 0)
            x_part(1, 1)
            gelu(0, 0)
            with act.Fori(0, NTL // 2 - 1) as i:
                for k in range(2):
                    j = i * 2 + k + 1
                    a_part(j - 1, k)
                    gelu(j, 1 - k)
                    x_part(j + 1, k)
                    out(j - 1, k, i)
            j = NTL - 1
            a_part(j - 1, 0)
            gelu(j, 1)
            out(j - 1, 0, NTL // 2 - 1)
            a_part(j, 1)
            out(j, 1, NTL // 2 - 1)

        @block.vector
        def _(dve):
            def x_part(j, k):
                dve.wait_ge(xhi_rdy, j + 1)
                dve.tensor_tensor(x_lo[:, k, :], tr[:, k, :], x_hi[:, k, :].bitcast(F32), ALU.subtract).then_inc(xlo_rdy, 1)

            def gate(j, k):
                dve.wait_ge(gl_rdy, j + 1)
                dve.tensor_tensor(ac[:, k, :], gu[:, 1, :], gl[:, k, :], ALU.mult).then_inc(ac_rdy, 1)

            def a_part(j, k):
                dve.wait_ge(ahi_rdy, j + 1)
                dve.tensor_tensor(a_lo[:, k, :], at[:, k, :], a_hi[:, k, :].bitcast(F32), ALU.subtract).then_inc(alo_rdy, 1)

            x_part(0, 0)
            x_part(1, 1)
            gate(0, 0)
            with dve.Fori(0, NTL // 2 - 1) as i:
                for k in range(2):
                    j = i * 2 + k + 1
                    a_part(j - 1, k)
                    gate(j, 1 - k)
                    x_part(j + 1, k)
            j = NTL - 1
            a_part(j - 1, 0)
            gate(j, 1)
            a_part(j, 1)


class Front:

    def __init__(self, mem, const, x, nx, ny, joined=None, x_new=None):
        self.const, self.x, self.nx, self.ny, self.joined, self.x_to = const, x, nx, ny, joined, x_new
        self.xb = mem.sb("xb", [P, nx, D])
        self.yb = mem.sb("yb", [P, ny, D])
        self.bn = mem.sb("bn", [P, 2, 6])
        self.mv = mem.sb("mv", [P, 2, 2])
        self.sd = mem.sb("sd", [P, 2])
        self.rstd = mem.sb("rstd", [P, 2])
        self.tr = mem.ps("tr", [P, 2, D])
        self.x_in = mem.sems("x_in", nx)
        (self.bn_rdy, self.mv_rdy, self.sd_rdy, self.rstd_rdy, self.y_rdy, self.tr_rdy, self.hi_rdy, self.lo_rdy) = (
            mem.sem(n) for n in ("bn_rdy", "mv_rdy", "sd_rdy", "rstd_rdy", "y_rdy", "tr_rdy", "hi_rdy", "lo_rdy"))
        if joined:
            self.gb = mem.sb("gb", [P, 2, TOPK, D])
            self.g_in = mem.sems("g_in", 2)
            self.x_st = mem.sems("x_st", nx)
            self.one_rdy, self.x_rdy = mem.sem("one_rdy"), mem.sem("x_rdy")

    def load(self, sp, t, k):
        sp.dma_start(self.xb[:, k, :], self.x[bass.ds(t * P, P), :]).then_inc(self.x_in[k], 16)

    def sp_tile(self, sp, t, k, i, ahead):
        if self.joined:
            sp.wait_ge(self.x_rdy, t + 1)
            sp.dma_start(self.x_to[bass.ds(t * P, P), :], self.xb[:, k, :]).then_inc(self.x_st[k], 16)
        if ahead:
            sp.wait_ge(self.y_rdy, t + 1)
            if self.joined:
                sp.wait_ge(self.x_st[k], 16 * (i + 1))
            self.load(sp, t + self.nx, k)

    def sp_end(self, sp):
        if self.joined:
            for k in range(self.nx):
                sp.wait_ge(self.x_st[k], 16 * (NT // self.nx))

    def gather(self, pool, begin=0, end=NT):
        ys, plan = self.joined
        for t in range(begin, end):
            if t >= 2:
                pool.wait_ge(self.x_rdy, t - 1)
            for k in range(TOPK):
                pool.indirect_dma_start(
                    self.gb[:, t % 2, k, :], None, ys, bass.IndirectOffsetOnAxis(ap=plan["slot"][:, k, t:t + 1], axis=0),
                ).then_inc(self.g_in[t % 2], 16)

    def stats(self, dve, t, k, i, g):
        xk = self.xb[:, k, :]
        dve.wait_ge(self.x_in[k], 16 * (i + 1))
        if self.joined:
            w = self.joined[1]["weight"]
            dve.wait_ge(self.g_in[k % 2], 16 * TOPK * (g + 1))
            dve.scalar_tensor_tensor(xk, self.gb[:, k % 2, 0, :], w[:, 0, bass.ds(t, 1)], xk, ALU.mult, ALU.add).then_inc(self.one_rdy, 1)
            dve.wait_ge(self.one_rdy, t + 1)
            dve.scalar_tensor_tensor(xk, self.gb[:, k % 2, 1, :], w[:, 1, bass.ds(t, 1)], xk, ALU.mult, ALU.add).then_inc(self.x_rdy, 1)
            dve.wait_ge(self.x_rdy, t + 1)
        dve.bn_stats(self.bn[:, k % 2, :], xk).then_inc(self.bn_rdy, 1)

    def moments(self, dve, k):
        dve.bn_aggr(self.mv[:, k % 2, :], self.bn[:, k % 2, :]).then_inc(self.mv_rdy, 1)

    def first(self, dve):
        self.stats(dve, 0, 0, 0, 0)
        dve.wait_ge(self.bn_rdy, 1)
        self.moments(dve, 0)

    def normalise(self, dve, t, k, i, ky, ahead, after=None):
        kn = (k + 1) % self.nx
        if ahead:
            n = i + (1 if kn == 0 else 0)
            g = i * (self.nx // 2) + (k + 1) // 2
            self.stats(dve, t + 1, kn, n, g)
            dve.wait_ge(self.bn_rdy, t + 2)
        dve.wait_ge(self.sd_rdy, t + 1)
        dve.reciprocal(self.rstd[:, k % 2:k % 2 + 1], self.sd[:, k % 2:k % 2 + 1]).then_inc(self.rstd_rdy, 1)
        if ahead:
            self.moments(dve, kn)
        dve.wait_ge(self.rstd_rdy, t + 1)
        dve.tensor_scalar(self.yb[:, ky, :], self.xb[:, k, :], self.mv[:, k % 2, 0:1], self.rstd[:, k % 2:k % 2 + 1],
                          ALU.subtract, ALU.mult).then_inc(self.y_rdy, 1)

    def deviation(self, act, t, k):
        act.wait_ge(self.mv_rdy, t + 1)
        act.activation(self.sd[:, k % 2:k % 2 + 1], self.mv[:, k % 2, 1:2], ACT.Sqrt, bias=self.const["eps"][:]).then_inc(self.sd_rdy, 1)

    def free(self, pe):
        pe.sem_inc(self.lo_rdy, 2)

    def turn(self, pe, t, k, ky):
        pe.wait_ge(self.y_rdy, t + 1)
        pe.wait_ge(self.lo_rdy, t + 1)
        for c in range(DC):
            ins = pe.transpose(self.tr[:, k % 2, c * P:(c + 1) * P], self.yb[:, ky, c * P:(c + 1) * P], self.const["ident"][:])
        ins.then_inc(self.tr_rdy, 1)

    def hi(self, act, t, k, to):
        act.wait_ge(self.tr_rdy, t + 1)
        act.activation(to, self.tr[:, k % 2, :].rearrange("p (c m) -> p c m", c=DC), ACT.Copy).then_inc(self.hi_rdy, 1)

    def lo(self, dve, t, k, to, hi):
        dve.wait_ge(self.hi_rdy, t + 1)
        dve.tensor_tensor(to, self.tr[:, k % 2, :].rearrange("p (c m) -> p c m", c=DC), hi.bitcast(F32), ALU.subtract).then_inc(self.lo_rdy, 1)


def products(parts_a, parts_b):
    (ah, al), (bh, bl) = parts_a, parts_b
    return ((ah, bh), (ah, bl), (al, bh))


GA = 4
QW = GA * P


def projection_stage(nc, stage, const, x, x_new, joined, q_w, k_w, v_w, q_parts, kst, v):
    with ExitStack() as ctx:
        mem = Memory(nc, ctx, stage)
        f = Front(mem, const, x, 4, GA, joined, x_new)
        y_hi = mem.sb("y_hi", [P, 2, DC, QW], F32R)
        y_lo = mem.sb("y_lo", [P, 2, DC, QW], F32R)
        NQ = HEADS * HD
        raw = {"q": mem.sb("q_raw", [P, DC, NQ]), "k": mem.sb("k_raw", [P, DC, 3 * HD]), "v": mem.sb("v_raw", [P, DC, HD])}
        w_hi = {n: mem.sb(f"{n}_whi", list(r.shape), F32R) for n, r in raw.items()}
        w_lo = {n: mem.sb(f"{n}_wlo", list(r.shape), F32R) for n, r in raw.items()}
        q_hi = mem.sb("q_hi", [P, 2, QW], F32R)
        q_lo = mem.sb("q_lo", [P, 2, QW], F32R)
        q_ps = mem.ps("q", [P, 2, QW])
        k_ps = mem.ps("k", [P, QW])
        v_ps = mem.ps("v", [P, GA, HD])
        w_in, whi_rdy, wlo_rdy, ones_rdy = (mem.sem(n) for n in ("w_in", "whi_rdy", "wlo_rdy", "ones_rdy"))
        q_rdy, qhi_rdy, qlo_rdy, k_rdy, khi_rdy, klo_rdy, v_rdy, v_kept = (
            mem.sem(n) for n in ("q_rdy", "qhi_rdy", "qlo_rdy", "k_rdy", "khi_rdy", "klo_rdy", "v_rdy", "v_kept"))
        q_st = mem.sems("q_st", 2)
        block = ctx.enter_context(nc.Block())
        NG = NT // GA
        QC = NQ // P

        def parts(g2):
            return (y_hi[:, g2], y_lo[:, g2])

        def tile_of(buf, g2, j):
            return buf[:, g2, :, j * P:(j + 1) * P]

        @block.sync
        def _(sp):
            for s in range(2):
                sp.sem_inc(q_st[s], 32)
            for t in range(4):
                f.load(sp, t, t)
            sp.dma_start(raw["q"][:], q_w).then_inc(w_in, 16)
            for n in range(3):
                sp.dma_start(raw["k"][:, :, n * HD:(n + 1) * HD], k_w).then_inc(w_in, 16)
            sp.dma_start(raw["v"][:], v_w).then_inc(w_in, 16)

            def group(g, gi, ahead):
                for j in range(GA):
                    f.sp_tile(sp, g * GA + j, j, gi, ahead)

            def queries(g):
                for m in range(QC):
                    s = m % 2
                    sp.wait_ge(qlo_rdy, g * QC + m + 3)
                    for n, part in enumerate((q_hi, q_lo)):
                        sp.dma_start(q_parts[n, m * P:(m + 1) * P, bass.ds(g * QW, QW)], part[:, s, :].bitcast(F32)).then_inc(q_st[s], 16)

            group(0, 0, True)
            group(1, 1, True)

            with sp.Fori(0, NG // 2 - 2) as i:
                for g2 in range(2):
                    group(i * 2 + g2 + 2, i * 2 + g2 + 2, True)
                    queries(i * 2 + g2)
            for g in range(NG - 4, NG):
                if g + 2 < NG:
                    for j in range(GA):
                        f.sp_tile(sp, (g + 2) * GA + j, j, g + 2, g + 3 < NG)
                queries(g)
            f.sp_end(sp)
            for s in range(2):
                sp.wait_ge(q_st[s], 32 * (NG * QC // 2 + 1))

        @block.gpsimd
        def _(pool):
            pool.memset(kst[96:98, :].bitcast(F32), 1.0).then_inc(ones_rdy, 1)
            pool.wait_ge(ones_rdy, 1)
            pool.wait_ge(w_in, 80)
            for n in ("k", "q", "v"):
                pool.tensor_scalar(w_hi[n][:], raw[n][:], 1.0, None, ALU.mult).then_inc(whi_rdy, 1)
            f.gather(pool)

        @block.tensor
        def _(pe):
            f.free(pe)
            pe.sem_inc(qlo_rdy, 2)
            pe.sem_inc(klo_rdy, 1)
            pe.sem_inc(v_kept, 1)

            def group_turn(g, g2):
                for j in range(GA):
                    f.turn(pe, g * GA + j, j, j)

            def main(g, g2):
                yp = parts(g2)
                pe.wait_ge(f.lo_rdy, (g + 1) * GA + 2)
                pe.wait_ge(klo_rdy, g + 1)
                for c in range(DC):
                    for n, (a, b) in enumerate(products((w_hi["k"][:, c, :], w_lo["k"][:, c, :]), (yp[0][:, c, :], yp[1][:, c, :]))):
                        ins = pe.matmul(k_ps[0:3 * HD, :], a, b, start=(c == 0 and n == 0), stop=(c == DC - 1 and n == 2))
                ins.then_inc(k_rdy, 1)
                for m in range(QC):
                    pe.wait_ge(qlo_rdy, g * QC + m + 1)
                    for c in range(DC):
                        wq = (w_hi["q"][:, c, m * P:(m + 1) * P], w_lo["q"][:, c, m * P:(m + 1) * P])
                        for n, (a, b) in enumerate(products(wq, (yp[0][:, c, :], yp[1][:, c, :]))):
                            ins = pe.matmul(q_ps[:, m % 2, :], a, b, start=(c == 0 and n == 0), stop=(c == DC - 1 and n == 2))
                    ins.then_inc(q_rdy, 1)
                pe.wait_ge(v_kept, g + 1)
                for j in range(GA):
                    for c in range(DC):
                        yt = (tile_of(y_hi, g2, j)[:, c, :], tile_of(y_lo, g2, j)[:, c, :])
                        for n, (a, b) in enumerate(products(yt, (w_hi["v"][:, c, :], w_lo["v"][:, c, :]))):
                            ins = pe.matmul(v_ps[:, j, :], a, b, start=(c == 0 and n == 0), stop=(c == DC - 1 and n == 2))
                ins.then_inc(v_rdy, 1)

            group_turn(0, 0)
            pe.wait_ge(wlo_rdy, 3)

            def step(g, g2, i, last):
                if not (last and g2 == 1):
                    group_turn(g + 1, 1 - g2)
                main(g, g2)

            looped(pe, NG, 2, step)

        @block.scalar
        def _(act):
            f.deviation(act, 0, 0)

            def front(g, last=False):
                for j in range(GA):
                    if not (last and j == GA - 1):
                        f.deviation(act, g * GA + j + 1, (j + 1) % 4)

            def group_hi(g, g2):
                for j in range(GA):
                    f.hi(act, g * GA + j, j, tile_of(y_hi, g2, j))

            def main(g, g2):
                act.wait_ge(k_rdy, g + 1)
                act.activation(kst[0:3 * HD, bass.ds(g * QW, QW)], k_ps[0:3 * HD, :], ACT.Copy).then_inc(khi_rdy, 1)
                for m in range(QC):
                    s = m % 2
                    act.wait_ge(q_rdy, g * QC + m + 1)
                    act.wait_ge(q_st[s], 32 * (g * (QC // 2) + m // 2 + 1))
                    act.activation(q_hi[:, s, :], q_ps[:, s, :], ACT.Copy).then_inc(qhi_rdy, 1)
                act.wait_ge(v_rdy, g + 1)
                act.activation(v[:, bass.ds(g * GA, GA), :], v_ps[:], ACT.Copy).then_inc(v_kept, 1)

            front(0)
            group_hi(0, 0)
            front(1)

            def step(g, g2, i, last):
                if not (last and g2 == 1):
                    group_hi(g + 1, 1 - g2)
                if not last:
                    front(g + 2)
                main(g, g2)

            with act.Fori(0, NG // 2 - 2) as i:
                for g2 in range(2):
                    step(i * 2 + g2, g2, i, False)
            for g in range(NG - 4, NG):
                if g + 1 < NG:
                    group_hi(g + 1, 1 - g % 2)
                if g + 2 < NG:
                    front(g + 2, g + 2 == NG - 1)
                main(g, g % 2)

        @block.vector
        def _(dve):
            f.first(dve)

            def front(g, last=False):
                for j in range(GA):
                    f.normalise(dve, g * GA + j, j, g, j, not (last and j == GA - 1))

            def group_lo(g, g2):
                for j in range(GA):
                    f.lo(dve, g * GA + j, j, tile_of(y_lo, g2, j), tile_of(y_hi, g2, j))

            def main(g, g2):
                dve.wait_ge(khi_rdy, g + 1)
                kl = kst[HD:2 * HD, bass.ds(g * QW, QW)]
                dve.tensor_tensor(kl, k_ps[HD:2 * HD, :], kl.bitcast(F32), ALU.subtract).then_inc(klo_rdy, 1)
                for m in range(QC):
                    s = m % 2
                    dve.wait_ge(qhi_rdy, g * QC + m + 1)
                    dve.tensor_tensor(q_lo[:, s, :], q_ps[:, s, :], q_hi[:, s, :].bitcast(F32), ALU.subtract).then_inc(qlo_rdy, 1)

            for n, name in enumerate(("k", "q", "v")):
                dve.wait_ge(whi_rdy, n + 1)
                dve.tensor_tensor(w_lo[name][:], raw[name][:], w_hi[name][:].bitcast(F32), ALU.subtract).then_inc(wlo_rdy, 1)
            front(0)
            group_lo(0, 0)
            front(1)

            def step(g, g2, i, last):
                group_lo(g + 1, 1 - g2)
                front(g + 2)
                main(g, g2)

            with dve.Fori(0, NG // 2 - 2) as i:
                for g2 in range(2):
                    step(i * 2 + g2, g2, i, False)
            for g in range(NG - 4, NG):
                if g + 1 < NG:
                    group_lo(g + 1, 1 - g % 2)
                if g + 2 < NG:
                    front(g + 2, g + 2 == NG - 1)
                main(g, g % 2)


QT = S // P
HALF = HEADS // 2
UNITS = 2 * QT
OUT_AT = 8
TURN_AT = 11
KROWS = 3 * HD


def attention_stage(nc, stage, const, q_parts, kst, v, m_rows, attn):
    with ExitStack() as ctx:
        mem = Memory(nc, ctx, stage)
        qst = mem.sb("qst", [P, 2, HEADS, P], F32R)
        pt = mem.sb("pt", [P, 4, HALF * P])
        pairs = mem.sb("pairs", [P, 4, 2, HALF * P])
        quads = mem.sb("quads", [P, 2, HALF * P])
        mx = mem.sb("mx", [P, HEADS, 4])
        neg = mem.sb("neg", [P, HALF])
        msplit = mem.sb("msplit", [P, 2, HALF], F32R)
        mT = mem.sb("mT", [2 * HALF, P])
        inv = mem.sb("inv", [P, 2 * P])
        sc = mem.ps("sc", [P, 2, HALF * P])
        am = mem.ps("am", [P, 2, 4 * P])
        pv = mem.ps("pv", [P, 2, 2, 2 * P])
        q_in = [mem.sems(f"q_in{k}_", 2) for k in range(2)]
        m_in, m_st = mem.sems("m_in", 2), mem.sems("m_st", 2)
        am_rdy, mx_rdy, neg_rdy, mhi_rdy, ms_rdy, mT_rdy, mT_kept, s_rdy, p_rdy, pv_rdy, pair_rdy, quad_rdy, half_rdy, sum_rdy, inv_rdy, o_rdy = (
            mem.sem(n) for n in ("am_rdy", "mx_rdy", "neg_rdy", "mhi_rdy", "ms_rdy", "mT_rdy", "mT_kept", "s_rdy",
                                 "p_rdy", "pv_rdy", "pair_rdy", "quad_rdy", "half_rdy", "sum_rdy", "inv_rdy", "o_rdy"))
        block = ctx.enter_context(nc.Block())
        N = B * QT
        QUADS = UNITS // 4

        def rounds(eng, step):
            for k in range(2):
                step(k, k, 0, 0, 0)
            for b in range(B):
                with eng.Fori(0 if b else 1, QT // 2 - 1) as i:
                    for k in range(2):
                        step(i * 2 + (k + b * QT), k, i + b * (QT // 2), b, b)
                for k in range(2):
                    n = (b + 1) * QT - 2 + k
                    step(n, k, n // 2, b, b if k == 0 else (b + 1 if b + 1 < B else None))

        def lagging(do, n, q, size=UNITS):
            if q >= 0:
                do(n, q)
            elif not is_first(n):
                do(n - 1, q + size)

        def is_first(n):
            return isinstance(n, int) and n == 0

        @block.sync
        def _(sp):
            def load(n, k, h):
                for r, part in enumerate((0, 0, 1)):
                    src = q_parts[part, h * HALF * HD:(h + 1) * HALF * HD, bass.ds(n * P, P)].rearrange("(h d) q -> d h q", d=HD)
                    sp.dma_start(qst[r * HD:(r + 1) * HD, k, h * HALF:(h + 1) * HALF, :].bitcast(F32), src).then_inc(q_in[k][h], 16)

            def maxima(n, k, h):
                sp.wait_ge(mT_kept, n * 2 + (h + 1))
                sp.wait_ge(m_in[h], n * 16 + 16)
                sp.dma_start(m_rows[h], mT[:]).then_inc(m_st[h], 16)
                sp.wait_ge(m_st[h], n * 16 + 16)
                sp.dma_start(qst[KROWS:KROWS + 2, k, h * HALF:(h + 1) * HALF, :].bitcast(F32),
                             m_rows[h].rearrange("(s h) q -> s h q", s=2)).then_inc(m_in[h], 16)

            for h in range(2):
                sp.sem_inc(m_in[h], 16)
            for n in range(2):
                for h in range(2):
                    load(n, n, h)
            maxima(0, 0, 0)

            def step(n, k, i, b, nb):
                more = not (isinstance(n, int) and n + 2 >= N)
                maxima(n, k, 1)
                sp.wait_ge(s_rdy, n * UNITS + QT)
                if more:
                    load(n + 2, k, 0)
                if nb is not None:
                    maxima(n + 1, 1 - k, 0)
                sp.wait_ge(s_rdy, n * UNITS + UNITS)
                if more:
                    load(n + 2, k, 1)

            rounds(sp, step)

        @block.tensor
        def _(pe):
            pe.sem_inc(mx_rdy, 2)
            pe.sem_inc(p_rdy, 2)
            pe.sem_inc(o_rdy, 2)

            def score(n, k, b, u):
                h, kt = divmod(u, QT)
                if kt == 0:
                    pe.wait_ge(m_in[h], n * 16 + 32)
                pe.wait_ge(p_rdy, n * UNITS + (u + 1))
                key = kst[0:KROWS + 2, b * S + kt * P:b * S + (kt + 1) * P]
                for g in range(2):
                    hh = h * HALF + g * 4
                    ins = pe.matmul(sc[:, u % 2, g * 4 * P:(g + 1) * 4 * P], key, qst[0:KROWS + 2, k, hh:hh + 4, :], start=True, stop=True)
                ins.then_inc(s_rdy, 1)

            def maxi(n, k, i, b, u, g):
                hd, kh = divmod(u, 2)
                if u % QT == 0 and g == 0:
                    pe.wait_ge(q_in[k][u // QT], i * 48 + 48)
                pe.wait_ge(mx_rdy, n * (2 * UNITS) + (2 * u + g + 1))
                o = b * S + kh * (S // 2) + g * 4 * P
                pe.matmul(am[:, g, :], qst[0:KROWS, k, hd, :], kst[0:KROWS, o:o + 4 * P], start=True, stop=True).then_inc(am_rdy, 1)

            def turn(n, h):
                pe.wait_ge(ms_rdy, n * 2 + (h + 1))
                pe.wait_ge(o_rdy, n * 2 + (h + 1))
                pe.transpose(pv[0:2 * HALF, h, 0, 0:P], msplit[:].rearrange("p s h -> p (s h)").bitcast(F32),
                             const["ident"][:]).then_inc(mT_rdy, 1)

            def values(n, b, u):
                h, kt = divmod(u, QT)
                if kt == 0:
                    pe.wait_ge(o_rdy, n * 2 + (h + 1))
                    pe.wait_ge(mT_kept, n * 2 + (h + 1))
                pe.wait_ge(p_rdy, n * UNITS + (u + 3))
                for j in range(4):
                    ins = pe.matmul(pv[HD * j:HD * (j + 1), h, 0, :], v[:, b * QT + kt, :], pt[:, u % 4, 2 * P * j:2 * P * (j + 1)],
                                    start=(kt == 0), stop=(kt == QT - 1), skip_group_check=True)
                ins.then_inc(pv_rdy, 1)

            def sums(n, q):
                h, part = divmod(q, QUADS // 2)
                pe.wait_ge(quad_rdy, n * (2 * QUADS) + (2 * q + 10))
                pe.wait_ge(half_rdy, n * QUADS + (q + 5))
                for j in range(4):
                    ins = pe.matmul(pv[HD * j:HD * (j + 1), h, 1, :], const["ones"][:, 0:HD], quads[:, q % 2, 2 * P * j:2 * P * (j + 1)],
                                    start=False, stop=(part == QUADS // 2 - 1), skip_group_check=True)
                ins.then_inc(sum_rdy, 1)

            for u in range(UNITS):
                for g in range(2):
                    maxi(0, 0, 0, 0, u, g)
                if u == QT + TURN_AT:
                    turn(0, 0)
            score(0, 0, 0, 0)

            def step(n, k, i, b, nb):
                for u in range(UNITS):
                    if u == TURN_AT:
                        turn(n, 1)
                    if u == QT + TURN_AT and nb is not None:
                        turn(n + 1, 0)
                    if nb is not None:
                        maxi(n + 1, 1 - k, i + k, nb, u, 0)
                    if u + 1 < UNITS:
                        score(n, k, b, u + 1)
                    elif nb is not None:
                        score(n + 1, 1 - k, nb, 0)
                    if nb is not None:
                        maxi(n + 1, 1 - k, i + k, nb, u, 1)
                    values(n, b, u)
                    if u % 4 == 2:
                        lagging(sums, n, u // 4 - 2, QUADS)

            rounds(pe, step)
            sums(N - 1, QUADS - 2)
            sums(N - 1, QUADS - 1)

        @block.scalar
        def _(act):
            act.sem_inc(pv_rdy, 4)
            act.sem_inc(pair_rdy, 2)

            def step(n, k, i, b, nb):
                for u in range(UNITS):
                    act.wait_ge(s_rdy, n * UNITS + (u + 1))
                    act.wait_ge(pv_rdy, n * UNITS + (u + 1))
                    if u % 2 == 0:
                        act.wait_ge(pair_rdy, n * (UNITS // 2) + (u // 2 + 1))
                    act.activation(pt[:, u % 4, :], sc[:, u % 2, :], ACT.Exp, scale=HD ** -0.5).then_inc(p_rdy, 1)

            rounds(act, step)

        @block.gpsimd
        def _(pool):
            pool.sem_inc(half_rdy, 4)

            def step(n, k, i, b, nb):
                for p in range(UNITS // 2):
                    q = p // 2
                    if p % 2 == 0:
                        pool.wait_ge(quad_rdy, n * (2 * QUADS) + (2 * q + 2))
                        pool.wait_ge(half_rdy, n * QUADS + (q + 1))
                    pool.wait_ge(p_rdy, n * UNITS + (2 * p + 4))
                    pool.tensor_tensor(pairs[:, q % 4, p % 2, :], pt[:, 2 * p % 4, :], pt[:, (2 * p + 1) % 4, :], ALU.add).then_inc(pair_rdy, 1)
                    if p % 2:
                        pool.wait_ge(pair_rdy, n * (UNITS // 2) + (p + 3))
                        pool.wait_ge(sum_rdy, n * QUADS + (q + 1))
                        pool.tensor_tensor(quads[:, q % 2, 4 * P:], pairs[:, q % 4, 0, 4 * P:], pairs[:, q % 4, 1, 4 * P:], ALU.add).then_inc(half_rdy, 1)

            rounds(pool, step)

        @block.vector
        def _(dve):
            dve.sem_inc(mT_rdy, 1)
            dve.sem_inc(quad_rdy, 8)
            dve.sem_inc(sum_rdy, 2)

            def maxi(n, u):
                for g in range(2):
                    dve.wait_ge(am_rdy, n * (2 * UNITS) + (2 * u + g + 1))
                    at = u % 2 * 2 + g
                    dve.tensor_reduce(mx[:, u // 2, at:at + 1], am[:, g, :], AX.X, ALU.max).then_inc(mx_rdy, 1)

            def split(n, h):
                dve.wait_ge(mx_rdy, n * (2 * UNITS) + (2 * QT * (h + 1) + 2))
                dve.tensor_reduce(neg[:], mx[:, h * HALF:(h + 1) * HALF, :], AX.X, ALU.max, negate=True).then_inc(neg_rdy, 1)
                dve.wait_ge(neg_rdy, n * 2 + (h + 1))
                dve.wait_ge(mT_rdy, n * 2 + (h + 1))
                dve.tensor_copy(msplit[:, 0, :], neg[:]).then_inc(mhi_rdy, 1)
                dve.wait_ge(mhi_rdy, n * 2 + (h + 1))
                dve.tensor_tensor(msplit[:, 1, :], neg[:], msplit[:, 0, :].bitcast(F32), ALU.subtract).then_inc(ms_rdy, 1)

            def keep(n, h, first=False):
                dve.wait_ge(mT_rdy, n * 2 + (h + 2))
                if not first:
                    dve.wait_ge(m_st[1 - h], n * 16 + (16 if h else 0))
                dve.tensor_copy(mT[:], pv[0:2 * HALF, h, 0, 0:P]).then_inc(mT_kept, 1)

            def quad(n, piece):
                q, r = divmod(piece, 4)
                if r > 1:
                    return
                if r == 0:
                    dve.wait_ge(pair_rdy, n * (UNITS // 2) + (2 * q + 4))
                    dve.wait_ge(sum_rdy, n * QUADS + (q + 1))
                cut = slice(2 * P * r, 2 * P * (r + 1))
                dve.tensor_tensor(quads[:, q % 2, cut], pairs[:, q % 4, 0, cut], pairs[:, q % 4, 1, cut], ALU.add).then_inc(quad_rdy, 1)

            def shares(n, h):
                dve.wait_ge(sum_rdy, n * QUADS + (QUADS // 2 * (h + 1) + 2))
                dve.reciprocal(inv[:], pv[:, h, 1, :]).then_inc(inv_rdy, 1)

            def output(n, h):
                dve.wait_ge(inv_rdy, n * 2 + (h + 1))
                dve.tensor_tensor(attn[:, bass.ds(n, 1), h, :], pv[:, h, 0, :].unsqueeze(1), inv[:].unsqueeze(1), ALU.mult).then_inc(o_rdy, 1)

            for u in range(UNITS):
                maxi(0, u)
                if u == QT - 1:
                    split(0, 0)
                if u == QT + TURN_AT + 1:
                    keep(0, 0, True)
            split(0, 1)

            def step(n, k, i, b, nb):
                for u in range(UNITS):
                    if u == TURN_AT:
                        keep(n, 1)
                    if nb is not None:
                        maxi(n + 1, u)
                        if u == QT - 1:
                            split(n + 1, 0)
                        if u == QT + TURN_AT:
                            keep(n + 1, 0)
                    for m, h, at in ((n - 1, 1, OUT_AT), (n, 0, QT + OUT_AT)):
                        if u in (at, at + 1) and not (h and is_first(n)):
                            (output if u > at else shares)(m, h)
                    lagging(quad, n, u - 6)
                if nb is not None:
                    split(n + 1, 1)

            rounds(dve, step)
            for piece in range(UNITS - 6, UNITS):
                quad(N - 1, piece)
            shares(N - 1, 1)
            output(N - 1, 1)


def output_stage(nc, stage, const, attn, o_w, x, x_new):
    with ExitStack() as ctx:
        mem = Memory(nc, ctx, stage)
        NX = 4
        raw = mem.sb("raw", [P, DC, D])
        w_hi = mem.sb("w_hi", [P, DC, D], F32R)
        w_lo = mem.sb("w_lo", [P, DC, D], F32R)
        a_hi = mem.sb("a_hi", [P, 2, D], F32R)
        a_lo = mem.sb("a_lo", [P, 2, D], F32R)
        xb = mem.sb("xb", [P, NX, D])
        ob = mem.sb("ob", [P, 2, D])
        pr = mem.ps("pr", [P, 2, D])
        w_in, whi_rdy, wlo_rdy = (mem.sem(n) for n in ("w_in", "whi_rdy", "wlo_rdy"))
        x_in, st = mem.sems("x_in", NX), mem.sems("st", 2)
        hi_rdy, lo_rdy, pr_rdy, ob_rdy = (mem.sem(n) for n in ("hi_rdy", "lo_rdy", "pr_rdy", "ob_rdy"))
        block = ctx.enter_context(nc.Block())

        def rows(t):
            return attn[:, bass.ds(t, 1)].rearrange("p a h m -> p a (h m)")

        @block.sync
        def _(sp):
            def load(t, k):
                sp.dma_start(xb[:, k, :], x[bass.ds(t * P, P), :]).then_inc(x_in[k], 16)

            for k in range(2):
                sp.sem_inc(st[k], 16)
            for c in range(DC):
                sp.dma_start(raw[:, c, :], o_w[:, c, :]).then_inc(w_in, 16)
            for t in range(NX):
                load(t, t)

            def step(t, k, i, last):
                sp.wait_ge(ob_rdy, t + 3)
                sp.dma_start(x_new[bass.ds(t * P, P), :], ob[:, k % 2, :]).then_inc(st[k % 2], 16)
                if not last:
                    load(t + NX, k)

            looped(sp, NT, NX, step)
            for k in range(2):
                sp.wait_ge(st[k], 16 * (NT // 2 + 1))

        @block.scalar
        def _(act):
            act.wait_ge(w_in, 16 * DC)
            act.activation(w_hi[:, 0:2, :], raw[:, 0:2, :], ACT.Copy).then_inc(whi_rdy, 1)
            act.sem_inc(pr_rdy, 2)

            def step(t, k, i, last):
                act.wait_ge(pr_rdy, t + 1)
                act.activation(a_hi[:, k % 2, :].unsqueeze(1), rows(t), ACT.Copy).then_inc(hi_rdy, 1)

            looped(act, NT, NX, step)

        @block.gpsimd
        def _(pool):
            pool.wait_ge(w_in, 16 * DC)
            pool.tensor_scalar(w_hi[:, 2:4, :], raw[:, 2:4, :], 1.0, None, ALU.mult).then_inc(whi_rdy, 1)

        @block.vector
        def _(dve):
            dve.wait_ge(whi_rdy, 2)
            dve.tensor_tensor(w_lo[:], raw[:], w_hi[:].bitcast(F32), ALU.subtract).then_inc(wlo_rdy, 1)

            def low_part(t, k):
                dve.wait_ge(hi_rdy, t + 1)
                dve.tensor_tensor(a_lo[:, k % 2, :].unsqueeze(1), rows(t), a_hi[:, k % 2, :].bitcast(F32).unsqueeze(1), ALU.subtract).then_inc(lo_rdy, 1)

            low_part(0, 0)

            def step(t, k, i, last):
                if not (last and k == NX - 1):
                    low_part(t + 1, k + 1)
                dve.wait_ge(pr_rdy, t + 3)
                dve.wait_ge(x_in[k], i * 16 + 16)
                dve.wait_ge(st[k % 2], i * (16 * NX // 2) + (k // 2 * 16 + 16))
                dve.tensor_tensor(ob[:, k % 2, :], pr[:, k % 2, :], xb[:, k, :], ALU.add).then_inc(ob_rdy, 1)

            looped(dve, NT, NX, step)

        @block.tensor
        def _(pe):
            pe.sem_inc(ob_rdy, 2)
            pe.wait_ge(wlo_rdy, 1)

            def step(t, k, i, last):
                pe.wait_ge(lo_rdy, t + 1)
                pe.wait_ge(ob_rdy, t + 1)
                for c in range(DC):
                    cut = slice(c * P, (c + 1) * P)
                    for n, (a, b) in enumerate(products((a_hi[:, k % 2, cut], a_lo[:, k % 2, cut]), (w_hi[:, c, :], w_lo[:, c, :]))):
                        ins = pe.matmul(pr[:, k % 2, :], a, b, start=(c == 0 and n == 0), stop=(c == DC - 1 and n == 2))
                ins.then_inc(pr_rdy, 1)

            looped(pe, NT, NX, step)


GF = 2
FW = GF * P


def ffn_stage(nc, stage, const, x, x_new, joined, w_gate, w_up, w_down, gate_s, up_s, down_s, x_out):
    with ExitStack() as ctx:
        mem = Memory(nc, ctx, stage)
        f = Front(mem, const, x, 2 * GF, GF, joined, x_new)
        HALF_I = INTER // 2
        wg_hi, wg_lo = mem.sb("wg_hi", [P, DC, INTER], F32R), mem.sb("wg_lo", [P, DC, INTER], F32R)
        wu_hi, wu_lo = mem.sb("wu_hi", [P, DC, INTER], F32R), mem.sb("wu_lo", [P, DC, INTER], F32R)
        wd_hi, wd_lo = mem.sb("wd_hi", [P, IC, D], F32R), mem.sb("wd_lo", [P, IC, D], F32R)
        y_hi, y_lo = mem.sb("y_hi", [P, 2, DC, FW], F32R), mem.sb("y_lo", [P, 2, DC, FW], F32R)
        h_hi, h_lo = mem.sb("h_hi", [P, IC, FW], F32R), mem.sb("h_lo", [P, IC, FW], F32R)
        sg, hf = mem.sb("sg", [P, 2, FW]), mem.sb("hf", [P, 2, FW])
        rb, ob = mem.sb("rb", [P, GF, D]), mem.sb("ob", [P, GF, D])
        gs, us, ds_ = mem.sb("gs", [P, IC]), mem.sb("us", [P, IC]), mem.sb("ds", [P, D])
        gu = mem.ps("gu", [P, 2, 2, FW])
        dn = mem.ps("dn", [P, GF, D])
        raw_in = mem.sems("raw_in", 2)
        s_in, whi_rdy, wlo_rdy, ds_rdy = (mem.sem(n) for n in ("s_in", "whi_rdy", "wlo_rdy", "ds_rdy"))
        r_in, st = mem.sems("r_in", GF), mem.sems("st", GF)
        gu_rdy, sg_rdy, h_rdy, hhi_rdy, hlo_rdy, dn_rdy, o_half, o_rdy = (
            mem.sem(n) for n in ("gu_rdy", "sg_rdy", "h_rdy", "hhi_rdy", "hlo_rdy", "dn_rdy", "o_half", "o_rdy"))
        block = ctx.enter_context(nc.Block())
        NG = NT // GF
        res = x_new if joined else x

        raws = (rb[:].rearrange("p a d -> p (a d)"), ob[:].rearrange("p a d -> p (a d)"))
        pieces = []
        for src, hi, lo in ((w_gate, wg_hi, wg_lo), (w_up, wu_hi, wu_lo)):
            for c in range(DC):
                for a in range(2):
                    cut = (slice(None), c, slice(a * HALF_I, (a + 1) * HALF_I))
                    pieces.append((src[cut], hi[cut], lo[cut], HALF_I))
        for i in range(0, IC, 2):
            n = min(2, IC - i)
            flat = [t[:, i:i + n, :].rearrange("p a d -> p (a d)") for t in (w_down, wd_hi, wd_lo)]
            pieces.append((*flat, n * D))

        def tile_of(buf, g2, j):
            return buf[:, g2, :, j * P:(j + 1) * P]

        def groups(eng, step):
            with eng.Fori(0, NG // 2 - 2) as i:
                for g2 in range(2):
                    step(i * 2 + g2, g2, i)
            for g in range(NG - 4, NG):
                step(g, g % 2, g // 2)

        def exists(g):
            return not isinstance(g, int) or g < NG

        @block.sync
        def _(sp):
            for j in range(GF):
                sp.sem_inc(st[j], 16)
            for t in range(2 * GF):
                f.load(sp, t, t)
            for to, src in ((gs, gate_s), (us, up_s), (ds_, down_s.partition_broadcast(P))):
                sp.dma_start(to[:], src).then_inc(s_in, 16)
            for n, (src, hi, lo, w) in enumerate(pieces):
                if n >= 2:
                    sp.wait_ge(wlo_rdy, n - 1)
                sp.dma_start(raws[n % 2][:, 0:w], src).then_inc(raw_in[n % 2], 16)

            def tiles(g, g2, i):
                for j in range(GF):
                    f.sp_tile(sp, g * GF + j, g2 * GF + j, i, exists(g + 2))

            tiles(0, 0, 0)
            tiles(1, 1, 0)
            sp.wait_ge(wlo_rdy, len(pieces))

            def step(g, g2, i):
                for j in range(GF):
                    sp.wait_ge(o_rdy, g * GF + (j + 1))
                    if joined:
                        sp.wait_ge(f.x_st[g2 * GF + j], i * 16 + 16)
                    sp.dma_start(rb[:, j, :], res[bass.ds((g * GF + j) * P, P), :]).then_inc(r_in[j], 16)
                if exists(g + 2):
                    tiles(g + 2, g2, i + 1)
                for j in range(GF):
                    sp.wait_ge(o_rdy, g * GF + (j + 3))
                    sp.dma_start(x_out[bass.ds((g * GF + j) * P, P), :], ob[:, j, :]).then_inc(st[j], 16)

            groups(sp, step)
            f.sp_end(sp)
            for j in range(GF):
                sp.wait_ge(st[j], 16 * (NG + 1))

        @block.gpsimd
        def _(pool):
            if joined:
                f.gather(pool, 0, 2 * GF)
            for n, (src, hi, lo, w) in enumerate(pieces):
                pool.wait_ge(raw_in[n % 2], 16 * (n // 2 + 1))
                pool.tensor_scalar(hi, raws[n % 2][:, 0:w], 1.0, None, ALU.mult).then_inc(whi_rdy, 1)
            if joined:
                f.gather(pool, 2 * GF)

        @block.tensor
        def _(pe):
            f.free(pe)
            pe.sem_inc(h_rdy, 2)
            pe.sem_inc(o_rdy, 2)
            pe.sem_inc(hlo_rdy, 2)

            def turn(g, g2):
                for j in range(GF):
                    f.turn(pe, g * GF + j, j, j)

            turn(0, 0)
            pe.wait_ge(wlo_rdy, len(pieces))

            def step(g, g2, i):
                pe.wait_ge(f.lo_rdy, g * GF + (GF + 2))
                for m in range(IC):
                    k = (g2 * IC + m) % 2
                    pe.wait_ge(h_rdy, g * IC + (m + 1))
                    for q, (hi, lo) in enumerate(((wg_hi, wg_lo), (wu_hi, wu_lo))):
                        for c in range(DC):
                            w = (hi[:, c, m * P:(m + 1) * P], lo[:, c, m * P:(m + 1) * P])
                            for n, (a, b) in enumerate(products(w, (y_hi[:, g2, c, :], y_lo[:, g2, c, :]))):
                                ins = pe.matmul(gu[:, k, q, :], a, b, start=(c == 0 and n == 0), stop=(c == DC - 1 and n == 2))
                    ins.then_inc(gu_rdy, 1)
                if exists(g + 1):
                    turn(g + 1, 1 - g2)
                for j in range(GF):
                    pe.wait_ge(o_rdy, g * GF + (j + 1))
                    for m in range(IC):
                        if j == 0:
                            pe.wait_ge(hlo_rdy, g * IC + (m + 3))
                        hp = (h_hi[:, m, j * P:(j + 1) * P], h_lo[:, m, j * P:(j + 1) * P])
                        for n, (a, b) in enumerate(products(hp, (wd_hi[:, m, :], wd_lo[:, m, :]))):
                            ins = pe.matmul(dn[:, j, :], a, b, start=(m == 0 and n == 0), stop=(m == IC - 1 and n == 2))
                    ins.then_inc(dn_rdy, 1)

            groups(pe, step)

        @block.scalar
        def _(act):
            f.deviation(act, 0, 0)

            def front(g, g2):
                for j in range(GF):
                    if not (isinstance(g, int) and g * GF + j + 1 >= NT):
                        f.deviation(act, g * GF + (j + 1), (g2 * GF + j + 1) % 4)

            def group_hi(g, g2):
                for j in range(GF):
                    f.hi(act, g * GF + j, j, tile_of(y_hi, g2, j))

            front(0, 0)
            group_hi(0, 0)
            front(1, 1)
            act.wait_ge(s_in, 48)

            def part(g, g2, m):
                act.wait_ge(h_rdy, g * IC + (m + 3))
                act.activation(h_hi[:, m, :], hf[:, (g2 * IC + m) % 2, :], ACT.Copy).then_inc(hhi_rdy, 1)

            def step(g, g2, i):
                for m in range(IC):
                    k = (g2 * IC + m) % 2
                    act.wait_ge(gu_rdy, g * IC + (m + 1))
                    act.activation(sg[:, k, :], gu[:, k, 0, :], ACT.Silu, scale=gs[:, m:m + 1]).then_inc(sg_rdy, 1)
                    if m:
                        part(g, g2, m - 1)
                part(g, g2, IC - 1)
                if exists(g + 1):
                    group_hi(g + 1, 1 - g2)
                if exists(g + 2):
                    front(g + 2, g2)

            groups(act, step)

        @block.vector
        def _(dve):
            f.first(dve)

            def front(g, g2, i):
                for j in range(GF):
                    f.normalise(dve, g * GF + j, g2 * GF + j, i, j, not (isinstance(g, int) and g * GF + j + 1 >= NT))

            def group_lo(g, g2):
                for j in range(GF):
                    f.lo(dve, g * GF + j, j, tile_of(y_lo, g2, j), tile_of(y_hi, g2, j))

            front(0, 0, 0)
            for n, (src, hi, lo, w) in enumerate(pieces):
                dve.wait_ge(whi_rdy, n + 1)
                dve.tensor_tensor(lo, raws[n % 2][:, 0:w], hi.bitcast(F32), ALU.subtract).then_inc(wlo_rdy, 1)
            dve.wait_ge(s_in, 48)
            dve.tensor_scalar(ds_[:], ds_[:], 0.5, None, ALU.mult).then_inc(ds_rdy, 1)
            dve.wait_ge(ds_rdy, 1)
            group_lo(0, 0)
            front(1, 1, 0)

            def part(g, g2, m):
                dve.wait_ge(hhi_rdy, g * IC + (m + 1))
                dve.tensor_tensor(h_lo[:, m, :], hf[:, (g2 * IC + m) % 2, :], h_hi[:, m, :].bitcast(F32), ALU.subtract).then_inc(hlo_rdy, 1)

            def step(g, g2, i):
                for m in range(IC):
                    k = (g2 * IC + m) % 2
                    dve.wait_ge(sg_rdy, g * IC + (m + 1))
                    dve.wait_ge(hlo_rdy, g * IC + (m + 1))
                    dve.scalar_tensor_tensor(hf[:, k, :], gu[:, k, 1, :], us[:, m:m + 1], sg[:, k, :], ALU.mult, ALU.mult).then_inc(h_rdy, 1)
                    if m:
                        part(g, g2, m - 1)
                part(g, g2, IC - 1)
                if exists(g + 1):
                    group_lo(g + 1, 1 - g2)
                if exists(g + 2):
                    front(g + 2, g2, i + 1)
                for j in range(GF):
                    dve.wait_ge(dn_rdy, g * GF + (j + 1))
                    dve.wait_ge(st[j], i * 32 + (g2 * 16 + 16))
                    dve.tensor_tensor(ob[:, j, :], dn[:, j, :], ds_[:], ALU.mult).then_inc(o_half, 1)
                    dve.wait_ge(o_half, g * GF + (j + 1))
                    dve.wait_ge(r_in[j], i * 32 + (g2 * 16 + 16))
                    dve.tensor_tensor(ob[:, j, :], ob[:, j, :], rb[:, j, :], ALU.add).then_inc(o_rdy, 1)

            groups(dve, step)


def keyvalue_stage(nc, stage, const, x, w_kv, w_qT, w_out, b_kv, b_q, b_out, gamma, beta, angles, x_out):
    with ExitStack() as ctx:
        mem = Memory(nc, ctx, stage)
        NB = QT
        xb, yb, y2 = mem.sb("xb", [P, 2, D]), mem.sb("yb", [P, 2, D]), mem.sb("y2", [P, 2, D])
        xy = mem.sb("xy", [P, NB, D])
        yT = mem.sb("yT", [P, NB, D])
        bn, mv = mem.sb("bn", [P, 6]), mem.sb("mv", [P, 2])
        sd, rstd = mem.sb("sd", [P, 1]), mem.sb("rstd", [P, 1])
        bn2, mv2 = mem.sb("bn2", [P, 6]), mem.sb("mv2", [P, 2])
        sd2, rstd2 = mem.sb("sd2", [P, 1]), mem.sb("rstd2", [P, 1])
        pause = mem.sb("pause", [P, 1])
        t_hi, t_lo = mem.sb("t_hi", [P, 2, D], F32R), mem.sb("t_lo", [P, 2, D], F32R)
        raw = mem.sb("raw", [P, DC, 2 * D])
        wk_hi, wk_lo = mem.sb("wk_hi", [P, DC, 2 * D], F32R), mem.sb("wk_lo", [P, DC, 2 * D], F32R)
        wq, wo = mem.sb("wq", [P, DC, D]), mem.sb("wo", [P, DC, D])
        aw, m_raw = raw[:, :, 0:D], raw[:, :, D:2 * D]
        m_hi, m_lo = mem.sb("m_hi", [P, DC, D], F32R), mem.sb("m_lo", [P, DC, D], F32R)
        gam, bet, bq = mem.sb("gam", [P, DC]), mem.sb("bet", [P, DC]), mem.sb("bq", [P, DC])
        bet_w, bq_w = mem.sb("bet_w", [P, DC, P]), mem.sb("bq_w", [P, DC, P])
        borow = mem.sb("borow", [1, D])
        bkv, bo = mem.sb("bkv", [P, 2, D]), mem.sb("bo", [P, D])
        cs = mem.sb("cs", [P, 2, 2, P])
        kv, kvc, kvs = mem.sb("kv", [P, 2, 2, D]), mem.sb("kvc", [P, 2, 2, ROT]), mem.sb("kvs", [P, 2, 2, ROT])
        brow = kv[0:1, 0].rearrange("p v d -> p (v d)")
        prod, junk = mem.sb("prod", [P, 2, D]), mem.ps("junk", [P, D])
        sq, nrm, rn, rr = mem.sb("sq", [P, 2, 2]), mem.sb("nrm", [P, 2, 2]), mem.sb("rn", [P, 2, 2]), mem.sb("rr", [P, 2, 1])
        asum, afac = mem.sb("asum", [P, DC]), mem.sb("afac", [P, DC])
        ob = mem.sb("ob", [P, 2, D])
        tr = mem.ps("tr", [P, 2, D])
        kv_ps = mem.ps("kv", [P, 2, 2, D])
        a_ps = mem.ps("a", [P, 2, DC])
        names = ("w_in", "wide_rdy", "bk_rdy", "bk_kept", "whi_rdy", "wlo_rdy", "bn_rdy", "mv_rdy", "sd_rdy", "rs_rdy", "y_rdy",
                 "xy_rdy", "bn2_rdy", "mv2_rdy", "sd2_rdy", "rs2_rdy", "y2_rdy", "tr_rdy", "yT_rdy", "thi_rdy", "tlo_rdy",
                 "kv_rdy", "kv_kept", "cos_rdy", "sin_rdy", "rot_rdy", "sq_rdy", "nrm_rdy", "rn_rdy", "rr_rdy", "prod_rdy",
                 "a_rdy", "a_kept", "zero_rdy", "af_rdy", "aw_rdy", "m_rdy", "mraw_rdy", "mhi_rdy", "mlo_rdy", "b_rdy",
                 "b_kept", "ohi_rdy", "olo_rdy", "o_rdy", "o_half", "ob_rdy")
        sm = {n: mem.sem(n) for n in names}
        x_in, cs_in, o_st = (mem.sems(n, 2) for n in ("x_in", "cs_in", "o_st"))
        block = ctx.enter_context(nc.Block())

        def spans(eng, b, step):
            def one(s, k, n, head, last):
                step(s + b * NB, s, k, n + b * (NB // 2), head, last)

            for k in range(2):
                one(k, k, 0, True, False)
            with eng.Fori(1, NB // 2 - 1) as n:
                for k in range(2):
                    one(n * 2 + k, k, n, False, False)
            for k in range(2):
                one(NB - 2 + k, k, NB // 2 - 1, False, True)

        def chunks(flat):
            return flat.rearrange("p (c m) -> p c m", c=DC)

        @block.sync
        def _(sp):
            def load(t, k):
                sp.dma_start(xb[:, k, :], x[bass.ds(t * P, P), :]).then_inc(x_in[k], 16)

            def load_angles(s, k):
                sp.dma_start(cs[:, k], angles[bass.ds(s * P, P), :, :]).then_inc(cs_in[k], 16)

            for k in range(2):
                sp.sem_inc(o_st[k], 16)
            load(0, 0)
            load(1, 1)
            for to, src in ((gam, gamma), (bet, beta), (bq, b_q), (borow, b_out), (raw, w_kv), (wq, w_qT), (wo, w_out)):
                sp.dma_start(to[:], src).then_inc(sm["w_in"], 16)
            sp.dma_start(brow, b_kv).then_inc(sm["w_in"], 16)
            for b in range(B):
                for k in range(2):
                    load_angles(k, k)

                def first(t, s, k, i, head, last):
                    if not (last and b == B - 1):
                        sp.wait_ge(sm["xy_rdy"], t + 1)
                        load(t + 2, k)
                    if not last:
                        sp.wait_ge(sm["rot_rdy"], t * 2 + 2)
                        load_angles(s + 2, k)

                spans(sp, b, first)
                sp.wait_ge(sm["rot_rdy"], (b + 1) * NB * 2)

                def second(t, s, k, i, head, last):
                    sp.wait_ge(sm["ob_rdy"], t + 1)
                    sp.dma_start(x_out[bass.ds(t * P, P), :], ob[:, k, :]).then_inc(o_st[k], 16)

                spans(sp, b, second)
            for k in range(2):
                sp.wait_ge(o_st[k], 16 * (NT // 2 + 1))

        @block.tensor
        def _(pe):
            pe.sem_inc(sm["yT_rdy"], 2)
            pe.sem_inc(sm["kv_kept"], 2)
            pe.sem_inc(sm["a_kept"], 2)
            pe.sem_inc(sm["o_half"], 2)
            pe.wait_ge(sm["wide_rdy"], 2 * DC)
            pe.wait_ge(sm["w_in"], 128)
            for h in range(2):
                for c in range(DC):
                    pe.matmul(kv_ps[:, 0, h, :], bet_w[:, c, :], raw[:, c, h * D:(h + 1) * D], start=(c == 0), stop=False)
                ins = pe.matmul(kv_ps[:, 0, h, :], const["ones"][0:1, :], brow[:, h * D:(h + 1) * D], start=False, stop=True)
            ins.then_inc(sm["bk_rdy"], 1)

            def turn(t, k):
                pe.wait_ge(sm["y2_rdy"], t + 1)
                pe.wait_ge(sm["yT_rdy"], t + 1)
                for c in range(DC):
                    ins = pe.transpose(tr[:, k, c * P:(c + 1) * P], y2[:, k, c * P:(c + 1) * P], const["ident"][:])
                ins.then_inc(sm["tr_rdy"], 1)

            def keysvalues(t, k):
                pe.wait_ge(sm["tlo_rdy"], t + 1)
                pe.wait_ge(sm["kv_kept"], t + 1)
                for h in range(2):
                    for c in range(DC):
                        w = (wk_hi[:, c, h * D:(h + 1) * D], wk_lo[:, c, h * D:(h + 1) * D])
                        for n, (a, bb) in enumerate(products((t_hi[:, k, c * P:(c + 1) * P], t_lo[:, k, c * P:(c + 1) * P]), w)):
                            ins = pe.matmul(kv_ps[:, k, h, :], a, bb, start=(c == 0 and n == 0), stop=(c == DC - 1 and n == 2))
                ins.then_inc(sm["kv_rdy"], 1)

            def sums(t, k):
                pe.wait_ge(sm["prod_rdy"], t * 2 + 5)
                pe.wait_ge(sm["rr_rdy"], t + 1)
                pe.wait_ge(sm["a_kept"], t + 1)
                for c in range(DC):
                    ins = pe.matmul(a_ps[:, k, c:c + 1], prod[:, k, c * P:(c + 1) * P], rr[:, k, :], start=True, stop=True)
                ins.then_inc(sm["a_rdy"], 1)

            for b in range(B):
                if b:
                    pe.wait_ge(sm["o_half"], b * NB + 2)
                turn(b * NB, 0)
                if not b:
                    pe.wait_ge(sm["bk_kept"], 1)
                    pe.wait_ge(sm["wlo_rdy"], DC)
                keysvalues(b * NB, 0)
                turn(b * NB + 1, 1)

                def first(t, s, k, i, head, last):
                    if not (last and k == 1):
                        keysvalues(t + 1, 1 - k)
                    if not last:
                        turn(t + 2, k)
                    sums(t, k)

                spans(pe, b, first)
                pe.wait_ge(sm["aw_rdy"], DC * (b + 1))
                pe.wait_ge(sm["kv_kept"], 2 + (b + 1) * NB)
                for m in range(DC):
                    for c in range(DC):
                        ins = pe.matmul(kv_ps[:, m // 2, m % 2, :], wq[:, c, m * P:(m + 1) * P], aw[:, c, :], start=(c == 0), stop=(c == DC - 1))
                    ins.then_inc(sm["m_rdy"], 1)
                for c in range(DC):
                    pe.matmul(tr[:, 0, :], bq_w[:, c, :], aw[:, c, :], start=(c == 0), stop=False)
                for m in range(DC):
                    pe.wait_ge(sm["mraw_rdy"], DC * b + m + 1)
                    pe.matmul(tr[:, 0, :], bet_w[:, m, :], m_raw[:, m, :], start=False, stop=False)
                pe.matmul(tr[:, 0, :], const["ones"][0:1, :], borow[:], start=False, stop=True).then_inc(sm["b_rdy"], 1)
                pe.wait_ge(sm["mlo_rdy"], DC * (b + 1))
                pe.wait_ge(sm["b_kept"], b + 1)

                def second(t, s, k, i, head, last):
                    pe.wait_ge(sm["olo_rdy"], t + 1)
                    pe.wait_ge(sm["o_half"], t + 1)
                    for c in range(DC):
                        for n, (a, bb) in enumerate(products((t_hi[:, k, c * P:(c + 1) * P], t_lo[:, k, c * P:(c + 1) * P]), (m_hi[:, c, :], m_lo[:, c, :]))):
                            ins = pe.matmul(tr[:, k, :], a, bb, start=(c == 0 and n == 0), stop=(c == DC - 1 and n == 2))
                    ins.then_inc(sm["o_rdy"], 1)

                spans(pe, b, second)

        @block.gpsimd
        def _(pool):
            pool.sem_inc(sm["prod_rdy"], 3)

            def total(t, s, k):
                pool.wait_ge(sm["y_rdy"], t + 1)
                pool.tensor_tensor(xy[:, bass.ds(s, 1), :], xb[:, k, :].unsqueeze(1), yb[:, k, :].unsqueeze(1), ALU.add).then_inc(sm["xy_rdy"], 1)

            for b in range(B):
                if b:
                    pool.wait_ge(sm["ob_rdy"], b * NB)
                total(b * NB, 0, 0)
                total(b * NB + 1, 1, 1)

                def first(t, s, k, i, head, last):
                    pool.wait_ge(sm["kv_kept"], t + 3)
                    pool.wait_ge(cs_in[k], i * 16 + 16)
                    pool.wait_ge(sm["prod_rdy"], t * 2 + 1)
                    pairs = kv[:, k, :, 0:ROT].rearrange("p v (d two) -> p v d two", two=2)
                    c_pairs = kvc[:, k].rearrange("p v (d two) -> p v d two", two=2)
                    s_pairs = kvs[:, k].rearrange("p v (d two) -> p v d two", two=2)
                    for e in range(2):
                        cosine, sine = (spread(cs[:, k, n, :], 2, 1) for n in range(2))
                        pool.tensor_tensor(c_pairs[:, :, :, e], pairs[:, :, :, e], cosine, ALU.mult).then_inc(sm["cos_rdy"], 1)
                        pool.tensor_tensor(s_pairs[:, :, :, e], pairs[:, :, :, 1 - e], sine, ALU.mult).then_inc(sm["sin_rdy"], 1)
                    pool.wait_ge(sm["cos_rdy"], t * 2 + 2)
                    pool.wait_ge(sm["sin_rdy"], t * 2 + 2)
                    pool.tensor_tensor(c_pairs[:, :, :, 0], c_pairs[:, :, :, 0], s_pairs[:, :, :, 0], ALU.subtract).then_inc(sm["rot_rdy"], 1)
                    pool.tensor_tensor(c_pairs[:, :, :, 1], c_pairs[:, :, :, 1], s_pairs[:, :, :, 1], ALU.add).then_inc(sm["rot_rdy"], 1)
                    if not last:
                        total(t + 2, s + 2, k)

                spans(pool, b, first)

        @block.scalar
        def _(act):
            def root(t):
                act.wait_ge(sm["mv_rdy"], t + 1)
                act.activation(sd[:], mv[:, 1:2], ACT.Sqrt, bias=const["eps"][:]).then_inc(sm["sd_rdy"], 1)
                act.wait_ge(sm["mv2_rdy"], t + 1)
                act.activation(sd2[:], mv2[:, 1:2], ACT.Sqrt, bias=const["eps"][:]).then_inc(sm["sd2_rdy"], 1)

            def parts(t, s, k):
                act.wait_ge(sm["tr_rdy"], t + 1)
                act.activation(t_hi[:, k, :], tr[:, k, :], ACT.Copy).then_inc(sm["thi_rdy"], 1)
                act.activation(yT[:, bass.ds(s, 1), :], tr[:, k, :].unsqueeze(1), ACT.Copy).then_inc(sm["yT_rdy"], 1)

            for b in range(B):
                root(b * NB)
                parts(b * NB, 0, 0)
                root(b * NB + 1)

                def first(t, s, k, i, head, last):
                    if not (last and k == 1):
                        parts(t + 1, s + 1, 1 - k)
                    if not last:
                        root(t + 2)
                    act.wait_ge(sm["kv_kept"], t + 3)
                    for h in range(2):
                        act.activation(junk[:], kv[:, k, h, :], ACT.Square, accum_out=sq[:, k, h:h + 1]).then_inc(sm["sq_rdy"], 1)
                        act.wait_ge(sm["sq_rdy"], t * 2 + (h + 1))
                    act.activation(nrm[:, k, :], sq[:, k, :], ACT.Sqrt).then_inc(sm["nrm_rdy"], 1)

                spans(act, b, first)
                for m in range(DC):
                    act.wait_ge(sm["m_rdy"], b * DC + m + 1)
                    act.activation(m_raw[:, m, :], kv_ps[:, m // 2, m % 2, :], ACT.Copy).then_inc(sm["mraw_rdy"], 1)
                act.wait_ge(sm["yT_rdy"], (b + 1) * NB + 2)

                def second(t, s, k, i, head, last):
                    if head:
                        act.wait_ge(sm["kv_rdy"], (b + 1) * NB)
                    else:
                        act.wait_ge(sm["o_rdy"], t - 1)
                    act.activation(t_hi[:, k, :].unsqueeze(1), yT[:, bass.ds(s, 1), :], ACT.Copy).then_inc(sm["ohi_rdy"], 1)

                spans(act, b, second)

        @block.vector
        def _(dve):
            dve.wait_ge(sm["w_in"], 128)
            for to, src in ((bet_w, bet), (bq_w, bq)):
                for c in range(DC):
                    dve.tensor_scalar(to[:, c, :], const["ones"][:], src[:, c:c + 1], None, ALU.mult).then_inc(sm["wide_rdy"], 1)
            for c in range(DC):
                dve.tensor_scalar(wk_hi[:, c, :], raw[:, c, :], gam[:, c:c + 1], None, ALU.mult).then_inc(sm["whi_rdy"], 1)
            for c in range(DC):
                dve.wait_ge(sm["whi_rdy"], c + 1)
                dve.scalar_tensor_tensor(wk_lo[:, c, :], raw[:, c, :], gam[:, c:c + 1], wk_hi[:, c, :].bitcast(F32), ALU.mult, ALU.subtract).then_inc(sm["wlo_rdy"], 1)
            dve.wait_ge(sm["bk_rdy"], 1)
            dve.tensor_copy(bkv[:], kv_ps[:, 0]).then_inc(sm["bk_kept"], 1)

            def aggregate(stats, out, done, signal, t):
                dve.wait_ge(sm[done], t + 1)
                dve.tensor_copy(pause[:], const["eps"][:])
                dve.bn_aggr(out[:], stats[:]).then_inc(sm[signal], 1)

            def norms(t, k, i):
                dve.wait_ge(x_in[k], i * 16 + 16)
                dve.bn_stats(bn[:], xb[:, k, :]).then_inc(sm["bn_rdy"], 1)
                aggregate(bn, mv, "bn_rdy", "mv_rdy", t)
                dve.wait_ge(sm["sd_rdy"], t + 1)
                dve.reciprocal(rstd[:], sd[:]).then_inc(sm["rs_rdy"], 1)
                dve.wait_ge(sm["rs_rdy"], t + 1)
                dve.tensor_scalar(yb[:, k, :], xb[:, k, :], mv[:, 0:1], rstd[:], ALU.subtract, ALU.mult).then_inc(sm["y_rdy"], 1)
                dve.wait_ge(sm["y_rdy"], t + 1)
                dve.bn_stats(bn2[:], yb[:, k, :]).then_inc(sm["bn2_rdy"], 1)
                aggregate(bn2, mv2, "bn2_rdy", "mv2_rdy", t)
                dve.wait_ge(sm["sd2_rdy"], t + 1)
                dve.reciprocal(rstd2[:], sd2[:]).then_inc(sm["rs2_rdy"], 1)
                dve.wait_ge(sm["rs2_rdy"], t + 1)
                dve.tensor_scalar(y2[:, k, :], yb[:, k, :], mv2[:, 0:1], rstd2[:], ALU.subtract, ALU.mult).then_inc(sm["y2_rdy"], 1)

            def low_part(t, s, k):
                dve.wait_ge(sm["thi_rdy"], t + 1)
                dve.wait_ge(sm["yT_rdy"], t + 3)
                dve.tensor_tensor(t_lo[:, k, :].unsqueeze(1), yT[:, bass.ds(s, 1), :], t_hi[:, k, :].bitcast(F32).unsqueeze(1),
                                  ALU.subtract).then_inc(sm["tlo_rdy"], 1)

            def take_sums(t, k):
                dve.wait_ge(sm["a_rdy"], t + 1)
                dve.wait_ge(sm["a_kept"], t + 2)
                dve.tensor_tensor(asum[:], asum[:], a_ps[:, k, :], ALU.add).then_inc(sm["a_kept"], 1)

            for b in range(B):
                dve.memset(asum[:], 0.0).then_inc(sm["zero_rdy"], 1)
                norms(b * NB, 0, b * (NB // 2))
                low_part(b * NB, 0, 0)
                norms(b * NB + 1, 1, b * (NB // 2))

                def first(t, s, k, i, head, last):
                    dve.wait_ge(sm["kv_rdy"], t + 1)
                    dve.tensor_tensor(kv[:, k], kv_ps[:, k], bkv[:], ALU.add).then_inc(sm["kv_kept"], 1)
                    if not (last and k == 1):
                        low_part(t + 1, s + 1, 1 - k)
                    if not last:
                        norms(t + 2, k, i + 1)
                    if head and k == 0:
                        dve.wait_ge(sm["zero_rdy"], b + 1)
                    else:
                        take_sums(t - 1, 1 - k)
                    dve.wait_ge(sm["nrm_rdy"], t + 1)
                    dve.reciprocal(rn[:, k, :], nrm[:, k, :]).then_inc(sm["rn_rdy"], 1)
                    dve.tensor_tensor(prod[:, k, ROT:D], kv[:, k, 0, ROT:D], kv[:, k, 1, ROT:D], ALU.mult).then_inc(sm["prod_rdy"], 1)
                    dve.wait_ge(sm["rn_rdy"], t + 1)
                    dve.tensor_tensor(rr[:, k, :], rn[:, k, 0:1], rn[:, k, 1:2], ALU.mult).then_inc(sm["rr_rdy"], 1)
                    dve.wait_ge(sm["rot_rdy"], t * 2 + 2)
                    dve.tensor_tensor(prod[:, k, 0:ROT], kvc[:, k, 0, :], kvc[:, k, 1, :], ALU.mult).then_inc(sm["prod_rdy"], 1)

                spans(dve, b, first)
                take_sums((b + 1) * NB - 1, 1)
                dve.wait_ge(sm["a_kept"], (b + 1) * NB + 2)
                dve.tensor_scalar(afac[:], asum[:], 0.5, 0.5, ALU.mult, ALU.add).then_inc(sm["af_rdy"], 1)
                dve.wait_ge(sm["af_rdy"], b + 1)
                for c in range(DC):
                    dve.tensor_scalar(aw[:, c, :], wo[:, c, :], afac[:, c:c + 1], None, ALU.mult).then_inc(sm["aw_rdy"], 1)
                for m in range(DC):
                    dve.wait_ge(sm["mraw_rdy"], b * DC + m + 1)
                    dve.tensor_scalar(m_hi[:, m, :], m_raw[:, m, :], gam[:, m:m + 1], None, ALU.mult).then_inc(sm["mhi_rdy"], 1)
                    dve.wait_ge(sm["mhi_rdy"], b * DC + m + 1)
                    dve.scalar_tensor_tensor(m_lo[:, m, :], m_raw[:, m, :], gam[:, m:m + 1], m_hi[:, m, :].bitcast(F32),
                                             ALU.mult, ALU.subtract).then_inc(sm["mlo_rdy"], 1)
                dve.wait_ge(sm["b_rdy"], b + 1)
                dve.tensor_copy(bo[:], tr[:, 0, :]).then_inc(sm["b_kept"], 1)
                dve.wait_ge(sm["b_kept"], b + 1)

                def part(t, s, k):
                    dve.wait_ge(sm["ohi_rdy"], t + 1)
                    dve.tensor_tensor(t_lo[:, k, :].unsqueeze(1), yT[:, bass.ds(s, 1), :], t_hi[:, k, :].bitcast(F32).unsqueeze(1),
                                      ALU.subtract).then_inc(sm["olo_rdy"], 1)

                part(b * NB, 0, 0)

                def second(t, s, k, i, head, last):
                    if not (last and k == 1):
                        part(t + 1, s + 1, 1 - k)
                    dve.wait_ge(sm["o_rdy"], t + 1)
                    dve.wait_ge(o_st[k], i * 16 + 16)
                    dve.tensor_tensor(ob[:, k, :], tr[:, k, :], bo[:], ALU.add).then_inc(sm["o_half"], 1)
                    dve.wait_ge(sm["o_half"], t + 3)
                    dve.tensor_tensor(ob[:, k, :].unsqueeze(1), ob[:, k, :].unsqueeze(1), xy[:, bass.ds(s, 1), :], ALU.add).then_inc(sm["ob_rdy"], 1)

                spans(dve, b, second)


def build(nc, a, out):
    def scratch(name, shape):
        return nc.dram_tensor(name, shape, F32, kind="Internal").ap()

    x = [a["x"]] + [scratch(f"x{n}", (T, D)) for n in range(1, 6)]
    xs, ys = scratch("xs", (SLOTS, D)), scratch("ys", (SLOTS, D))
    q_parts, m_rows = scratch("q_parts", (2, HEADS * HD, T)), scratch("m_rows", (2, HEADS, P))
    with ExitStack() as ctx:
        mem = Memory(nc, ctx, "all")
        const = {"ident": mem.sb("ident", [P, P]), "before": mem.sb("before", [P, P]), "ones": mem.sb("ones", [P, P]), "eps": mem.sb("eps", [P, 1])}
        plan = {"slot": mem.sb("slot", [P, TOPK, NT], U32), "weight": mem.sb("weight", [P, TOPK, NT]),
                "tile": mem.sb("tile", [1, 2, SLOT_TILES], I32), "release": mem.sb("release", [1, E], I32)}
        setup_stage(nc, const)

        def experts(n, src, clear):
            routing_stage(nc, f"route{n}", const, src, a["router_scale"], a["router_w"], a["expert_scale"], xs, plan, clear)
            expert_stage(nc, f"expert{n}", const, xs, ys, a["experts"], plan)

        def ffn(n, src, joined_to, joined, to):
            ffn_stage(nc, f"ffn{n}", const, src, joined_to, joined, a["gate_w"], a["up_w"], a["down_w"], a["gate_s"], a["up_s"], a["down_s"], to)

        experts(0, x[0], True)
        with ExitStack() as attended:
            attn = Memory(nc, attended, "attended").sb("attn", [P, NT, 2, 2 * P])
            with ExitStack() as attention:
                held = Memory(nc, attention, "attention")
                kst, v = held.sb("kst", [P, T], F32R), held.sb("v", [P, NT, HD])
                projection_stage(nc, "project", const, x[0], x[1], (ys, plan), a["q_w"], a["k_w"], a["v_w"], q_parts, kst, v)
                attention_stage(nc, "attend", const, q_parts, kst, v, m_rows, attn)
            output_stage(nc, "output", const, attn, a["o_w"], x[1], x[2])
        experts(1, x[2], False)
        ffn(0, x[2], x[3], (ys, plan), x[4])
        keyvalue_stage(nc, "keyvalue", const, x[4], a["kv_w"], a["qT_w"], a["out_w"], a["kv_b"], a["q_b"], a["out_b"],
                       a["gamma"], a["beta"], a["angles"], x[5])
        ffn(1, x[5], None, None, out)


def layout(np, i):
    def chunked(w):
        return w.reshape(w.shape[0] // P, P, -1).transpose(1, 0, 2)

    def column(v):
        return v.reshape(-1, P).T

    gate_up = i["L0_ffn_gating_einsum"].transpose(0, 3, 1, 2).reshape(E, DC, P, WPIECE).transpose(0, 2, 1, 3)
    down = i["L0_ffn_linear"].reshape(E, H // P // 2, 2, P, D).transpose(0, 3, 1, 2, 4).reshape(E, P, H // P // 2, WPIECE)
    w_in, b_in = i["L1_attn_W_in"], i["L1_attn_b_in"]
    inv_freq = np.float32(1.0) / np.float32(10000.0) ** (np.arange(0, ROT, 2, dtype=np.float32) / np.float32(ROT))
    turns = np.arange(S, dtype=np.float32)[:, None] * inv_freq[None, :]
    return {
        "x": i["L0_attn_x"].reshape(T, D),
        "router_scale": column(i["L0_ffn_router_scale"]), "router_w": chunked(i["L0_ffn_router_logits"]),
        "expert_scale": i["L0_ffn_per_expert_scale"], "experts": np.concatenate([gate_up, down], axis=2),
        "q_w": chunked(i["L0_attn_q_w"].T), "k_w": chunked(i["L0_attn_k_w"].T), "v_w": chunked(i["L0_attn_v_w"].T),
        "o_w": i["L0_attn_o_w"].T.reshape(2, HALF // 2, 2, HD, D).transpose(1, 3, 0, 2, 4).reshape(P, DC, D),
        "gate_w": chunked(i["L1_ffn_gate_w"].T), "up_w": chunked(i["L1_ffn_up_w"].T), "down_w": chunked(i["L1_ffn_down_w"].T),
        "gate_s": column(i["L1_ffn_gate_s"]), "up_s": column(i["L1_ffn_up_s"]), "down_s": i["L1_ffn_down_s"],
        "kv_w": chunked(w_in[:, D:]), "qT_w": chunked(w_in[:, :D].T), "out_w": chunked(i["L1_attn_W_out"]),
        "kv_b": b_in[None, D:], "q_b": column(b_in[:D]), "out_b": i["L1_attn_b_out"][None, :],
        "gamma": column(i["L1_attn_gamma"]), "beta": column(i["L1_attn_beta"]),
        "angles": np.stack([np.cos(turns), np.sin(turns)], axis=1),
    }


def kernel(**inputs):
    import numpy as np
    import concourse.bacc as bacc
    from concourse.bass_utils import run_bass_kernel_spmd

    nc = bacc.Bacc("TRN2", target_bir_lowering=False, num_devices=1)
    arrays = {n: np.ascontiguousarray(v) for n, v in layout(np, {n: np.asarray(v) for n, v in inputs.items()}).items()}
    drams = {n: nc.dram_tensor(f"{n}_dram", v.shape, mybir.dt.from_np(v.dtype), kind="ExternalInput").ap() for n, v in arrays.items()}
    out = nc.dram_tensor("out_dram", (T, D), F32, kind="ExternalOutput").ap()
    build(nc, drams, out)
    r = run_bass_kernel_spmd(nc, [{f"{n}_dram": v for n, v in arrays.items()}], core_ids=[0])
    return r.results[0]["out_dram"].reshape(B, S, D)
```

```python
from contextlib import ExitStack

import concourse.bass as bass
from concourse import mybir

F32 = mybir.dt.float32
F32R = mybir.dt.float32r
I32 = mybir.dt.int32
U32 = mybir.dt.uint32
ALU = mybir.AluOpType
ACT = mybir.ActivationFunctionType
AX = mybir.AxisListType

P = 128
B, S, D = 2, 2048, 512
T = B * S
NT = T // P
DC = D // P
E, H = 8, 512
TOPK = 2
SLOT_TILES = T * TOPK // P + E
SLOTS = SLOT_TILES * P
LEVELS = T // P
HEADS, HD = 16, 32
INTER = 1408
IC = INTER // P
ROT = D // 2
LN_EPS = 1e-5
RMS_EPS = 1e-6
WPIECES = 6
WPIECE = 2 * H


class Memory:

    def __init__(self, nc, ctx, stage):
        self.nc, self.ctx, self.stage = nc, ctx, stage
        self.sems_held = []
        ctx.callback(self.zero_sems)

    def sb(self, name, shape, dt=F32):
        return self.ctx.enter_context(self.nc.sbuf_tensor(f"{self.stage}_{name}", shape, dt))

    def ps(self, name, shape, dt=F32):
        return self.ctx.enter_context(self.nc.psum_tensor(f"{self.stage}_{name}_ps", shape, dt))

    def sem(self, name):
        handle = self.nc.alloc_semaphore(f"{self.stage}_{name}_sem")
        self.sems_held.append(handle)
        return handle

    def zero_sems(self):
        if self.sems_held:
            self.nc.clear_and_free_semaphores(self.sems_held)
            self.nc.all_engine_barrier()

    def sems(self, name, n):
        return [self.sem(f"{name}{k}") for k in range(n)]


def looped(eng, n, unroll, step):
    rounds = n // unroll
    with eng.Fori(0, rounds - 1) as i:
        for k in range(unroll):
            step(i * unroll + k, k, i, False)
    for k in range(unroll):
        step((rounds - 1) * unroll + k, k, rounds - 1, True)


def spread(ap, n, axis=2):
    wide = ap.unsqueeze(axis)
    shape = list(wide.shape)
    shape[axis] = n
    return wide.to_broadcast(shape)


def setup_stage(nc, const):
    with ExitStack() as ctx:
        mem = Memory(nc, ctx, "setup")
        filled, picked = mem.sem("filled"), mem.sem("picked")
        block = ctx.enter_context(nc.Block())

        @block.gpsimd
        def _(pool):
            pool.memset(const["ident"][:], 0.0).then_inc(filled, 1)
            pool.memset(const["before"][:], 1.0).then_inc(filled, 1)
            pool.memset(const["ones"][:], 1.0).then_inc(filled, 1)
            pool.memset(const["eps"][:], LN_EPS).then_inc(filled, 1)
            pool.wait_ge(filled, 4)
            pool.affine_select(out=const["ident"][:], in_=const["ident"][:], compare_op=ALU.not_equal, fill=1.0,
                               base=0, pattern=[[-1, P]], channel_multiplier=1).then_inc(picked, 1)
            pool.affine_select(out=const["before"][:], in_=const["before"][:], compare_op=ALU.is_gt, fill=0.0,
                               base=0, pattern=[[1, P]], channel_multiplier=-1).then_inc(picked, 1)
            pool.wait_ge(picked, 2)


def routing_stage(nc, stage, const, x, scale, logits_w, expert_scale, w_experts, box, xs, plan, clear):
    with ExitStack() as ctx:
        mem = Memory(nc, ctx, stage)
        NX = 4
        xb = mem.sb("xb", [P, NX, D])
        y = mem.sb("y", [P, NT, D])
        yb = mem.sb("yb", [P, 2, D])
        yT = mem.sb("yT", [P, 2, D])
        bn = mem.sb("bn", [P, 2, 6])
        mv = mem.sb("mv", [P, 2, 2])
        var = mem.sb("var", [P, NT])
        sd = mem.sb("sd", [P, NT])
        rstd = mem.sb("rstd", [P, NT])
        wl = mem.sb("wl", [P, DC, E])
        rs = mem.sb("rs", [P, DC])
        wr = mem.sb("wr", [P, DC, E])
        esc = mem.sb("esc", [P, E])
        zero = box["raw"][:].rearrange("p n m -> p (n m)")
        small = {n: mem.sb(n, [P, NT]) for n in
                 ("ms", "msd", "rr", "top1", "top2", "at1", "at2", "gap", "egap", "den", "w1", "w2", "s1", "s2", "c1", "c2", "p1", "p2")}
        wide = {n: mem.sb(n, [P, NT, E]) for n in
                ("lg", "eq", "cand", "oh1", "oh2", "left", "both", "tot", "sumA", "sumB", "pos", "tmp", "tmp2")}
        iota_e = mem.sb("iota_e", [P, E])
        iota_e8 = mem.sb("iota_e8", [P, E])
        levels = mem.sb("levels", [P, E, LEVELS])
        over = mem.sb("over", [P, E, LEVELS])
        tiles = mem.sb("tiles", [P, E])
        endA = mem.sb("endA", [P, E])
        endB = mem.sb("endB", [P, E])
        base = mem.sb("base", [P, E])
        jota = mem.sb("jota", [1, SLOT_TILES, E])
        flip = mem.sb("flip", [1, E])
        upto = mem.sb("upto", [1, E])
        past, past2 = (xb[0:1].rearrange("p n d -> p (n d)")[:, n * SLOT_TILES * E:(n + 1) * SLOT_TILES * E]
                       .rearrange("p (j e) -> p j e", e=E) for n in range(2))
        tabf = mem.sb("tabf", [1, 2, SLOT_TILES])
        relf = mem.sb("relf", [1, E])
        tr = mem.ps("tr", [P, 2, D])
        lg_ps = mem.ps("lg", [P, NT, E])
        pre_ps = mem.ps("pre", [P, NT, E])
        tot_ps = mem.ps("tot", [P, NT, E])

        x_in, raw_in = mem.sems("x_in", NX), mem.sems("raw_in", 2)
        raw_free, whi_rdy, wlo_rdy = mem.sem("raw_free"), mem.sem("whi_rdy"), mem.sem("wlo_rdy")
        FIRST = 2 * WPIECES
        w_in, wr_rdy, zeroed, cleared, iotas = (mem.sem(n) for n in ("w_in", "wr_rdy", "zeroed", "cleared", "iotas"))
        bn_rdy, mv_rdy, sd_rdy, rstd_rdy, y_rdy, tr_rdy, yT_rdy, lg_rdy = (
            mem.sem(n) for n in ("bn_rdy", "mv_rdy", "sd_rdy", "rstd_rdy", "y_rdy", "tr_rdy", "yT_rdy", "lg_rdy"))
        step_done, msd_rdy, gap_rdy, egap_rdy, both_rdy, counted, pos_rdy, scattered = (
            mem.sem(n) for n in ("step_done", "msd_rdy", "gap_rdy", "egap_rdy", "both_rdy", "counted", "pos_rdy", "scattered"))
        kept = mem.sem("kept")
        block = ctx.enter_context(nc.Block())

        @block.sync
        def _(sp):
            def load(t, k):
                sp.dma_start(xb[:, k, :], x[bass.ds(t * P, P), :]).then_inc(x_in[k], 16)

            for t in range(NX):
                load(t, t)
            sp.dma_start(wl[:], logits_w).then_inc(w_in, 16)
            sp.dma_start(rs[:], scale).then_inc(w_in, 16)
            sp.dma_start(esc[:], expert_scale.partition_broadcast(P)).then_inc(w_in, 16)

            def step(t, k, i, last):
                if not last:
                    sp.wait_ge(y_rdy, t + 1)
                    load(t + NX, k)

            looped(sp, NT, NX, step)
            if clear:
                sp.wait_ge(cleared, 16 * (SLOT_TILES // 4))
            for n in range(FIRST):
                if n >= 2:
                    sp.wait_ge(wlo_rdy, n - 1)
                sp.dma_start(box["raw"][:, n % 2, :], w_experts[n // WPIECES, :, n % WPIECES, :]).then_inc(raw_in[n % 2], 16)

        @block.gpsimd
        def _(pool):
            if clear:
                pool.memset(zero, 0.0).then_inc(zeroed, 1)
            pool.iota(iota_e[:], [[1, E]], base=0, channel_multiplier=0, allow_small_or_imprecise_dtypes=True).then_inc(iotas, 1)
            pool.iota(iota_e8[:], [[1, E]], base=E, channel_multiplier=0, allow_small_or_imprecise_dtypes=True).then_inc(iotas, 1)
            pool.iota(levels[:], [[0, E], [P, LEVELS]], base=0, channel_multiplier=0, allow_small_or_imprecise_dtypes=True).then_inc(iotas, 1)
            pool.iota(jota[:], [[1, SLOT_TILES], [0, E]], base=0, channel_multiplier=0, allow_small_or_imprecise_dtypes=True).then_inc(iotas, 1)
            for e in range(E):
                pool.memset(flip[:, e:e + 1], 0.0 if e == E - 1 else (-1.0) ** e).then_inc(iotas, 1)
                pool.memset(upto[:, e:e + 1], 0.0 if e == E - 1 else 1.0).then_inc(iotas, 1)
            pool.wait_ge(kept, NT + 2)
            pool.wait_ge(pos_rdy, 1)
            if clear:
                pool.wait_ge(cleared, 16 * (SLOT_TILES // 4))
            for t in range(NT):
                for k in range(TOPK):
                    pool.indirect_dma_start(
                        xs, bass.IndirectOffsetOnAxis(ap=plan["slot"][:, k, t:t + 1], axis=0), y[:, t, :], None,
                    ).then_inc(scattered, 16)
            pool.wait_ge(scattered, 16 * NT * TOPK)

        @block.scalar
        def _(act):
            def zeros(n):
                act.dma_start(xs[bass.ds(n * 4 * P, 4 * P), :].rearrange("(p r) d -> p (r d)", r=4), zero).then_inc(cleared, 16)

            def deviation(t, k):
                act.wait_ge(mv_rdy, t + 1)
                act.activation(sd[:, bass.ds(t, 1)], mv[:, k % 2, 1:2], ACT.Sqrt, bias=const["eps"][:]).then_inc(sd_rdy, 1)

            def step(t, k, i, last):
                if not (last and k == NX - 1):
                    deviation(t + 1, k + 1)
                act.wait_ge(tr_rdy, t + 1)
                act.activation(yT[:, k % 2, :], tr[:, k % 2, :], ACT.Copy).then_inc(yT_rdy, 1)
                act.activation(y[:, bass.ds(t, 1), :], yb[:, k % 2, :].unsqueeze(1), ACT.Copy).then_inc(kept, 1)
                if clear and k % 2:
                    zeros(i * (NX // 2) + k // 2)

            deviation(0, 0)
            act.sem_inc(kept, 2)
            if clear:
                act.wait_ge(zeroed, 1)
            looped(act, NT, NX, step)
            if clear:
                for n in range(NT // 2, SLOT_TILES // 4):
                    zeros(n)
            act.wait_ge(step_done, 3)
            act.activation(small["msd"][:], small["ms"][:], ACT.Sqrt).then_inc(msd_rdy, 1)
            act.wait_ge(gap_rdy, 1)
            act.activation(small["egap"][:], small["gap"][:], ACT.Exp).then_inc(egap_rdy, 1)
            for n in range(FIRST):
                act.wait_ge(raw_in[n % 2], 16 * (n // 2 + 1))
                act.activation(box["hi"][:, n * WPIECE:(n + 1) * WPIECE], box["raw"][:, n % 2, :], ACT.Copy).then_inc(whi_rdy, 1)

        @block.tensor
        def _(pe):
            pe.sem_inc(yT_rdy, 2)
            pe.wait_ge(wr_rdy, DC)

            def turn(t, k):
                pe.wait_ge(y_rdy, t + 1)
                pe.wait_ge(yT_rdy, t + 1)
                for c in range(DC):
                    ins = pe.transpose(tr[:, k % 2, c * P:(c + 1) * P], yb[:, k % 2, c * P:(c + 1) * P], const["ident"][:])
                ins.then_inc(tr_rdy, 1)

            turn(0, 0)

            def step(t, k, i, last):
                if not (last and k == NX - 1):
                    turn(t + 1, k + 1)
                pe.wait_ge(yT_rdy, t + 3)
                for c in range(DC):
                    ins = pe.matmul(lg_ps[:, bass.ds(t, 1), :], yT[:, k % 2, c * P:(c + 1) * P], wr[:, c, :],
                                    start=(c == 0), stop=(c == DC - 1), skip_group_check=True)
                ins.then_inc(lg_rdy, 1)

            looped(pe, NT, NX, step)
            pe.wait_ge(both_rdy, 1)
            pe.matmul(pre_ps[:], const["before"][:], wide["both"][:], start=True, stop=True)
            pe.matmul(tot_ps[:], const["ones"][:], wide["both"][:], start=True, stop=True).then_inc(counted, 1)

        @block.vector
        def _(dve):
            steps = [0]

            def then(ins):
                steps[0] += 1
                ins.then_inc(step_done, 1)
                dve.wait_ge(step_done, steps[0])

            dve.wait_ge(w_in, 48)
            for c in range(DC):
                dve.tensor_scalar(wr[:, c, :], wl[:, c, :], rs[:, c:c + 1], float(D) ** -0.5, ALU.mult, ALU.mult).then_inc(wr_rdy, 1)

            def stats(t, k, i):
                dve.wait_ge(x_in[k], 16 * (i + 1))
                dve.bn_stats(bn[:, k % 2, :], xb[:, k, :]).then_inc(bn_rdy, 1)

            def moments(t, k):
                dve.bn_aggr(mv[:, k % 2, :], bn[:, k % 2, :]).then_inc(mv_rdy, 1)
                dve.wait_ge(mv_rdy, t + 1)
                dve.tensor_copy(var[:, bass.ds(t, 1)], mv[:, k % 2, 1:2])

            stats(0, 0, 0)
            dve.wait_ge(bn_rdy, 1)
            moments(0, 0)

            def step(t, k, i, last):
                ahead = not (last and k == NX - 1)
                kn = (k + 1) % NX
                if ahead:
                    stats(t + 1, kn, i + (1 if kn == 0 else 0))
                    dve.wait_ge(bn_rdy, t + 2)
                dve.wait_ge(sd_rdy, t + 1)
                dve.reciprocal(rstd[:, bass.ds(t, 1)], sd[:, bass.ds(t, 1)]).then_inc(rstd_rdy, 1)
                if ahead:
                    moments(t + 1, kn)
                dve.wait_ge(rstd_rdy, t + 1)
                dve.wait_ge(kept, t + 1)
                dve.tensor_scalar(yb[:, k % 2, :], xb[:, k, :], mv[:, k % 2, 0:1], rstd[:, bass.ds(t, 1)],
                                  ALU.subtract, ALU.mult).then_inc(y_rdy, 1)

            looped(dve, NT, NX, step)
            then(dve.tensor_tensor(small["ms"][:], rstd[:], rstd[:], ALU.mult))
            then(dve.tensor_tensor(small["ms"][:], small["ms"][:], var[:], ALU.mult))
            then(dve.tensor_scalar(small["ms"][:], small["ms"][:], RMS_EPS, None, ALU.add))
            dve.wait_ge(msd_rdy, 1)
            then(dve.reciprocal(small["rr"][:], small["msd"][:]))
            dve.wait_ge(lg_rdy, NT)
            dve.wait_ge(iotas, 4 + 2 * E)
            lg = wide["lg"]
            then(dve.tensor_tensor(lg[:], lg_ps[:], spread(small["rr"][:], E), ALU.mult))

            def best(values, top, at, onehot):
                then(dve.tensor_reduce(top[:], values[:], AX.X, ALU.max))
                then(dve.tensor_tensor(wide["eq"][:], values[:], spread(top[:], E), ALU.is_equal))
                then(dve.tensor_scalar(wide["cand"][:], wide["eq"][:], -float(E), None, ALU.mult))
                then(dve.tensor_tensor(wide["cand"][:], wide["cand"][:], spread(iota_e8[:], NT, 1), ALU.add))
                then(dve.tensor_reduce(at[:], wide["cand"][:], AX.X, ALU.min))
                then(dve.tensor_tensor(onehot[:], spread(at[:], E), spread(iota_e[:], NT, 1), ALU.is_equal))

            best(lg, small["top1"], small["at1"], wide["oh1"])
            then(dve.scalar_tensor_tensor(wide["left"][:], wide["oh1"][:], -3e38, lg[:], ALU.mult, ALU.add))
            best(wide["left"], small["top2"], small["at2"], wide["oh2"])
            dve.tensor_tensor(small["gap"][:], small["top2"][:], small["top1"][:], ALU.subtract).then_inc(gap_rdy, 1)
            dve.tensor_tensor(wide["both"][:], wide["oh1"][:], wide["oh2"][:], ALU.add).then_inc(both_rdy, 1)
            dve.wait_ge(egap_rdy, 1)
            then(dve.tensor_scalar(small["den"][:], small["egap"][:], 1.0, None, ALU.add))
            then(dve.reciprocal(small["w1"][:], small["den"][:]))
            then(dve.tensor_tensor(small["w2"][:], small["w1"][:], small["egap"][:], ALU.mult))
            for k, (oh, s, w) in enumerate((("oh1", "s1", "w1"), ("oh2", "s2", "w2"))):
                then(dve.tensor_tensor(wide["tmp"][:], wide[oh][:], spread(esc[:], NT, 1), ALU.mult))
                then(dve.tensor_reduce(small[s][:], wide["tmp"][:], AX.X, ALU.add))
                then(dve.scalar_tensor_tensor(plan["weight"][:, k, :], small[s][:], 0.5, small[w][:], ALU.mult, ALU.mult))
            dve.wait_ge(counted, 1)
            then(dve.tensor_copy(wide["tot"][:], tot_ps[:]))
            now, nxt = wide["tot"], wide["sumA"]
            for sh in (1, 2, 4, 8, 16):
                then(dve.tensor_copy(nxt[:, 0:sh, :], now[:, 0:sh, :]))
                then(dve.tensor_tensor(nxt[:, sh:NT, :], now[:, sh:NT, :], now[:, 0:NT - sh, :], ALU.add))
                now, nxt = nxt, (wide["sumB"] if nxt is wide["sumA"] else wide["sumA"])
            then(dve.tensor_tensor(over[:], spread(now[:, NT - 1, :], LEVELS), levels[:], ALU.is_gt))
            then(dve.tensor_reduce(tiles[:], over[:], AX.X, ALU.add))
            then(dve.tensor_scalar(tiles[:], tiles[:], 1.0, None, ALU.max))
            end, nend = tiles, endA
            for sh in (1, 2, 4):
                then(dve.tensor_copy(nend[:, 0:sh], end[:, 0:sh]))
                then(dve.tensor_tensor(nend[:, sh:E], end[:, sh:E], end[:, 0:E - sh], ALU.add))
                end, nend = nend, (endB if nend is endA else endA)
            then(dve.tensor_tensor(base[:], end[:], tiles[:], ALU.subtract))
            then(dve.tensor_scalar(base[:], base[:], float(P), None, ALU.mult))
            then(dve.tensor_tensor(wide["pos"][:], now[:], wide["tot"][:], ALU.subtract))
            then(dve.tensor_tensor(wide["pos"][:], wide["pos"][:], pre_ps[:], ALU.add))
            then(dve.tensor_tensor(wide["pos"][:], wide["pos"][:], spread(base[:], NT, 1), ALU.add))
            for k, (oh, p) in enumerate((("oh1", "p1"), ("oh2", "p2"))):
                then(dve.tensor_tensor(wide["tmp2"][:], wide[oh][:], wide["pos"][:], ALU.mult))
                then(dve.tensor_reduce(small[p][:], wide["tmp2"][:], AX.X, ALU.add))
                then(dve.tensor_copy(plan["slot"][:, k, :], small[p][:]))
            dve.sem_inc(pos_rdy, 1)
            then(dve.tensor_tensor(past, jota[:], spread(end[0:1, :], SLOT_TILES, 1), ALU.is_ge))
            then(dve.tensor_tensor(past2, past, spread(upto[:], SLOT_TILES, 1), ALU.mult))
            then(dve.tensor_reduce(tabf[:, 0, :], past2, AX.X, ALU.add))
            then(dve.tensor_scalar(tabf[:, 0, :], tabf[:, 0, :], 1.0, None, ALU.add))
            then(dve.tensor_tensor(past2, past, spread(flip[:], SLOT_TILES, 1), ALU.mult))
            then(dve.tensor_reduce(tabf[:, 1, :], past2, AX.X, ALU.add))
            then(dve.tensor_scalar(tabf[:, 1, :], tabf[:, 1, :], float(WPIECES * WPIECE), None, ALU.mult))
            then(dve.tensor_copy(plan["tile"][:], tabf[:]))
            then(dve.memset(relf[:], 1.0))
            then(dve.tensor_scalar(relf[:, 2:E], end[0:1, 0:E - 2], 1.0, None, ALU.add))
            then(dve.tensor_copy(plan["release"][:], relf[:]))
            for n in range(FIRST):
                dve.wait_ge(whi_rdy, n + 1)
                cut = slice(n * WPIECE, (n + 1) * WPIECE)
                dve.tensor_tensor(box["lo"][:, cut], box["raw"][:, n % 2, :], box["hi"][:, cut].bitcast(F32), ALU.subtract).then_inc(wlo_rdy, 1)


def expert_stage(nc, stage, const, xs, ys, w_experts, box, plan):
    with ExitStack() as ctx:
        mem = Memory(nc, ctx, stage)
        w_hi, w_lo, raw = box["hi"], box["lo"], box["raw"]
        xb = mem.sb("xb", [P, 2, D])
        x_hi = mem.sb("x_hi", [P, 2, D], F32R)
        x_lo = mem.sb("x_lo", [P, 2, D], F32R)
        gl = mem.sb("gl", [P, 2, H])
        ac = mem.sb("ac", [P, 2, H])
        a_hi = mem.sb("a_hi", [P, 2, H], F32R)
        a_lo = mem.sb("a_lo", [P, 2, H], F32R)
        ob = mem.sb("ob", [P, 2, D])
        tr = mem.ps("tr", [P, 2, D])
        gu = mem.ps("gu", [P, 2, H])
        at = mem.ps("at", [P, 2, H])
        dn = mem.ps("dn", [P, 2, D])

        raw_in, raw_free, w_rdy, hi_w = mem.sems("raw_in", 2), mem.sem("raw_free"), mem.sem("w_rdy"), mem.sem("hi_w")
        x_in, st = mem.sems("x_in", 2), mem.sems("st", 2)
        tr_rdy, xhi_rdy, xlo_rdy, gu_rdy, gl_rdy, ac_rdy, at_rdy, ahi_rdy, alo_rdy, dn_rdy, ob_rdy = (
            mem.sem(n) for n in ("tr_rdy", "xhi_rdy", "xlo_rdy", "gu_rdy", "gl_rdy", "ac_rdy", "at_rdy", "ahi_rdy",
                                 "alo_rdy", "dn_rdy", "ob_rdy"))
        block = ctx.enter_context(nc.Block())
        NTL = SLOT_TILES

        @block.gpsimd
        def _(pool):
            def load(e, n, s):
                pool.dma_start(raw[:, s, :], w_experts[bass.ds(e, 1), :, n, :].rearrange("a p m -> (a p) m")).then_inc(raw_in[s], 16)

            def split(e, par, i):
                pool.wait_ge(dn_rdy, pool.value_load(plan["release"][0:1, bass.ds(e, 1)], min_val=1, max_val=SLOT_TILES + 1))
                for n in range(WPIECES):
                    s = n % 2
                    g = e * WPIECES + n
                    later = e - 2
                    pool.wait_ge(raw_in[s], 16 * (later * (WPIECES // 2) + n // 2 + 1))
                    o = (par * WPIECES + n) * WPIECE
                    pool.tensor_tensor(w_hi[:, o:o + WPIECE], raw[:, s, :], const["ones"][:, 0:1].to_broadcast([P, WPIECE]), ALU.mult).then_inc(hi_w, 1)
                    pool.wait_ge(hi_w, later * WPIECES + (n + 1))
                    ins = pool.tensor_tensor(w_lo[:, o:o + WPIECE], raw[:, s, :], w_hi[:, o:o + WPIECE].bitcast(F32), ALU.subtract)
                    ins.then_inc(w_rdy, 1)
                    pool.wait_ge(w_rdy, g + 1)
                    if n + 2 < WPIECES:
                        load(e, n + 2, s)
                    else:
                        yield n + 2 - WPIECES, s

            pool.sem_inc(w_rdy, 2 * WPIECES)
            load(2, 0, 0)
            load(2, 1, 1)
            with pool.Fori(1, E // 2 - 1) as i:
                for par in range(2):
                    for n, s in split(i * 2 + par, par, i):
                        load(i * 2 + par + 1, n, s)
            for n, s in split(E - 2, 0, E // 2 - 1):
                load(E - 1, n, s)
            for n, s in split(E - 1, 1, E // 2 - 1):
                pass

        @block.sync
        def _(sp):
            def load(j, k):
                sp.dma_start(xb[:, k, :], xs[bass.ds(j * P, P), :]).then_inc(x_in[k], 16)

            sp.sem_inc(st[0], 16)
            sp.sem_inc(st[1], 16)
            load(0, 0)
            load(1, 1)

            def step(j, k, i, last):
                if not last:
                    sp.wait_ge(tr_rdy, j + 1)
                    load(j + 2, k)
                sp.wait_ge(ob_rdy, j + 1)
                sp.dma_start(ys[bass.ds(j * P, P), :], ob[:, k, :]).then_inc(st[k], 16)

            looped(sp, NTL, 2, step)
            for k in range(2):
                sp.wait_ge(st[k], 16 * (NTL // 2 + 1))

        @block.tensor
        def _(pe):
            def turn_rows(j, k, i):
                pe.wait_ge(x_in[k], 16 * (i + 1))
                pe.wait_ge(xlo_rdy, j + 1)
                for c in range(DC):
                    ins = pe.transpose(tr[:, k, c * P:(c + 1) * P], xb[:, k, c * P:(c + 1) * P], const["ident"][:])
                ins.then_inc(tr_rdy, 1)

            def up(j, k):
                need = pe.value_load(plan["tile"][0:1, 0, bass.ds(j, 1)], min_val=1, max_val=E)
                off = pe.value_load(plan["tile"][0:1, 1, bass.ds(j, 1)], min_val=0, max_val=WPIECES * WPIECE)
                pe.wait_ge(w_rdy, need * WPIECES)
                pe.wait_ge(xlo_rdy, j + 3)
                pe.wait_ge(ac_rdy, j + 1)
                for c in range(DC):
                    xh, xl = x_hi[:, k, c * P:(c + 1) * P], x_lo[:, k, c * P:(c + 1) * P]
                    for n, (a, w) in enumerate(((xh, w_hi), (xh, w_lo), (xl, w_hi))):
                        for q in range(2):
                            ins = pe.matmul(gu[:, q, :], a, w[:, bass.ds(off + (c * WPIECE + q * H), H)],
                                            start=(c == 0 and n == 0), stop=(c == DC - 1 and n == 2))
                ins.then_inc(gu_rdy, 1)
                return off

            def turn_act(j, k):
                pe.wait_ge(ac_rdy, j + 2)
                pe.wait_ge(alo_rdy, j + 1)
                for c in range(DC):
                    ins = pe.transpose(at[:, k, c * P:(c + 1) * P], ac[:, k, c * P:(c + 1) * P], const["ident"][:])
                ins.then_inc(at_rdy, 1)

            def down(j, k):
                off = pe.value_load(plan["tile"][0:1, 1, bass.ds(j, 1)], min_val=0, max_val=WPIECES * WPIECE)
                pe.wait_ge(alo_rdy, j + 3)
                for c in range(DC):
                    ah, al = a_hi[:, k, c * P:(c + 1) * P], a_lo[:, k, c * P:(c + 1) * P]
                    for n, (a, w) in enumerate(((ah, w_hi), (ah, w_lo), (al, w_hi))):
                        ins = pe.matmul(dn[:, k, :], a, w[:, bass.ds(off + (DC * WPIECE + c * D), D)],
                                        start=(c == 0 and n == 0), stop=(c == DC - 1 and n == 2))
                ins.then_inc(dn_rdy, 1)

            pe.sem_inc(xlo_rdy, 2)
            pe.sem_inc(alo_rdy, 2)
            pe.sem_inc(ac_rdy, 1)
            pe.sem_inc(dn_rdy, 1)
            turn_rows(0, 0, 0)
            turn_rows(1, 1, 0)
            up(0, 0)
            with pe.Fori(0, NTL // 2 - 1) as i:
                for k in range(2):
                    j = i * 2 + k + 1
                    turn_act(j - 1, k)
                    up(j, 1 - k)
                    turn_rows(j + 1, k, i + 1)
                    down(j - 1, k)
            j = NTL - 1
            turn_act(j - 1, 0)
            up(j, 1)
            down(j - 1, 0)
            turn_act(j, 1)
            down(j, 1)

        @block.scalar
        def _(act):
            def x_part(j, k):
                act.wait_ge(tr_rdy, j + 1)
                act.activation(x_hi[:, k, :], tr[:, k, :], ACT.Copy).then_inc(xhi_rdy, 1)

            def gelu(j, k):
                act.wait_ge(gu_rdy, j + 1)
                act.activation(gl[:, k, :], gu[:, 0, :], ACT.Gelu_apprx_tanh).then_inc(gl_rdy, 1)

            def a_part(j, k):
                act.wait_ge(at_rdy, j + 1)
                act.activation(a_hi[:, k, :], at[:, k, :], ACT.Copy).then_inc(ahi_rdy, 1)

            def out(j, k, i):
                act.wait_ge(dn_rdy, j + 2)
                act.wait_ge(st[k], 16 * (i + 1))
                act.activation(ob[:, k, :], dn[:, k, :], ACT.Copy).then_inc(ob_rdy, 1)

            x_part(0, 0)
            x_part(1, 1)
            gelu(0, 0)
            with act.Fori(0, NTL // 2 - 1) as i:
                for k in range(2):
                    j = i * 2 + k + 1
                    a_part(j - 1, k)
                    gelu(j, 1 - k)
                    x_part(j + 1, k)
                    out(j - 1, k, i)
            j = NTL - 1
            a_part(j - 1, 0)
            gelu(j, 1)
            out(j - 1, 0, NTL // 2 - 1)
            a_part(j, 1)
            out(j, 1, NTL // 2 - 1)

        @block.vector
        def _(dve):
            def x_part(j, k):
                dve.wait_ge(xhi_rdy, j + 1)
                dve.tensor_tensor(x_lo[:, k, :], tr[:, k, :], x_hi[:, k, :].bitcast(F32), ALU.subtract).then_inc(xlo_rdy, 1)

            def gate(j, k):
                dve.wait_ge(gl_rdy, j + 1)
                dve.tensor_tensor(ac[:, k, :], gu[:, 1, :], gl[:, k, :], ALU.mult).then_inc(ac_rdy, 1)

            def a_part(j, k):
                dve.wait_ge(ahi_rdy, j + 1)
                dve.tensor_tensor(a_lo[:, k, :], at[:, k, :], a_hi[:, k, :].bitcast(F32), ALU.subtract).then_inc(alo_rdy, 1)

            x_part(0, 0)
            x_part(1, 1)
            gate(0, 0)
            with dve.Fori(0, NTL // 2 - 1) as i:
                for k in range(2):
                    j = i * 2 + k + 1
                    a_part(j - 1, k)
                    gate(j, 1 - k)
                    x_part(j + 1, k)
            j = NTL - 1
            a_part(j - 1, 0)
            gate(j, 1)
            a_part(j, 1)


class Front:

    def __init__(self, mem, const, x, nx, ny, joined=None, x_new=None, ng=2):
        self.const, self.x, self.nx, self.ny, self.joined, self.x_to, self.ng = const, x, nx, ny, joined, x_new, ng
        self.xb = mem.sb("xb", [P, nx, D])
        self.yb = mem.sb("yb", [P, ny, D])
        self.bn = mem.sb("bn", [P, 2, 6])
        self.mv = mem.sb("mv", [P, 2, 2])
        self.sd = mem.sb("sd", [P, 2])
        self.rstd = mem.sb("rstd", [P, 2])
        self.tr = mem.ps("tr", [P, 2, D])
        self.x_in = mem.sems("x_in", nx)
        (self.bn_rdy, self.mv_rdy, self.sd_rdy, self.rstd_rdy, self.y_rdy, self.tr_rdy, self.hi_rdy, self.lo_rdy) = (
            mem.sem(n) for n in ("bn_rdy", "mv_rdy", "sd_rdy", "rstd_rdy", "y_rdy", "tr_rdy", "hi_rdy", "lo_rdy"))
        if joined:
            self.gb = mem.sb("gb", [P, ng, TOPK, D])
            self.g_in = mem.sems("g_in", ng)
            self.x_st = mem.sems("x_st", nx)
            self.one_rdy, self.x_rdy = mem.sem("one_rdy"), mem.sem("x_rdy")

    def load(self, sp, t, k):
        sp.dma_start(self.xb[:, k, :], self.x[bass.ds(t * P, P), :]).then_inc(self.x_in[k], 16)

    def sp_tile(self, sp, t, k, i, ahead):
        if self.joined:
            sp.wait_ge(self.x_rdy, t + 1)
            sp.dma_start(self.x_to[bass.ds(t * P, P), :], self.xb[:, k, :]).then_inc(self.x_st[k], 16)
        if ahead:
            sp.wait_ge(self.y_rdy, t + 1)
            if self.joined:
                sp.wait_ge(self.x_st[k], 16 * (i + 1))
            self.load(sp, t + self.nx, k)

    def sp_end(self, sp):
        if self.joined:
            for k in range(self.nx):
                sp.wait_ge(self.x_st[k], 16 * (NT // self.nx))

    def gather(self, pool, begin=0, end=NT):
        ys, plan = self.joined
        for t in range(begin, end):
            if t >= self.ng:
                pool.wait_ge(self.x_rdy, t - self.ng + 1)
            for k in range(TOPK):
                pool.indirect_dma_start(
                    self.gb[:, t % self.ng, k, :], None, ys, bass.IndirectOffsetOnAxis(ap=plan["slot"][:, k, t:t + 1], axis=0),
                ).then_inc(self.g_in[t % self.ng], 16)

    def stats(self, dve, t, k, i, g):
        kg = k % self.ng
        xk = self.xb[:, k, :]
        dve.wait_ge(self.x_in[k], 16 * (i + 1))
        if self.joined:
            w = self.joined[1]["weight"]
            dve.wait_ge(self.g_in[kg], 16 * TOPK * (g + 1))
            dve.scalar_tensor_tensor(xk, self.gb[:, kg, 0, :], w[:, 0, bass.ds(t, 1)], xk, ALU.mult, ALU.add).then_inc(self.one_rdy, 1)
            dve.wait_ge(self.one_rdy, t + 1)
            dve.scalar_tensor_tensor(xk, self.gb[:, kg, 1, :], w[:, 1, bass.ds(t, 1)], xk, ALU.mult, ALU.add).then_inc(self.x_rdy, 1)
            dve.wait_ge(self.x_rdy, t + 1)
        dve.bn_stats(self.bn[:, k % 2, :], xk).then_inc(self.bn_rdy, 1)

    def moments(self, dve, k):
        dve.bn_aggr(self.mv[:, k % 2, :], self.bn[:, k % 2, :]).then_inc(self.mv_rdy, 1)

    def first(self, dve):
        self.stats(dve, 0, 0, 0, 0)
        dve.wait_ge(self.bn_rdy, 1)
        self.moments(dve, 0)

    def resume(self, dve, t, k):
        self.stats(dve, t, k, 0, t // self.ng)
        dve.wait_ge(self.bn_rdy, t + 1)
        self.moments(dve, k)

    def normalise(self, dve, t, k, i, ky, ahead):
        kn = (k + 1) % self.nx
        if ahead:
            n = i + (1 if kn == 0 else 0)
            g = i * (self.nx // self.ng) + (k + 1) // self.ng
            self.stats(dve, t + 1, kn, n, g)
            dve.wait_ge(self.bn_rdy, t + 2)
        dve.wait_ge(self.sd_rdy, t + 1)
        dve.reciprocal(self.rstd[:, k % 2:k % 2 + 1], self.sd[:, k % 2:k % 2 + 1]).then_inc(self.rstd_rdy, 1)
        if ahead:
            self.moments(dve, kn)
        dve.wait_ge(self.rstd_rdy, t + 1)
        dve.tensor_scalar(self.yb[:, ky, :], self.xb[:, k, :], self.mv[:, k % 2, 0:1], self.rstd[:, k % 2:k % 2 + 1],
                          ALU.subtract, ALU.mult).then_inc(self.y_rdy, 1)

    def deviation(self, act, t, k):
        act.wait_ge(self.mv_rdy, t + 1)
        act.activation(self.sd[:, k % 2:k % 2 + 1], self.mv[:, k % 2, 1:2], ACT.Sqrt, bias=self.const["eps"][:]).then_inc(self.sd_rdy, 1)

    def free(self, pe):
        pe.sem_inc(self.lo_rdy, 2)

    def turn(self, pe, t, k, ky):
        pe.wait_ge(self.y_rdy, t + 1)
        pe.wait_ge(self.lo_rdy, t + 1)
        for c in range(DC):
            ins = pe.transpose(self.tr[:, k % 2, c * P:(c + 1) * P], self.yb[:, ky, c * P:(c + 1) * P], self.const["ident"][:])
        ins.then_inc(self.tr_rdy, 1)

    def hi(self, act, t, k, to):
        act.wait_ge(self.tr_rdy, t + 1)
        act.activation(to, self.tr[:, k % 2, :].rearrange("p (c m) -> p c m", c=DC), ACT.Copy).then_inc(self.hi_rdy, 1)

    def lo(self, dve, t, k, to, hi):
        dve.wait_ge(self.hi_rdy, t + 1)
        dve.tensor_tensor(to, self.tr[:, k % 2, :].rearrange("p (c m) -> p c m", c=DC), hi.bitcast(F32), ALU.subtract).then_inc(self.lo_rdy, 1)


def products(parts_a, parts_b):
    (ah, al), (bh, bl) = parts_a, parts_b
    return ((ah, bh), (ah, bl), (al, bh))


GA = 4
QW = GA * P


def projection_stage(nc, stage, const, x, x_new, joined, q_w, k_w, v_w, q_parts, kst, v):
    with ExitStack() as ctx:
        mem = Memory(nc, ctx, stage)
        f = Front(mem, const, x, GA, GA, joined, x_new, GA)
        y_hi = mem.sb("y_hi", [P, 2, DC, QW], F32R)
        y_lo = mem.sb("y_lo", [P, 2, DC, QW], F32R)
        NQ = HEADS * HD
        raw = {"q": mem.sb("q_raw", [P, DC, NQ]), "k": mem.sb("k_raw", [P, DC, 3 * HD]), "v": mem.sb("v_raw", [P, DC, HD])}
        w_hi = {n: mem.sb(f"{n}_whi", list(r.shape), F32R) for n, r in raw.items()}
        w_lo = {n: mem.sb(f"{n}_wlo", list(r.shape), F32R) for n, r in raw.items()}
        q_hi = mem.sb("q_hi", [P, 2, QW], F32R)
        q_lo = mem.sb("q_lo", [P, 2, QW], F32R)
        q_ps = mem.ps("q", [P, 2, QW])
        k_ps = mem.ps("k", [P, QW])
        v_ps = mem.ps("v", [P, GA, HD])
        w_in, whi_rdy, wlo_rdy, ones_rdy = (mem.sem(n) for n in ("w_in", "whi_rdy", "wlo_rdy", "ones_rdy"))
        q_rdy, qhi_rdy, qlo_rdy, k_rdy, khi_rdy, klo_rdy, v_rdy, v_kept = (
            mem.sem(n) for n in ("q_rdy", "qhi_rdy", "qlo_rdy", "k_rdy", "khi_rdy", "klo_rdy", "v_rdy", "v_kept"))
        q_st = mem.sems("q_st", 2)
        block = ctx.enter_context(nc.Block())
        NG = NT // GA
        QC = NQ // P

        def parts(g2):
            return (y_hi[:, g2], y_lo[:, g2])

        def tile_of(buf, g2, j):
            return buf[:, g2, :, j * P:(j + 1) * P]

        def exists(g):
            return not isinstance(g, int) or g < NG

        def groups(eng, step):
            with eng.Fori(0, NG // 2 - 2) as i:
                for g2 in range(2):
                    step(i * 2 + g2, g2)
            for g in range(NG - 4, NG):
                step(g, g % 2)

        @block.sync
        def _(sp):
            for s in range(2):
                sp.sem_inc(q_st[s], 32)
            for t in range(4):
                f.load(sp, t, t)
            sp.dma_start(raw["q"][:], q_w).then_inc(w_in, 16)
            for n in range(3):
                sp.dma_start(raw["k"][:, :, n * HD:(n + 1) * HD], k_w).then_inc(w_in, 16)
            sp.dma_start(raw["v"][:], v_w).then_inc(w_in, 16)

            def query(g, m):
                s = m % 2
                sp.wait_ge(qlo_rdy, g * QC + m + 3)
                for n, part in enumerate((q_hi, q_lo)):
                    sp.dma_start(q_parts[n, m * P:(m + 1) * P, bass.ds(g * QW, QW)], part[:, s, :].bitcast(F32)).then_inc(q_st[s], 16)

            for g in range(2):
                for j in range(GA):
                    f.sp_tile(sp, g * GA + j, j, g, True)

            def step(g, g2):
                for m in range(QC):
                    query(g, m)
                    if exists(g + 2):
                        f.sp_tile(sp, (g + 2) * GA + m, m, g + 2, exists(g + 3))

            groups(sp, step)
            f.sp_end(sp)
            for s in range(2):
                sp.wait_ge(q_st[s], 32 * (NG * QC // 2 + 1))

        @block.gpsimd
        def _(pool):
            pool.memset(kst[96:98, :].bitcast(F32), 1.0).then_inc(ones_rdy, 1)
            pool.wait_ge(ones_rdy, 1)
            f.gather(pool, 0, GA)
            pool.wait_ge(w_in, 80)
            for n in ("k", "q", "v"):
                pool.tensor_scalar(w_hi[n][:], raw[n][:], 1.0, None, ALU.mult).then_inc(whi_rdy, 1)
            f.gather(pool, GA)

        @block.tensor
        def _(pe):
            f.free(pe)
            pe.sem_inc(qlo_rdy, 2)
            pe.sem_inc(klo_rdy, 1)
            pe.sem_inc(v_kept, 1)

            def main(g, g2):
                yp = parts(g2)
                pe.wait_ge(f.lo_rdy, (g + 1) * GA + 2)
                pe.wait_ge(klo_rdy, g + 1)
                for c in range(DC):
                    for n, (a, b) in enumerate(products((w_hi["k"][:, c, :], w_lo["k"][:, c, :]), (yp[0][:, c, :], yp[1][:, c, :]))):
                        ins = pe.matmul(k_ps[0:3 * HD, :], a, b, start=(c == 0 and n == 0), stop=(c == DC - 1 and n == 2))
                ins.then_inc(k_rdy, 1)
                for m in range(QC):
                    pe.wait_ge(qlo_rdy, g * QC + m + 1)
                    for c in range(DC):
                        wq = (w_hi["q"][:, c, m * P:(m + 1) * P], w_lo["q"][:, c, m * P:(m + 1) * P])
                        for n, (a, b) in enumerate(products(wq, (yp[0][:, c, :], yp[1][:, c, :]))):
                            ins = pe.matmul(q_ps[:, m % 2, :], a, b, start=(c == 0 and n == 0), stop=(c == DC - 1 and n == 2))
                    ins.then_inc(q_rdy, 1)
                    if exists(g + 1):
                        f.turn(pe, (g + 1) * GA + m, m, m)
                pe.wait_ge(v_kept, g + 1)
                for j in range(GA):
                    for c in range(DC):
                        yt = (tile_of(y_hi, g2, j)[:, c, :], tile_of(y_lo, g2, j)[:, c, :])
                        for n, (a, b) in enumerate(products(yt, (w_hi["v"][:, c, :], w_lo["v"][:, c, :]))):
                            ins = pe.matmul(v_ps[:, j, :], a, b, start=(c == 0 and n == 0), stop=(c == DC - 1 and n == 2))
                ins.then_inc(v_rdy, 1)

            for j in range(GA):
                f.turn(pe, j, j, j)
            pe.wait_ge(wlo_rdy, 3)
            groups(pe, main)

        @block.scalar
        def _(act):
            f.deviation(act, 0, 0)

            def front(g):
                for j in range(GA):
                    f.deviation(act, g * GA + j + 1, (j + 1) % GA)

            def main(g, m):
                if m == 0:
                    act.wait_ge(k_rdy, g + 1)
                    act.activation(kst[0:3 * HD, bass.ds(g * QW, QW)], k_ps[0:3 * HD, :], ACT.Copy).then_inc(khi_rdy, 1)
                s = m % 2
                act.wait_ge(q_rdy, g * QC + m + 1)
                act.wait_ge(q_st[s], 32 * (g * (QC // 2) + m // 2 + 1))
                act.activation(q_hi[:, s, :], q_ps[:, s, :], ACT.Copy).then_inc(qhi_rdy, 1)

            front(0)
            for j in range(GA):
                f.hi(act, j, j, tile_of(y_hi, 0, j))
            front(1)

            def step(g, g2):
                for m in range(QC):
                    main(g, m)
                    if exists(g + 1):
                        f.hi(act, (g + 1) * GA + m, m, tile_of(y_hi, 1 - g2, m))
                    t = (g + 2) * GA + m
                    if exists(g + 2) and not (isinstance(t, int) and t + 1 == NT):
                        f.deviation(act, t + 1, (m + 1) % GA)
                act.wait_ge(v_rdy, g + 1)
                act.activation(v[:, bass.ds(g * GA, GA), :], v_ps[:], ACT.Copy).then_inc(v_kept, 1)

            groups(act, step)

        @block.vector
        def _(dve):
            f.first(dve)

            def front(g, j):
                f.normalise(dve, g * GA + j, j, g, j, not (isinstance(g, int) and g * GA + j + 1 == NT))

            def low_part(g, g2, j):
                f.lo(dve, g * GA + j, j, tile_of(y_lo, g2, j), tile_of(y_hi, g2, j))

            def main(g, m):
                if m == 0:
                    dve.wait_ge(khi_rdy, g + 1)
                    kl = kst[HD:2 * HD, bass.ds(g * QW, QW)]
                    dve.tensor_tensor(kl, k_ps[HD:2 * HD, :], kl.bitcast(F32), ALU.subtract).then_inc(klo_rdy, 1)
                s = m % 2
                dve.wait_ge(qhi_rdy, g * QC + m + 1)
                dve.tensor_tensor(q_lo[:, s, :], q_ps[:, s, :], q_hi[:, s, :].bitcast(F32), ALU.subtract).then_inc(qlo_rdy, 1)

            for j in range(GA):
                front(0, j)
            for j in range(GA):
                low_part(0, 0, j)
            for n, name in enumerate(("k", "q", "v")):
                dve.wait_ge(whi_rdy, n + 1)
                dve.tensor_tensor(w_lo[name][:], raw[name][:], w_hi[name][:].bitcast(F32), ALU.subtract).then_inc(wlo_rdy, 1)
            for j in range(GA):
                front(1, j)

            def step(g, g2):
                for m in range(QC):
                    main(g, m)
                    if exists(g + 1):
                        low_part(g + 1, 1 - g2, m)
                    if exists(g + 2):
                        front(g + 2, m)

            groups(dve, step)


QT = S // P
HALF = HEADS // 2
UNITS = 2 * QT
OUT_AT = 8
TURN_AT = 11
KROWS = 3 * HD


def attention_stage(nc, stage, const, q_parts, kst, v, attn):
    with ExitStack() as ctx:
        mem = Memory(nc, ctx, stage)
        qst = mem.sb("qst", [P, 2, HEADS, P], F32R)
        pt = mem.sb("pt", [P, 4, HALF * P])
        pairs = mem.sb("pairs", [P, 4, 2, HALF * P])
        quads = mem.sb("quads", [P, 2, HALF * P])
        mx = mem.sb("mx", [P, HEADS, 2])
        neg = mem.sb("neg", [P, HALF])
        msplit = mem.sb("msplit", [P, 2, HALF], F32R)
        mT = mem.sb("mT", [2 * HALF, P])
        inv = mem.sb("inv", [P, 2 * P])
        sc = mem.ps("sc", [P, 2, 4 * P])
        am = mem.ps("am", [P, 2, 8 * P])
        pv = mem.ps("pv", [P, 2, 2, 2 * P])
        q_in = [mem.sems(f"q_in{k}_", 2) for k in range(2)]
        m_in = mem.sems("m_in", 2)
        am_rdy, mx_rdy, neg_rdy, mhi_rdy, ms_rdy, mT_rdy, mT_kept, s_rdy, p_rdy, pv_rdy, pair_rdy, quad_rdy, half_rdy, sum_rdy, inv_rdy, o_rdy = (
            mem.sem(n) for n in ("am_rdy", "mx_rdy", "neg_rdy", "mhi_rdy", "ms_rdy", "mT_rdy", "mT_kept", "s_rdy",
                                 "p_rdy", "pv_rdy", "pair_rdy", "quad_rdy", "half_rdy", "sum_rdy", "inv_rdy", "o_rdy"))
        block = ctx.enter_context(nc.Block())
        N = B * QT
        QUADS = UNITS // 4

        def rounds(eng, step):
            for k in range(2):
                step(k, k, 0, 0, 0)
            for b in range(B):
                with eng.Fori(0 if b else 1, QT // 2 - 1) as i:
                    for k in range(2):
                        step(i * 2 + (k + b * QT), k, i + b * (QT // 2), b, b)
                for k in range(2):
                    n = (b + 1) * QT - 2 + k
                    step(n, k, n // 2, b, b if k == 0 else (b + 1 if b + 1 < B else None))

        def lagging(do, n, q, size=UNITS):
            if q >= 0:
                do(n, q)
            elif not is_first(n):
                do(n - 1, q + size)

        def is_first(n):
            return isinstance(n, int) and n == 0

        @block.sync
        def _(sp):
            def load(n, k, h):
                for r, part in enumerate((0, 0, 1)):
                    src = q_parts[part, h * HALF * HD:(h + 1) * HALF * HD, bass.ds(n * P, P)].rearrange("(h d) q -> d h q", d=HD)
                    sp.dma_start(qst[r * HD:(r + 1) * HD, k, h * HALF:(h + 1) * HALF, :].bitcast(F32), src).then_inc(q_in[k][h], 16)

            def maxima(n, k, h):
                sp.wait_ge(mT_kept, n * 2 + (h + 1))
                for part in range(2):
                    row = KROWS + part
                    sp.dma_start(qst[row:row + 1, k, h * HALF:(h + 1) * HALF, :].bitcast(F32),
                                 mT[part * HALF:(part + 1) * HALF, :]).then_inc(m_in[h], 16)

            for n in range(2):
                for h in range(2):
                    load(n, n, h)
            maxima(0, 0, 0)

            def step(n, k, i, b, nb):
                more = not (isinstance(n, int) and n + 2 >= N)
                maxima(n, k, 1)
                sp.wait_ge(s_rdy, n * (2 * UNITS) + 2 * QT)
                if more:
                    load(n + 2, k, 0)
                if nb is not None:
                    maxima(n + 1, 1 - k, 0)
                sp.wait_ge(s_rdy, n * (2 * UNITS) + 2 * UNITS)
                if more:
                    load(n + 2, k, 1)

            rounds(sp, step)

        @block.tensor
        def _(pe):
            pe.sem_inc(mx_rdy, 2)
            pe.sem_inc(p_rdy, 2)
            pe.sem_inc(o_rdy, 2)

            def score(n, k, b, u, g):
                h, kt = divmod(u, QT)
                if kt == 0 and g == 0:
                    pe.wait_ge(m_in[h], n * 32 + 32)
                pe.wait_ge(p_rdy, n * (2 * UNITS) + (2 * u + g + 1))
                hh = h * HALF + g * 4
                pe.matmul(sc[:, g, :], kst[0:KROWS + 2, b * S + kt * P:b * S + (kt + 1) * P], qst[0:KROWS + 2, k, hh:hh + 4, :],
                          start=True, stop=True).then_inc(s_rdy, 1)

            def maxi(n, k, i, b, u, g):
                hd, kh = divmod(u, 2)
                if g == 0:
                    if u % QT == 0:
                        pe.wait_ge(q_in[k][u // QT], i * 48 + 48)
                    pe.wait_ge(mx_rdy, n * UNITS + (u + 1))
                o = b * S + kh * (S // 2) + g * 4 * P
                ins = pe.matmul(am[:, u % 2, g * 4 * P:(g + 1) * 4 * P], qst[0:KROWS, k, hd, :], kst[0:KROWS, o:o + 4 * P], start=True, stop=True)
                if g:
                    ins.then_inc(am_rdy, 1)

            def turn(n, h):
                pe.wait_ge(ms_rdy, n * 2 + (h + 1))
                pe.wait_ge(o_rdy, n * 2 + (h + 1))
                pe.transpose(pv[0:2 * HALF, h, 0, 0:P], msplit[:].rearrange("p s h -> p (s h)").bitcast(F32),
                             const["ident"][:]).then_inc(mT_rdy, 1)

            def values(n, b, u):
                h, kt = divmod(u, QT)
                if kt == 0:
                    pe.wait_ge(o_rdy, n * 2 + (h + 1))
                    pe.wait_ge(mT_kept, n * 2 + (h + 1))
                pe.wait_ge(p_rdy, n * (2 * UNITS) + (2 * u + 4))
                for j in range(4):
                    ins = pe.matmul(pv[HD * j:HD * (j + 1), h, 0, :], v[:, b * QT + kt, :], pt[:, u % 4, 2 * P * j:2 * P * (j + 1)],
                                    start=(kt == 0), stop=(kt == QT - 1), skip_group_check=True)
                ins.then_inc(pv_rdy, 1)

            def sums(n, q):
                h, part = divmod(q, QUADS // 2)
                pe.wait_ge(quad_rdy, n * (2 * QUADS) + (2 * q + 10))
                pe.wait_ge(half_rdy, n * QUADS + (q + 5))
                for j in range(4):
                    ins = pe.matmul(pv[HD * j:HD * (j + 1), h, 1, :], const["ones"][:, 0:HD], quads[:, q % 2, 2 * P * j:2 * P * (j + 1)],
                                    start=False, stop=(part == QUADS // 2 - 1), skip_group_check=True)
                ins.then_inc(sum_rdy, 1)

            for u in range(UNITS):
                for g in range(2):
                    maxi(0, 0, 0, 0, u, g)
                if u == QT + TURN_AT:
                    turn(0, 0)
            for g in range(2):
                score(0, 0, 0, 0, g)

            def step(n, k, i, b, nb):
                for u in range(UNITS):
                    if u == TURN_AT:
                        turn(n, 1)
                    if u == QT + TURN_AT and nb is not None:
                        turn(n + 1, 0)
                    for g in range(2):
                        if nb is not None:
                            maxi(n + 1, 1 - k, i + k, nb, u, g)
                        if u + 1 < UNITS:
                            score(n, k, b, u + 1, g)
                        elif nb is not None:
                            score(n + 1, 1 - k, nb, 0, g)
                    values(n, b, u)
                    if u % 4 == 2:
                        lagging(sums, n, u // 4 - 2, QUADS)

            rounds(pe, step)
            sums(N - 1, QUADS - 2)
            sums(N - 1, QUADS - 1)

        @block.scalar
        def _(act):
            act.sem_inc(pv_rdy, 4)
            act.sem_inc(pair_rdy, 2)

            def step(n, k, i, b, nb):
                for u in range(UNITS):
                    for g in range(2):
                        act.wait_ge(s_rdy, n * (2 * UNITS) + (2 * u + g + 1))
                        if g == 0:
                            act.wait_ge(pv_rdy, n * UNITS + (u + 1))
                            if u % 2 == 0:
                                act.wait_ge(pair_rdy, n * (UNITS // 2) + (u // 2 + 1))
                        act.activation(pt[:, u % 4, g * 4 * P:(g + 1) * 4 * P], sc[:, g, :], ACT.Exp, scale=HD ** -0.5).then_inc(p_rdy, 1)

            rounds(act, step)

        @block.gpsimd
        def _(pool):
            pool.sem_inc(half_rdy, 4)

            def step(n, k, i, b, nb):
                for p in range(UNITS // 2):
                    q = p // 2
                    if p % 2 == 0:
                        pool.wait_ge(quad_rdy, n * (2 * QUADS) + (2 * q + 2))
                        pool.wait_ge(half_rdy, n * QUADS + (q + 1))
                    pool.wait_ge(p_rdy, n * (2 * UNITS) + (4 * p + 6))
                    pool.tensor_tensor(pairs[:, q % 4, p % 2, :], pt[:, 2 * p % 4, :], pt[:, (2 * p + 1) % 4, :], ALU.add).then_inc(pair_rdy, 1)
                    if p % 2:
                        pool.wait_ge(pair_rdy, n * (UNITS // 2) + (p + 3))
                        pool.wait_ge(sum_rdy, n * QUADS + (q + 1))
                        pool.tensor_tensor(quads[:, q % 2, 4 * P:], pairs[:, q % 4, 0, 4 * P:], pairs[:, q % 4, 1, 4 * P:], ALU.add).then_inc(half_rdy, 1)

            rounds(pool, step)

        @block.vector
        def _(dve):
            dve.sem_inc(mT_rdy, 1)
            dve.sem_inc(quad_rdy, 8)
            dve.sem_inc(sum_rdy, 2)

            def maxi(n, u):
                dve.wait_ge(am_rdy, n * UNITS + (u + 1))
                dve.tensor_reduce(mx[:, u // 2, u % 2:u % 2 + 1], am[:, u % 2, :], AX.X, ALU.max).then_inc(mx_rdy, 1)

            def split(n, h):
                dve.wait_ge(mx_rdy, n * UNITS + (QT * (h + 1) + 2))
                dve.tensor_reduce(neg[:], mx[:, h * HALF:(h + 1) * HALF, :], AX.X, ALU.max, negate=True).then_inc(neg_rdy, 1)
                dve.wait_ge(neg_rdy, n * 2 + (h + 1))
                dve.wait_ge(mT_rdy, n * 2 + (h + 1))
                dve.tensor_copy(msplit[:, 0, :], neg[:]).then_inc(mhi_rdy, 1)
                dve.wait_ge(mhi_rdy, n * 2 + (h + 1))
                dve.tensor_tensor(msplit[:, 1, :], neg[:], msplit[:, 0, :].bitcast(F32), ALU.subtract).then_inc(ms_rdy, 1)

            def keep(n, h, first=False):
                dve.wait_ge(mT_rdy, n * 2 + (h + 2))
                if not first:
                    dve.wait_ge(m_in[1 - h], n * 32 + (32 if h else 0))
                dve.tensor_copy(mT[:], pv[0:2 * HALF, h, 0, 0:P]).then_inc(mT_kept, 1)

            def quad(n, piece):
                q, r = divmod(piece, 4)
                if r > 1:
                    return
                if r == 0:
                    dve.wait_ge(pair_rdy, n * (UNITS // 2) + (2 * q + 4))
                    dve.wait_ge(sum_rdy, n * QUADS + (q + 1))
                cut = slice(2 * P * r, 2 * P * (r + 1))
                dve.tensor_tensor(quads[:, q % 2, cut], pairs[:, q % 4, 0, cut], pairs[:, q % 4, 1, cut], ALU.add).then_inc(quad_rdy, 1)

            def shares(n, h):
                dve.wait_ge(sum_rdy, n * QUADS + (QUADS // 2 * (h + 1) + 2))
                dve.reciprocal(inv[:], pv[:, h, 1, :]).then_inc(inv_rdy, 1)

            def output(n, h):
                dve.wait_ge(inv_rdy, n * 2 + (h + 1))
                dve.tensor_tensor(attn[:, bass.ds(n, 1), h, :], pv[:, h, 0, :].unsqueeze(1), inv[:].unsqueeze(1), ALU.mult).then_inc(o_rdy, 1)

            for u in range(UNITS):
                maxi(0, u)
                if u == QT - 1:
                    split(0, 0)
                if u == QT + TURN_AT + 1:
                    keep(0, 0, True)
            split(0, 1)

            def step(n, k, i, b, nb):
                for u in range(UNITS):
                    if u == TURN_AT:
                        keep(n, 1)
                    if nb is not None:
                        maxi(n + 1, u)
                        if u == QT - 1:
                            split(n + 1, 0)
                        if u == QT + TURN_AT:
                            keep(n + 1, 0)
                    for m, h, at in ((n - 1, 1, OUT_AT), (n, 0, QT + OUT_AT)):
                        if u in (at, at + 1) and not (h and is_first(n)):
                            (output if u > at else shares)(m, h)
                    lagging(quad, n, u - 6)
                if nb is not None:
                    split(n + 1, 1)

            rounds(dve, step)
            for piece in range(UNITS - 6, UNITS):
                quad(N - 1, piece)
            shares(N - 1, 1)
            output(N - 1, 1)


def output_stage(nc, stage, const, attn, o_w, x, x_new):
    with ExitStack() as ctx:
        mem = Memory(nc, ctx, stage)
        NX = 4
        raw = mem.sb("raw", [P, DC, D])
        w_hi = mem.sb("w_hi", [P, DC, D], F32R)
        w_lo = mem.sb("w_lo", [P, DC, D], F32R)
        a_hi = mem.sb("a_hi", [P, 2, D], F32R)
        a_lo = mem.sb("a_lo", [P, 2, D], F32R)
        xb = mem.sb("xb", [P, NX, D])
        ob = mem.sb("ob", [P, 2, D])
        pr = mem.ps("pr", [P, 2, D])
        w_in, whi_rdy, wlo_rdy = (mem.sem(n) for n in ("w_in", "whi_rdy", "wlo_rdy"))
        x_in, st = mem.sems("x_in", NX), mem.sems("st", 2)
        hi_rdy, lo_rdy, pr_rdy, ob_rdy = (mem.sem(n) for n in ("hi_rdy", "lo_rdy", "pr_rdy", "ob_rdy"))
        block = ctx.enter_context(nc.Block())

        def rows(t):
            return attn[:, bass.ds(t, 1)].rearrange("p a h m -> p a (h m)")

        @block.sync
        def _(sp):
            def load(t, k):
                sp.dma_start(xb[:, k, :], x[bass.ds(t * P, P), :]).then_inc(x_in[k], 16)

            for k in range(2):
                sp.sem_inc(st[k], 16)
            for c in range(DC):
                sp.dma_start(raw[:, c, :], o_w[:, c, :]).then_inc(w_in, 16)
            for t in range(NX):
                load(t, t)

            def step(t, k, i, last):
                sp.wait_ge(ob_rdy, t + 3)
                sp.dma_start(x_new[bass.ds(t * P, P), :], ob[:, k % 2, :]).then_inc(st[k % 2], 16)
                if not last:
                    load(t + NX, k)

            looped(sp, NT, NX, step)
            for k in range(2):
                sp.wait_ge(st[k], 16 * (NT // 2 + 1))

        @block.scalar
        def _(act):
            act.wait_ge(w_in, 16 * DC)
            act.activation(w_hi[:, 0:2, :], raw[:, 0:2, :], ACT.Copy).then_inc(whi_rdy, 1)
            act.sem_inc(pr_rdy, 2)

            def step(t, k, i, last):
                act.wait_ge(pr_rdy, t + 1)
                act.activation(a_hi[:, k % 2, :].unsqueeze(1), rows(t), ACT.Copy).then_inc(hi_rdy, 1)

            looped(act, NT, NX, step)

        @block.gpsimd
        def _(pool):
            pool.wait_ge(w_in, 16 * DC)
            pool.tensor_scalar(w_hi[:, 2:4, :], raw[:, 2:4, :], 1.0, None, ALU.mult).then_inc(whi_rdy, 1)

        @block.vector
        def _(dve):
            dve.wait_ge(whi_rdy, 2)
            dve.tensor_tensor(w_lo[:], raw[:], w_hi[:].bitcast(F32), ALU.subtract).then_inc(wlo_rdy, 1)

            def low_part(t, k):
                dve.wait_ge(hi_rdy, t + 1)
                dve.tensor_tensor(a_lo[:, k % 2, :].unsqueeze(1), rows(t), a_hi[:, k % 2, :].bitcast(F32).unsqueeze(1), ALU.subtract).then_inc(lo_rdy, 1)

            low_part(0, 0)

            def step(t, k, i, last):
                if not (last and k == NX - 1):
                    low_part(t + 1, k + 1)
                dve.wait_ge(pr_rdy, t + 3)
                dve.wait_ge(x_in[k], i * 16 + 16)
                dve.wait_ge(st[k % 2], i * (16 * NX // 2) + (k // 2 * 16 + 16))
                dve.tensor_tensor(ob[:, k % 2, :], pr[:, k % 2, :], xb[:, k, :], ALU.add).then_inc(ob_rdy, 1)

            looped(dve, NT, NX, step)

        @block.tensor
        def _(pe):
            pe.sem_inc(ob_rdy, 2)
            pe.wait_ge(wlo_rdy, 1)

            def step(t, k, i, last):
                pe.wait_ge(lo_rdy, t + 1)
                pe.wait_ge(ob_rdy, t + 1)
                for c in range(DC):
                    cut = slice(c * P, (c + 1) * P)
                    for n, (a, b) in enumerate(products((a_hi[:, k % 2, cut], a_lo[:, k % 2, cut]), (w_hi[:, c, :], w_lo[:, c, :]))):
                        ins = pe.matmul(pr[:, k % 2, :], a, b, start=(c == 0 and n == 0), stop=(c == DC - 1 and n == 2))
                ins.then_inc(pr_rdy, 1)

            looped(pe, NT, NX, step)


GF = 2
FW = GF * P


def ffn_stage(nc, stage, const, x, x_new, joined, w_gate, w_up, w_down, gate_s, up_s, down_s, x_out):
    with ExitStack() as ctx:
        mem = Memory(nc, ctx, stage)
        f = Front(mem, const, x, 2 * GF, GF, joined, x_new)
        HALF_I = INTER // 2
        wg_hi, wg_lo = mem.sb("wg_hi", [P, DC, INTER], F32R), mem.sb("wg_lo", [P, DC, INTER], F32R)
        wu_hi, wu_lo = mem.sb("wu_hi", [P, DC, INTER], F32R), mem.sb("wu_lo", [P, DC, INTER], F32R)
        wd_hi, wd_lo = mem.sb("wd_hi", [P, IC, D], F32R), mem.sb("wd_lo", [P, IC, D], F32R)
        y_hi, y_lo = mem.sb("y_hi", [P, 2, DC, FW], F32R), mem.sb("y_lo", [P, 2, DC, FW], F32R)
        h_hi, h_lo = mem.sb("h_hi", [P, IC, FW], F32R), mem.sb("h_lo", [P, IC, FW], F32R)
        sg, hf = mem.sb("sg", [P, 2, FW]), mem.sb("hf", [P, 2, FW])
        rb, ob = mem.sb("rb", [P, GF, D]), mem.sb("ob", [P, GF, D])
        gs, us, ds_ = mem.sb("gs", [P, IC]), mem.sb("us", [P, IC]), mem.sb("ds", [P, D])
        diff, total, flag = mem.sb("diff", [P, IC + DC * 4]), mem.sb("total", [P, 1]), mem.sb("flag", [1, 1], I32)
        gu = mem.ps("gu", [P, 2, 2, FW])
        dn = mem.ps("dn", [P, GF, D])
        raw_in = mem.sems("raw_in", 3)
        s_in, whi_rdy, wlo_rdy, ds_rdy, cmp_rdy, diff_rdy, flag_rdy = (
            mem.sem(n) for n in ("s_in", "whi_rdy", "wlo_rdy", "ds_rdy", "cmp_rdy", "diff_rdy", "flag_rdy"))
        r_in, st = mem.sems("r_in", GF), mem.sems("st", GF)
        gu_rdy, sg_rdy, h_rdy, hhi_rdy, hlo_rdy, dn_rdy, o_half, o_rdy = (
            mem.sem(n) for n in ("gu_rdy", "sg_rdy", "h_rdy", "hhi_rdy", "hlo_rdy", "dn_rdy", "o_half", "o_rdy"))
        block = ctx.enter_context(nc.Block())
        NG = NT // GF
        res = x_new if joined else x

        raws = [t.rearrange("p a d -> p (a d)") for t in (rb[:], ob[:], f.xb[:, GF:2 * GF, :])]
        NR = len(raws)
        pieces = []
        for src, hi, lo in ((w_gate, wg_hi, wg_lo), (w_up, wu_hi, wu_lo)):
            for c in range(DC):
                for a in range(2):
                    cut = (slice(None), c, slice(a * HALF_I, (a + 1) * HALF_I))
                    pieces.append((src[cut], hi[cut], lo[cut], HALF_I))
        for i in range(0, IC, 2):
            n = min(2, IC - i)
            flat = [t[:, i:i + n, :].rearrange("p a d -> p (a d)") for t in (w_down, wd_hi, wd_lo)]
            pieces.append((*flat, n * D))

        def tile_of(buf, g2, j):
            return buf[:, g2, :, j * P:(j + 1) * P]

        def groups(eng, step):
            with eng.Fori(0, NG // 2 - 2) as i:
                for g2 in range(2):
                    step(i * 2 + g2, g2, i)
            for g in range(NG - 4, NG):
                step(g, g % 2, g // 2)

        def exists(g):
            return not isinstance(g, int) or g < NG

        @block.sync
        def _(sp):
            for j in range(GF):
                sp.sem_inc(st[j], 16)
            for t in range(GF):
                f.load(sp, t, t)
            for to, src in ((gs, gate_s), (us, up_s), (ds_, down_s.partition_broadcast(P))):
                sp.dma_start(to[:], src).then_inc(s_in, 16)
            for n, (src, hi, lo, w) in enumerate(pieces):
                if n >= NR:
                    sp.wait_ge(cmp_rdy, n - NR + 1)
                sp.dma_start(raws[n % NR][:, 0:w], src).then_inc(raw_in[n % NR], 16)
            sp.wait_ge(cmp_rdy, len(pieces))
            for t in range(GF, 2 * GF):
                f.load(sp, t, t)

            def tiles(g, g2, i):
                for j in range(GF):
                    f.sp_tile(sp, g * GF + j, g2 * GF + j, i, exists(g + 2))

            tiles(0, 0, 0)
            tiles(1, 1, 0)

            def step(g, g2, i):
                for j in range(GF):
                    sp.wait_ge(o_rdy, g * GF + (j + 1))
                    if joined:
                        sp.wait_ge(f.x_st[g2 * GF + j], i * 16 + 16)
                    sp.dma_start(rb[:, j, :], res[bass.ds((g * GF + j) * P, P), :]).then_inc(r_in[j], 16)
                if exists(g + 2):
                    tiles(g + 2, g2, i + 1)
                for j in range(GF):
                    sp.wait_ge(o_rdy, g * GF + (j + 3))
                    sp.dma_start(x_out[bass.ds((g * GF + j) * P, P), :], ob[:, j, :]).then_inc(st[j], 16)

            groups(sp, step)
            f.sp_end(sp)
            for j in range(GF):
                sp.wait_ge(st[j], 16 * (NG + 1))

        @block.gpsimd
        def _(pool):
            if joined:
                f.gather(pool, 0, GF)
            for n, (src, hi, lo, w) in enumerate(pieces):
                pool.wait_ge(raw_in[n % NR], 16 * (n // NR + 1))
                pool.tensor_scalar(hi, raws[n % NR][:, 0:w], 1.0, None, ALU.mult).then_inc(whi_rdy, 1)
            if joined:
                f.gather(pool, GF)

        @block.tensor
        def _(pe):
            f.free(pe)
            pe.sem_inc(h_rdy, 2)
            pe.sem_inc(o_rdy, 2)
            pe.sem_inc(hlo_rdy, 2)

            def turn(g, g2):
                for j in range(GF):
                    f.turn(pe, g * GF + j, j, j)

            turn(0, 0)
            pe.wait_ge(diff_rdy, 1)
            pe.matmul(dn[0:1, 0, 0:1], const["ones"][:, 0:1], total[:], start=True, stop=True).then_inc(diff_rdy, 1)
            pe.wait_ge(flag_rdy, 1)
            some_low = pe.value_load(flag[0:1, 0:1], min_val=0, max_val=1)
            pe.wait_ge(wlo_rdy, len(pieces))

            def passes(a, b, low):
                return [(x, y) for x, y, is_low in zip(*zip(*products(a, b)), (False, True, False)) if low or not is_low]

            def step(g, g2, i, low):
                pe.wait_ge(f.lo_rdy, g * GF + (GF + 2))
                for m in range(IC):
                    k = (g2 * IC + m) % 2
                    pe.wait_ge(h_rdy, g * IC + (m + 1))
                    for q, (hi, lo) in enumerate(((wg_hi, wg_lo), (wu_hi, wu_lo))):
                        for c in range(DC):
                            w = (hi[:, c, m * P:(m + 1) * P], lo[:, c, m * P:(m + 1) * P])
                            ab = passes((y_hi[:, g2, c, :], y_lo[:, g2, c, :]), w, low)
                            for n, (y, w) in enumerate(ab):
                                ins = pe.matmul(gu[:, k, q, :], w, y, start=(c == 0 and n == 0), stop=(c == DC - 1 and n == len(ab) - 1))
                    ins.then_inc(gu_rdy, 1)
                if exists(g + 1):
                    turn(g + 1, 1 - g2)
                for j in range(GF):
                    pe.wait_ge(o_rdy, g * GF + (j + 1))
                    for m in range(IC):
                        if j == 0:
                            pe.wait_ge(hlo_rdy, g * IC + (m + 3))
                        hp = (h_hi[:, m, j * P:(j + 1) * P], h_lo[:, m, j * P:(j + 1) * P])
                        ab = passes(hp, (wd_hi[:, m, :], wd_lo[:, m, :]), low)
                        for n, (a, b) in enumerate(ab):
                            ins = pe.matmul(dn[:, j, :], a, b, start=(m == 0 and n == 0), stop=(m == IC - 1 and n == len(ab) - 1))
                    ins.then_inc(dn_rdy, 1)

            with pe.If(some_low == 0):
                groups(pe, lambda g, g2, i: step(g, g2, i, False))
            with pe.Else():
                groups(pe, lambda g, g2, i: step(g, g2, i, True))

        @block.scalar
        def _(act):
            f.deviation(act, 0, 0)

            def front(g, g2):
                for j in range(GF):
                    if not (isinstance(g, int) and g * GF + j + 1 >= NT):
                        f.deviation(act, g * GF + (j + 1), (g2 * GF + j + 1) % 4)

            def group_hi(g, g2):
                for j in range(GF):
                    f.hi(act, g * GF + j, j, tile_of(y_hi, g2, j))

            front(0, 0)
            group_hi(0, 0)
            front(1, 1)
            act.wait_ge(s_in, 48)

            def part(g, g2, m):
                act.wait_ge(h_rdy, g * IC + (m + 3))
                act.activation(h_hi[:, m, :], hf[:, (g2 * IC + m) % 2, :], ACT.Copy).then_inc(hhi_rdy, 1)

            def step(g, g2, i):
                for m in range(IC):
                    k = (g2 * IC + m) % 2
                    act.wait_ge(gu_rdy, g * IC + (m + 1))
                    act.activation(sg[:, k, :], gu[:, k, 0, :], ACT.Silu, scale=gs[:, m:m + 1]).then_inc(sg_rdy, 1)
                    if m:
                        part(g, g2, m - 1)
                part(g, g2, IC - 1)
                if exists(g + 1):
                    group_hi(g + 1, 1 - g2)
                if exists(g + 2):
                    front(g + 2, g2)

            groups(act, step)

        @block.vector
        def _(dve):
            f.first(dve)

            def front(g, g2, i):
                for j in range(GF):
                    f.normalise(dve, g * GF + j, g2 * GF + j, i, j, not (isinstance(g, int) and g * GF + j + 1 >= NT))

            def group_lo(g, g2):
                for j in range(GF):
                    f.lo(dve, g * GF + j, j, tile_of(y_lo, g2, j), tile_of(y_hi, g2, j))

            for j in range(GF):
                f.normalise(dve, j, j, 0, j, j + 1 < GF)
            for n, (src, hi, lo, w) in enumerate(pieces):
                dve.wait_ge(whi_rdy, n + 1)
                dve.tensor_tensor(lo, raws[n % NR][:, 0:w], hi.bitcast(F32), ALU.subtract).then_inc(wlo_rdy, 1)
                dve.wait_ge(wlo_rdy, n + 1)
                dve.scalar_tensor_tensor(raws[n % NR][:, 0:w], raws[n % NR][:, 0:w], 1.0, hi.bitcast(F32), ALU.mult, ALU.not_equal,
                                         accum_out=diff[:, n:n + 1]).then_inc(cmp_rdy, 1)
            dve.wait_ge(cmp_rdy, len(pieces))
            dve.tensor_reduce(total[:], diff[:, 0:len(pieces)], AX.X, ALU.add).then_inc(diff_rdy, 1)
            dve.wait_ge(diff_rdy, 2)
            dve.tensor_scalar(flag[:], dn[0:1, 0, 0:1], 1.0, None, ALU.min).then_inc(flag_rdy, 1)
            f.resume(dve, GF, GF)
            dve.wait_ge(s_in, 48)
            dve.tensor_scalar(ds_[:], ds_[:], 0.5, None, ALU.mult).then_inc(ds_rdy, 1)
            dve.wait_ge(ds_rdy, 1)
            group_lo(0, 0)
            front(1, 1, 0)

            def part(g, g2, m):
                dve.wait_ge(hhi_rdy, g * IC + (m + 1))
                dve.tensor_tensor(h_lo[:, m, :], hf[:, (g2 * IC + m) % 2, :], h_hi[:, m, :].bitcast(F32), ALU.subtract).then_inc(hlo_rdy, 1)

            def step(g, g2, i):
                for m in range(IC):
                    k = (g2 * IC + m) % 2
                    dve.wait_ge(sg_rdy, g * IC + (m + 1))
                    dve.wait_ge(hlo_rdy, g * IC + (m + 1))
                    dve.scalar_tensor_tensor(hf[:, k, :], gu[:, k, 1, :], us[:, m:m + 1], sg[:, k, :], ALU.mult, ALU.mult).then_inc(h_rdy, 1)
                    if m:
                        part(g, g2, m - 1)
                part(g, g2, IC - 1)
                if exists(g + 1):
                    group_lo(g + 1, 1 - g2)
                if exists(g + 2):
                    front(g + 2, g2, i + 1)
                for j in range(GF):
                    dve.wait_ge(dn_rdy, g * GF + (j + 1))
                    dve.wait_ge(st[j], i * 32 + (g2 * 16 + 16))
                    dve.tensor_tensor(ob[:, j, :], dn[:, j, :], ds_[:], ALU.mult).then_inc(o_half, 1)
                    dve.wait_ge(o_half, g * GF + (j + 1))
                    dve.wait_ge(r_in[j], i * 32 + (g2 * 16 + 16))
                    dve.tensor_tensor(ob[:, j, :], ob[:, j, :], rb[:, j, :], ALU.add).then_inc(o_rdy, 1)

            groups(dve, step)


def keyvalue_stage(nc, stage, const, x, w_kv, w_qT, w_out, b_kv, b_q, b_out, gamma, beta, angles, x_out):
    with ExitStack() as ctx:
        mem = Memory(nc, ctx, stage)
        NB = QT
        xb, yb, y2 = mem.sb("xb", [P, 2, D]), mem.sb("yb", [P, 2, D]), mem.sb("y2", [P, 2, D])
        xy = mem.sb("xy", [P, NB, D])
        yT = mem.sb("yT", [P, NB, D])
        bn, mv = mem.sb("bn", [P, 6]), mem.sb("mv", [P, 2])
        sd, rstd = mem.sb("sd", [P, 1]), mem.sb("rstd", [P, 1])
        bn2, mv2 = mem.sb("bn2", [P, 6]), mem.sb("mv2", [P, 2])
        sd2, rstd2 = mem.sb("sd2", [P, 1]), mem.sb("rstd2", [P, 1])
        pause = mem.sb("pause", [P, 1])
        t_hi, t_lo = mem.sb("t_hi", [P, 2, D], F32R), mem.sb("t_lo", [P, 2, D], F32R)
        raw = mem.sb("raw", [P, DC, 2 * D])
        wk_hi, wk_lo = mem.sb("wk_hi", [P, DC, 2 * D], F32R), mem.sb("wk_lo", [P, DC, 2 * D], F32R)
        wq, wo = mem.sb("wq", [P, DC, D]), mem.sb("wo", [P, DC, D])
        aw, m_raw = raw[:, :, 0:D], raw[:, :, D:2 * D]
        m_hi, m_lo = mem.sb("m_hi", [P, DC, D], F32R), mem.sb("m_lo", [P, DC, D], F32R)
        gam, bet, bq = mem.sb("gam", [P, DC]), mem.sb("bet", [P, DC]), mem.sb("bq", [P, DC])
        bet_w, bq_w = mem.sb("bet_w", [P, DC, P]), mem.sb("bq_w", [P, DC, P])
        borow = mem.sb("borow", [1, D])
        bkv, bo = mem.sb("bkv", [P, 2, D]), mem.sb("bo", [P, D])
        cs = mem.sb("cs", [P, 2, 2, P])
        kv, kvc, kvs = mem.sb("kv", [P, 2, 2, D]), mem.sb("kvc", [P, 2, 2, ROT]), mem.sb("kvs", [P, 2, 2, ROT])
        brow = kv[0:1, 0].rearrange("p v d -> p (v d)")
        prod, junk = mem.sb("prod", [P, 2, D]), mem.ps("junk", [P, D])
        sq, nrm, rn, rr = mem.sb("sq", [P, 2, 2]), mem.sb("nrm", [P, 2, 2]), mem.sb("rn", [P, 2, 2]), mem.sb("rr", [P, 2, 1])
        asum, afac = mem.sb("asum", [P, DC]), mem.sb("afac", [P, DC])
        ob = mem.sb("ob", [P, 2, D])
        tr = mem.ps("tr", [P, 2, D])
        kv_ps = mem.ps("kv", [P, 2, 2, D])
        a_ps = mem.ps("a", [P, 2, DC])
        names = ("w_in", "wide_rdy", "bk_rdy", "bk_kept", "whi_rdy", "wlo_rdy", "bn_rdy", "mv_rdy", "sd_rdy", "rs_rdy", "y_rdy",
                 "xy_rdy", "bn2_rdy", "mv2_rdy", "sd2_rdy", "rs2_rdy", "y2_rdy", "tr_rdy", "yT_rdy", "thi_rdy", "tlo_rdy",
                 "kv_rdy", "kv_kept", "cos_rdy", "sin_rdy", "rot_rdy", "sq_rdy", "nrm_rdy", "rn_rdy", "rr_rdy", "prod_rdy",
                 "a_rdy", "a_kept", "zero_rdy", "af_rdy", "aw_rdy", "m_rdy", "mraw_rdy", "mhi_rdy", "mlo_rdy", "b_rdy",
                 "b_kept", "ohi_rdy", "olo_rdy", "o_rdy", "o_half", "ob_rdy")
        sm = {n: mem.sem(n) for n in names}
        x_in, cs_in, o_st = (mem.sems(n, 2) for n in ("x_in", "cs_in", "o_st"))
        block = ctx.enter_context(nc.Block())

        def spans(eng, b, step):
            def one(s, k, n, head, last):
                step(s + b * NB, s, k, n + b * (NB // 2), head, last)

            for k in range(2):
                one(k, k, 0, True, False)
            with eng.Fori(1, NB // 2 - 1) as n:
                for k in range(2):
                    one(n * 2 + k, k, n, False, False)
            for k in range(2):
                one(NB - 2 + k, k, NB // 2 - 1, False, True)

        def chunks(flat):
            return flat.rearrange("p (c m) -> p c m", c=DC)

        @block.sync
        def _(sp):
            def load(t, k):
                sp.dma_start(xb[:, k, :], x[bass.ds(t * P, P), :]).then_inc(x_in[k], 16)

            def load_angles(s, k):
                sp.dma_start(cs[:, k], angles[bass.ds(s * P, P), :, :]).then_inc(cs_in[k], 16)

            for k in range(2):
                sp.sem_inc(o_st[k], 16)
            load(0, 0)
            load(1, 1)
            for to, src in ((gam, gamma), (bet, beta), (bq, b_q), (borow, b_out), (raw, w_kv), (wq, w_qT), (wo, w_out)):
                sp.dma_start(to[:], src).then_inc(sm["w_in"], 16)
            sp.dma_start(brow, b_kv).then_inc(sm["w_in"], 16)
            for b in range(B):
                for k in range(2):
                    load_angles(k, k)

                def first(t, s, k, i, head, last):
                    if not (last and b == B - 1):
                        sp.wait_ge(sm["xy_rdy"], t + 1)
                        load(t + 2, k)
                    if not last:
                        sp.wait_ge(sm["rot_rdy"], t * 2 + 2)
                        load_angles(s + 2, k)

                spans(sp, b, first)
                sp.wait_ge(sm["rot_rdy"], (b + 1) * NB * 2)

                def second(t, s, k, i, head, last):
                    sp.wait_ge(sm["ob_rdy"], t + 1)
                    sp.dma_start(x_out[bass.ds(t * P, P), :], ob[:, k, :]).then_inc(o_st[k], 16)

                spans(sp, b, second)
            for k in range(2):
                sp.wait_ge(o_st[k], 16 * (NT // 2 + 1))

        @block.tensor
        def _(pe):
            pe.sem_inc(sm["yT_rdy"], 2)
            pe.sem_inc(sm["kv_kept"], 2)
            pe.sem_inc(sm["a_kept"], 2)
            pe.sem_inc(sm["o_half"], 2)
            pe.wait_ge(sm["wide_rdy"], 2 * DC)
            pe.wait_ge(sm["w_in"], 128)
            for h in range(2):
                for c in range(DC):
                    pe.matmul(kv_ps[:, 0, h, :], bet_w[:, c, :], raw[:, c, h * D:(h + 1) * D], start=(c == 0), stop=False)
                ins = pe.matmul(kv_ps[:, 0, h, :], const["ones"][0:1, :], brow[:, h * D:(h + 1) * D], start=False, stop=True)
            ins.then_inc(sm["bk_rdy"], 1)

            def turn(t, k):
                pe.wait_ge(sm["y2_rdy"], t + 1)
                pe.wait_ge(sm["yT_rdy"], t + 1)
                for c in range(DC):
                    ins = pe.transpose(tr[:, k, c * P:(c + 1) * P], y2[:, k, c * P:(c + 1) * P], const["ident"][:])
                ins.then_inc(sm["tr_rdy"], 1)

            def keysvalues(t, k):
                pe.wait_ge(sm["tlo_rdy"], t + 1)
                pe.wait_ge(sm["kv_kept"], t + 1)
                for h in range(2):
                    for c in range(DC):
                        w = (wk_hi[:, c, h * D:(h + 1) * D], wk_lo[:, c, h * D:(h + 1) * D])
                        for n, (a, bb) in enumerate(products((t_hi[:, k, c * P:(c + 1) * P], t_lo[:, k, c * P:(c + 1) * P]), w)):
                            ins = pe.matmul(kv_ps[:, k, h, :], a, bb, start=(c == 0 and n == 0), stop=(c == DC - 1 and n == 2))
                ins.then_inc(sm["kv_rdy"], 1)

            def sums(t, k):
                pe.wait_ge(sm["prod_rdy"], t * 2 + 5)
                pe.wait_ge(sm["rr_rdy"], t + 1)
                pe.wait_ge(sm["a_kept"], t + 1)
                for c in range(DC):
                    ins = pe.matmul(a_ps[:, k, c:c + 1], prod[:, k, c * P:(c + 1) * P], rr[:, k, :], start=True, stop=True)
                ins.then_inc(sm["a_rdy"], 1)

            for b in range(B):
                if b:
                    pe.wait_ge(sm["o_half"], b * NB + 2)
                turn(b * NB, 0)
                if not b:
                    pe.wait_ge(sm["bk_kept"], 1)
                    pe.wait_ge(sm["wlo_rdy"], DC)
                keysvalues(b * NB, 0)
                turn(b * NB + 1, 1)

                def first(t, s, k, i, head, last):
                    if not (last and k == 1):
                        keysvalues(t + 1, 1 - k)
                    if not last:
                        turn(t + 2, k)
                    sums(t, k)

                spans(pe, b, first)
                pe.wait_ge(sm["aw_rdy"], DC * (b + 1))
                pe.wait_ge(sm["kv_kept"], 2 + (b + 1) * NB)
                for m in range(DC):
                    for c in range(DC):
                        ins = pe.matmul(kv_ps[:, m // 2, m % 2, :], wq[:, c, m * P:(m + 1) * P], aw[:, c, :], start=(c == 0), stop=(c == DC - 1))
                    ins.then_inc(sm["m_rdy"], 1)
                for c in range(DC):
                    pe.matmul(tr[:, 0, :], bq_w[:, c, :], aw[:, c, :], start=(c == 0), stop=False)
                for m in range(DC):
                    pe.wait_ge(sm["mraw_rdy"], DC * b + m + 1)
                    pe.matmul(tr[:, 0, :], bet_w[:, m, :], m_raw[:, m, :], start=False, stop=False)
                pe.matmul(tr[:, 0, :], const["ones"][0:1, :], borow[:], start=False, stop=True).then_inc(sm["b_rdy"], 1)
                pe.wait_ge(sm["mlo_rdy"], DC * (b + 1))
                pe.wait_ge(sm["b_kept"], b + 1)

                def second(t, s, k, i, head, last):
                    pe.wait_ge(sm["olo_rdy"], t + 1)
                    pe.wait_ge(sm["o_half"], t + 1)
                    for c in range(DC):
                        for n, (a, bb) in enumerate(products((t_hi[:, k, c * P:(c + 1) * P], t_lo[:, k, c * P:(c + 1) * P]), (m_hi[:, c, :], m_lo[:, c, :]))):
                            ins = pe.matmul(tr[:, k, :], a, bb, start=(c == 0 and n == 0), stop=(c == DC - 1 and n == 2))
                    ins.then_inc(sm["o_rdy"], 1)

                spans(pe, b, second)

        @block.gpsimd
        def _(pool):
            pool.sem_inc(sm["prod_rdy"], 3)

            def total(t, s, k):
                pool.wait_ge(sm["y_rdy"], t + 1)
                pool.tensor_tensor(xy[:, bass.ds(s, 1), :], xb[:, k, :].unsqueeze(1), yb[:, k, :].unsqueeze(1), ALU.add).then_inc(sm["xy_rdy"], 1)

            for b in range(B):
                if b:
                    pool.wait_ge(sm["ob_rdy"], b * NB)
                total(b * NB, 0, 0)
                total(b * NB + 1, 1, 1)

                def first(t, s, k, i, head, last):
                    pool.wait_ge(sm["kv_kept"], t + 3)
                    pool.wait_ge(cs_in[k], i * 16 + 16)
                    pool.wait_ge(sm["prod_rdy"], t * 2 + 1)
                    pairs = kv[:, k, :, 0:ROT].rearrange("p v (d two) -> p v d two", two=2)
                    c_pairs = kvc[:, k].rearrange("p v (d two) -> p v d two", two=2)
                    s_pairs = kvs[:, k].rearrange("p v (d two) -> p v d two", two=2)
                    for e in range(2):
                        cosine, sine = (spread(cs[:, k, n, :], 2, 1) for n in range(2))
                        pool.tensor_tensor(c_pairs[:, :, :, e], pairs[:, :, :, e], cosine, ALU.mult).then_inc(sm["cos_rdy"], 1)
                        pool.tensor_tensor(s_pairs[:, :, :, e], pairs[:, :, :, 1 - e], sine, ALU.mult).then_inc(sm["sin_rdy"], 1)
                    pool.wait_ge(sm["cos_rdy"], t * 2 + 2)
                    pool.wait_ge(sm["sin_rdy"], t * 2 + 2)
                    pool.tensor_tensor(c_pairs[:, :, :, 0], c_pairs[:, :, :, 0], s_pairs[:, :, :, 0], ALU.subtract).then_inc(sm["rot_rdy"], 1)
                    pool.tensor_tensor(c_pairs[:, :, :, 1], c_pairs[:, :, :, 1], s_pairs[:, :, :, 1], ALU.add).then_inc(sm["rot_rdy"], 1)
                    if not last:
                        total(t + 2, s + 2, k)

                spans(pool, b, first)

        @block.scalar
        def _(act):
            def root(t):
                act.wait_ge(sm["mv_rdy"], t + 1)
                act.activation(sd[:], mv[:, 1:2], ACT.Sqrt, bias=const["eps"][:]).then_inc(sm["sd_rdy"], 1)
                act.wait_ge(sm["mv2_rdy"], t + 1)
                act.activation(sd2[:], mv2[:, 1:2], ACT.Sqrt, bias=const["eps"][:]).then_inc(sm["sd2_rdy"], 1)

            def parts(t, s, k):
                act.wait_ge(sm["tr_rdy"], t + 1)
                act.activation(t_hi[:, k, :], tr[:, k, :], ACT.Copy).then_inc(sm["thi_rdy"], 1)
                act.activation(yT[:, bass.ds(s, 1), :], tr[:, k, :].unsqueeze(1), ACT.Copy).then_inc(sm["yT_rdy"], 1)

            for b in range(B):
                root(b * NB)
                parts(b * NB, 0, 0)
                root(b * NB + 1)

                def first(t, s, k, i, head, last):
                    if not (last and k == 1):
                        parts(t + 1, s + 1, 1 - k)
                    if not last:
                        root(t + 2)
                    act.wait_ge(sm["kv_kept"], t + 3)
                    for h in range(2):
                        act.activation(junk[:], kv[:, k, h, :], ACT.Square, accum_out=sq[:, k, h:h + 1]).then_inc(sm["sq_rdy"], 1)
                        act.wait_ge(sm["sq_rdy"], t * 2 + (h + 1))
                    act.activation(nrm[:, k, :], sq[:, k, :], ACT.Sqrt).then_inc(sm["nrm_rdy"], 1)

                spans(act, b, first)
                for m in range(DC):
                    act.wait_ge(sm["m_rdy"], b * DC + m + 1)
                    act.activation(m_raw[:, m, :], kv_ps[:, m // 2, m % 2, :], ACT.Copy).then_inc(sm["mraw_rdy"], 1)
                act.wait_ge(sm["yT_rdy"], (b + 1) * NB + 2)

                def second(t, s, k, i, head, last):
                    if head:
                        act.wait_ge(sm["kv_rdy"], (b + 1) * NB)
                    else:
                        act.wait_ge(sm["o_rdy"], t - 1)
                    act.activation(t_hi[:, k, :].unsqueeze(1), yT[:, bass.ds(s, 1), :], ACT.Copy).then_inc(sm["ohi_rdy"], 1)

                spans(act, b, second)

        @block.vector
        def _(dve):
            dve.wait_ge(sm["w_in"], 128)
            for to, src in ((bet_w, bet), (bq_w, bq)):
                for c in range(DC):
                    dve.tensor_scalar(to[:, c, :], const["ones"][:], src[:, c:c + 1], None, ALU.mult).then_inc(sm["wide_rdy"], 1)
            for c in range(DC):
                dve.tensor_scalar(wk_hi[:, c, :], raw[:, c, :], gam[:, c:c + 1], None, ALU.mult).then_inc(sm["whi_rdy"], 1)
            for c in range(DC):
                dve.wait_ge(sm["whi_rdy"], c + 1)
                dve.scalar_tensor_tensor(wk_lo[:, c, :], raw[:, c, :], gam[:, c:c + 1], wk_hi[:, c, :].bitcast(F32), ALU.mult, ALU.subtract).then_inc(sm["wlo_rdy"], 1)
            dve.wait_ge(sm["bk_rdy"], 1)
            dve.tensor_copy(bkv[:], kv_ps[:, 0]).then_inc(sm["bk_kept"], 1)

            def aggregate(stats, out, done, signal, t):
                dve.wait_ge(sm[done], t + 1)
                dve.tensor_copy(pause[:], const["eps"][:])
                dve.bn_aggr(out[:], stats[:]).then_inc(sm[signal], 1)

            def norms(t, k, i):
                dve.wait_ge(x_in[k], i * 16 + 16)
                dve.bn_stats(bn[:], xb[:, k, :]).then_inc(sm["bn_rdy"], 1)
                aggregate(bn, mv, "bn_rdy", "mv_rdy", t)
                dve.wait_ge(sm["sd_rdy"], t + 1)
                dve.reciprocal(rstd[:], sd[:]).then_inc(sm["rs_rdy"], 1)
                dve.wait_ge(sm["rs_rdy"], t + 1)
                dve.tensor_scalar(yb[:, k, :], xb[:, k, :], mv[:, 0:1], rstd[:], ALU.subtract, ALU.mult).then_inc(sm["y_rdy"], 1)
                dve.wait_ge(sm["y_rdy"], t + 1)
                dve.bn_stats(bn2[:], yb[:, k, :]).then_inc(sm["bn2_rdy"], 1)
                aggregate(bn2, mv2, "bn2_rdy", "mv2_rdy", t)
                dve.wait_ge(sm["sd2_rdy"], t + 1)
                dve.reciprocal(rstd2[:], sd2[:]).then_inc(sm["rs2_rdy"], 1)
                dve.wait_ge(sm["rs2_rdy"], t + 1)
                dve.tensor_scalar(y2[:, k, :], yb[:, k, :], mv2[:, 0:1], rstd2[:], ALU.subtract, ALU.mult).then_inc(sm["y2_rdy"], 1)

            def low_part(t, s, k):
                dve.wait_ge(sm["thi_rdy"], t + 1)
                dve.wait_ge(sm["yT_rdy"], t + 3)
                dve.tensor_tensor(t_lo[:, k, :].unsqueeze(1), yT[:, bass.ds(s, 1), :], t_hi[:, k, :].bitcast(F32).unsqueeze(1),
                                  ALU.subtract).then_inc(sm["tlo_rdy"], 1)

            def take_sums(t, k):
                dve.wait_ge(sm["a_rdy"], t + 1)
                dve.wait_ge(sm["a_kept"], t + 2)
                dve.tensor_tensor(asum[:], asum[:], a_ps[:, k, :], ALU.add).then_inc(sm["a_kept"], 1)

            for b in range(B):
                dve.memset(asum[:], 0.0).then_inc(sm["zero_rdy"], 1)
                norms(b * NB, 0, b * (NB // 2))
                low_part(b * NB, 0, 0)
                norms(b * NB + 1, 1, b * (NB // 2))

                def first(t, s, k, i, head, last):
                    dve.wait_ge(sm["kv_rdy"], t + 1)
                    dve.tensor_tensor(kv[:, k], kv_ps[:, k], bkv[:], ALU.add).then_inc(sm["kv_kept"], 1)
                    if not (last and k == 1):
                        low_part(t + 1, s + 1, 1 - k)
                    if not last:
                        norms(t + 2, k, i + 1)
                    if head and k == 0:
                        dve.wait_ge(sm["zero_rdy"], b + 1)
                    else:
                        take_sums(t - 1, 1 - k)
                    dve.wait_ge(sm["nrm_rdy"], t + 1)
                    dve.reciprocal(rn[:, k, :], nrm[:, k, :]).then_inc(sm["rn_rdy"], 1)
                    dve.tensor_tensor(prod[:, k, ROT:D], kv[:, k, 0, ROT:D], kv[:, k, 1, ROT:D], ALU.mult).then_inc(sm["prod_rdy"], 1)
                    dve.wait_ge(sm["rn_rdy"], t + 1)
                    dve.tensor_tensor(rr[:, k, :], rn[:, k, 0:1], rn[:, k, 1:2], ALU.mult).then_inc(sm["rr_rdy"], 1)
                    dve.wait_ge(sm["rot_rdy"], t * 2 + 2)
                    dve.tensor_tensor(prod[:, k, 0:ROT], kvc[:, k, 0, :], kvc[:, k, 1, :], ALU.mult).then_inc(sm["prod_rdy"], 1)

                spans(dve, b, first)
                take_sums((b + 1) * NB - 1, 1)
                dve.wait_ge(sm["a_kept"], (b + 1) * NB + 2)
                dve.tensor_scalar(afac[:], asum[:], 0.5, 0.5, ALU.mult, ALU.add).then_inc(sm["af_rdy"], 1)
                dve.wait_ge(sm["af_rdy"], b + 1)
                for c in range(DC):
                    dve.tensor_scalar(aw[:, c, :], wo[:, c, :], afac[:, c:c + 1], None, ALU.mult).then_inc(sm["aw_rdy"], 1)
                for m in range(DC):
                    dve.wait_ge(sm["mraw_rdy"], b * DC + m + 1)
                    dve.tensor_scalar(m_hi[:, m, :], m_raw[:, m, :], gam[:, m:m + 1], None, ALU.mult).then_inc(sm["mhi_rdy"], 1)
                    dve.wait_ge(sm["mhi_rdy"], b * DC + m + 1)
                    dve.scalar_tensor_tensor(m_lo[:, m, :], m_raw[:, m, :], gam[:, m:m + 1], m_hi[:, m, :].bitcast(F32),
                                             ALU.mult, ALU.subtract).then_inc(sm["mlo_rdy"], 1)
                dve.wait_ge(sm["b_rdy"], b + 1)
                dve.tensor_copy(bo[:], tr[:, 0, :]).then_inc(sm["b_kept"], 1)
                dve.wait_ge(sm["b_kept"], b + 1)

                def part(t, s, k):
                    dve.wait_ge(sm["ohi_rdy"], t + 1)
                    dve.tensor_tensor(t_lo[:, k, :].unsqueeze(1), yT[:, bass.ds(s, 1), :], t_hi[:, k, :].bitcast(F32).unsqueeze(1),
                                      ALU.subtract).then_inc(sm["olo_rdy"], 1)

                part(b * NB, 0, 0)

                def second(t, s, k, i, head, last):
                    if not (last and k == 1):
                        part(t + 1, s + 1, 1 - k)
                    dve.wait_ge(sm["o_rdy"], t + 1)
                    dve.wait_ge(o_st[k], i * 16 + 16)
                    dve.tensor_tensor(ob[:, k, :], tr[:, k, :], bo[:], ALU.add).then_inc(sm["o_half"], 1)
                    dve.wait_ge(sm["o_half"], t + 3)
                    dve.tensor_tensor(ob[:, k, :].unsqueeze(1), ob[:, k, :].unsqueeze(1), xy[:, bass.ds(s, 1), :], ALU.add).then_inc(sm["ob_rdy"], 1)

                spans(dve, b, second)


def build(nc, a, out):
    def scratch(name, shape):
        return nc.dram_tensor(name, shape, F32, kind="Internal").ap()

    x = [a["x"]] + [scratch(f"x{n}", (T, D)) for n in range(1, 6)]
    xs, ys = scratch("xs", (SLOTS, D)), scratch("ys", (SLOTS, D))
    q_parts = scratch("q_parts", (2, HEADS * HD, T))
    with ExitStack() as ctx:
        mem = Memory(nc, ctx, "all")
        const = {"ident": mem.sb("ident", [P, P]), "before": mem.sb("before", [P, P]), "ones": mem.sb("ones", [P, P]), "eps": mem.sb("eps", [P, 1])}
        plan = {"slot": mem.sb("slot", [P, TOPK, NT], U32), "weight": mem.sb("weight", [P, TOPK, NT]),
                "tile": mem.sb("tile", [1, 2, SLOT_TILES], I32), "release": mem.sb("release", [1, E], I32)}
        setup_stage(nc, const)

        def experts(n, src, clear):
            with ExitStack() as weights:
                held = Memory(nc, weights, f"weights{n}")
                box = {"hi": held.sb("hi", [P, 2 * WPIECES * WPIECE], F32R), "lo": held.sb("lo", [P, 2 * WPIECES * WPIECE], F32R),
                       "raw": held.sb("raw", [P, 2, WPIECE])}
                routing_stage(nc, f"route{n}", const, src, a["router_scale"], a["router_w"], a["expert_scale"], a["experts"], box, xs, plan, clear)
                expert_stage(nc, f"expert{n}", const, xs, ys, a["experts"], box, plan)

        def ffn(n, src, joined_to, joined, to):
            ffn_stage(nc, f"ffn{n}", const, src, joined_to, joined, a["gate_w"], a["up_w"], a["down_w"], a["gate_s"], a["up_s"], a["down_s"], to)

        experts(0, x[0], True)
        with ExitStack() as attended:
            attn = Memory(nc, attended, "attended").sb("attn", [P, NT, 2, 2 * P])
            with ExitStack() as attention:
                held = Memory(nc, attention, "attention")
                kst, v = held.sb("kst", [P, T], F32R), held.sb("v", [P, NT, HD])
                projection_stage(nc, "project", const, x[0], x[1], (ys, plan), a["q_w"], a["k_w"], a["v_w"], q_parts, kst, v)
                attention_stage(nc, "attend", const, q_parts, kst, v, attn)
            output_stage(nc, "output", const, attn, a["o_w"], x[1], x[2])
        experts(1, x[2], False)
        ffn(0, x[2], x[3], (ys, plan), x[4])
        keyvalue_stage(nc, "keyvalue", const, x[4], a["kv_w"], a["qT_w"], a["out_w"], a["kv_b"], a["q_b"], a["out_b"],
                       a["gamma"], a["beta"], a["angles"], x[5])
        ffn(1, x[5], None, None, out)


def layout(np, i):
    def chunked(w):
        return w.reshape(w.shape[0] // P, P, -1).transpose(1, 0, 2)

    def column(v):
        return v.reshape(-1, P).T

    gate_up = i["L0_ffn_gating_einsum"].transpose(0, 3, 1, 2).reshape(E, DC, P, WPIECE).transpose(0, 2, 1, 3)
    down = i["L0_ffn_linear"].reshape(E, H // P // 2, 2, P, D).transpose(0, 3, 1, 2, 4).reshape(E, P, H // P // 2, WPIECE)
    w_in, b_in = i["L1_attn_W_in"], i["L1_attn_b_in"]
    inv_freq = np.float32(1.0) / np.float32(10000.0) ** (np.arange(0, ROT, 2, dtype=np.float32) / np.float32(ROT))
    turns = np.arange(S, dtype=np.float32)[:, None] * inv_freq[None, :]
    return {
        "x": i["L0_attn_x"].reshape(T, D),
        "router_scale": column(i["L0_ffn_router_scale"]), "router_w": chunked(i["L0_ffn_router_logits"]),
        "expert_scale": i["L0_ffn_per_expert_scale"], "experts": np.concatenate([gate_up, down], axis=2),
        "q_w": chunked(i["L0_attn_q_w"].T), "k_w": chunked(i["L0_attn_k_w"].T), "v_w": chunked(i["L0_attn_v_w"].T),
        "o_w": i["L0_attn_o_w"].T.reshape(2, HALF // 2, 2, HD, D).transpose(1, 3, 0, 2, 4).reshape(P, DC, D),
        "gate_w": chunked(i["L1_ffn_gate_w"].T), "up_w": chunked(i["L1_ffn_up_w"].T), "down_w": chunked(i["L1_ffn_down_w"].T),
        "gate_s": column(i["L1_ffn_gate_s"]), "up_s": column(i["L1_ffn_up_s"]), "down_s": i["L1_ffn_down_s"],
        "kv_w": chunked(w_in[:, D:]), "qT_w": chunked(w_in[:, :D].T), "out_w": chunked(i["L1_attn_W_out"]),
        "kv_b": b_in[None, D:], "q_b": column(b_in[:D]), "out_b": i["L1_attn_b_out"][None, :],
        "gamma": column(i["L1_attn_gamma"]), "beta": column(i["L1_attn_beta"]),
        "angles": np.stack([np.cos(turns), np.sin(turns)], axis=1),
    }


def kernel(**inputs):
    import numpy as np
    import concourse.bacc as bacc
    from concourse.bass_utils import run_bass_kernel_spmd

    nc = bacc.Bacc("TRN2", target_bir_lowering=False, num_devices=1)
    arrays = {n: np.ascontiguousarray(v) for n, v in layout(np, {n: np.asarray(v) for n, v in inputs.items()}).items()}
    drams = {n: nc.dram_tensor(f"{n}_dram", v.shape, mybir.dt.from_np(v.dtype), kind="ExternalInput").ap() for n, v in arrays.items()}
    out = nc.dram_tensor("out_dram", (T, D), F32, kind="ExternalOutput").ap()
    build(nc, drams, out)
    r = run_bass_kernel_spmd(nc, [{f"{n}_dram": v for n, v in arrays.items()}], core_ids=[0])
    return r.results[0]["out_dram"].reshape(B, S, D)
```

```python
from contextlib import ExitStack

import concourse.bass as bass
from concourse import mybir

F32 = mybir.dt.float32
F32R = mybir.dt.float32r
I32 = mybir.dt.int32
U32 = mybir.dt.uint32
ALU = mybir.AluOpType
ACT = mybir.ActivationFunctionType
AX = mybir.AxisListType

P = 128
B, S, D = 2, 2048, 512
T = B * S
NT = T // P
DC = D // P
E, H = 8, 512
TOPK = 2
SLOT_TILES = T * TOPK // P + E
SLOTS = SLOT_TILES * P
LAG = 2
LEVELS = T // P
HEADS, HD = 16, 32
INTER = 1408
IC = INTER // P
ROT = D // 2
LN_EPS = 1e-5
RMS_EPS = 1e-6
WPIECES = 6
WPIECE = 2 * H


class Memory:

    def __init__(self, nc, ctx, stage):
        self.nc, self.ctx, self.stage = nc, ctx, stage
        self.sems_held = []
        ctx.callback(self.zero_sems)

    def sb(self, name, shape, dt=F32):
        return self.ctx.enter_context(self.nc.sbuf_tensor(f"{self.stage}_{name}", shape, dt))

    def ps(self, name, shape, dt=F32):
        return self.ctx.enter_context(self.nc.psum_tensor(f"{self.stage}_{name}_ps", shape, dt))

    def sem(self, name):
        handle = self.nc.alloc_semaphore(f"{self.stage}_{name}_sem")
        self.sems_held.append(handle)
        return handle

    def zero_sems(self):
        if self.sems_held:
            self.nc.clear_and_free_semaphores(self.sems_held)
            self.nc.all_engine_barrier()

    def sems(self, name, n):
        return [self.sem(f"{name}{k}") for k in range(n)]


def looped(eng, n, unroll, step, head=False):
    rounds = n // unroll
    for k in range(unroll if head else 0):
        step(k, k, 0, False)
    with eng.Fori(1 if head else 0, rounds - 1) as i:
        for k in range(unroll):
            step(i * unroll + k, k, i, False)
    for k in range(unroll):
        step((rounds - 1) * unroll + k, k, rounds - 1, True)


def spread(ap, n, axis=2):
    wide = ap.unsqueeze(axis)
    shape = list(wide.shape)
    shape[axis] = n
    return wide.to_broadcast(shape)


def setup_stage(nc, const):
    with ExitStack() as ctx:
        mem = Memory(nc, ctx, "setup")
        filled, picked = mem.sem("filled"), mem.sem("picked")
        block = ctx.enter_context(nc.Block())

        @block.gpsimd
        def _(pool):
            pool.memset(const["ident"][:], 0.0).then_inc(filled, 1)
            pool.memset(const["before"][:], 1.0).then_inc(filled, 1)
            pool.memset(const["ones"][:], 1.0).then_inc(filled, 1)
            pool.memset(const["eps"][:], LN_EPS).then_inc(filled, 1)
            pool.wait_ge(filled, 4)
            pool.affine_select(out=const["ident"][:], in_=const["ident"][:], compare_op=ALU.not_equal, fill=1.0,
                               base=0, pattern=[[-1, P]], channel_multiplier=1).then_inc(picked, 1)
            pool.affine_select(out=const["before"][:], in_=const["before"][:], compare_op=ALU.is_gt, fill=0.0,
                               base=0, pattern=[[1, P]], channel_multiplier=-1).then_inc(picked, 1)
            pool.wait_ge(picked, 2)


def routing_stage(nc, stage, const, x, scale, logits_w, expert_scale, w_experts, box, yn, plan):
    with ExitStack() as ctx:
        mem = Memory(nc, ctx, stage)
        NX = 4
        xb = mem.sb("xb", [P, NX, D])
        yb = mem.sb("yb", [P, NX, D])
        yT = mem.sb("yT", [P, 2, D])
        bn = mem.sb("bn", [P, 2, 6])
        mv = mem.sb("mv", [P, 2, 2])
        var = mem.sb("var", [P, NT])
        sd = mem.sb("sd", [P, NT])
        rstd = mem.sb("rstd", [P, NT])
        wl = mem.sb("wl", [P, DC, E])
        rs = mem.sb("rs", [P, DC])
        wr = mem.sb("wr", [P, DC, E])
        esc = mem.sb("esc", [P, E])
        small = {n: mem.sb(n, [P, NT]) for n in
                 ("ms", "msd", "rr", "top1", "top2", "at1", "at2", "gap", "egap", "den", "w1", "w2", "s1", "s2")}
        lgT = mem.sb("lgT", [P, NT, P])
        W = NT * E // P
        wide = {n: lgT[:, k * W:(k + 1) * W, :].rearrange("p w (t e) -> p (w t) e", e=E) for k, n in
                enumerate(("eq", "cand", "oh1", "oh2", "left", "both", "tot", "sumA", "sumB", "pos", "tmp", "tmp2"))}
        wide["lg"] = mem.sb("lg", [P, NT, E])
        iota_e = mem.sb("iota_e", [P, E])
        iota_e8 = mem.sb("iota_e8", [P, E])
        levels = mem.sb("levels", [P, E, LEVELS])
        over = mem.sb("over", [P, E, LEVELS])
        tiles = mem.sb("tiles", [P, E])
        endA = mem.sb("endA", [P, E])
        endB = mem.sb("endB", [P, E])
        base = mem.sb("base", [P, E])
        number, number1 = mem.sb("number", [P, 1]), mem.sb("number1", [P, 1])
        flip, upto, follow, tmp_e = (mem.sb(n, [P, E]) for n in ("flip", "upto", "follow", "tmp_e"))
        tabf = mem.sb("tabf", [P, 5])
        iota_tile, iota_row = mem.sb("iota_tile", [P, SLOT_TILES]), mem.sb("iota_row", [P, P])
        token, slotf, tilef, rowf = (mem.sb(n, [P, TOPK * NT]) for n in ("token", "slotf", "tilef", "rowf"))
        in_tile, in_row = mem.sb("in_tile", [P, TOPK * NT, SLOT_TILES], F32R), mem.sb("in_row", [P, TOPK * NT, P], F32R)
        tr = mem.ps("tr", [P, 2, D])
        lg_ps = mem.ps("lg", [P, NT, E])
        pre_ps = mem.ps("pre", [P, NT, E])
        tot_ps = mem.ps("tot", [P, NT, E])
        rows_ps = mem.ps("rows", [P, SLOT_TILES])
        tab_ps = mem.ps("tab", [1, 5, SLOT_TILES])
        lgT_ps = [t[0:E].rearrange("e t f -> e (t f)")[:, 0:P] for t in (pre_ps, tot_ps)]

        x_in, y_st, raw_in = mem.sems("x_in", NX), mem.sems("y_st", NX), mem.sems("raw_in", 2)
        whi_rdy, wlo_rdy = mem.sem("whi_rdy"), mem.sem("wlo_rdy")
        FIRST = 2 * WPIECES
        HOT = 8
        w_in, wr_rdy, iotas = (mem.sem(n) for n in ("w_in", "wr_rdy", "iotas"))
        bn_rdy, mv_rdy, sd_rdy, rstd_rdy, y_rdy, tr_rdy, yT_rdy, lgT_rdy, lgT_kept, lg_rdy = (
            mem.sem(n) for n in ("bn_rdy", "mv_rdy", "sd_rdy", "rstd_rdy", "y_rdy", "tr_rdy", "yT_rdy", "lgT_rdy", "lgT_kept", "lg_rdy"))
        step_done, msd_rdy, gap_rdy, egap_rdy, both_rdy, counted, eq_rdy, hot_rdy, rows_rdy, tab_rdy = (
            mem.sem(n) for n in ("step_done", "msd_rdy", "gap_rdy", "egap_rdy", "both_rdy", "counted", "eq_rdy", "hot_rdy", "rows_rdy", "tab_rdy"))
        block = ctx.enter_context(nc.Block())

        @block.sync
        def _(sp):
            def load(t, k):
                sp.dma_start(xb[:, k, :], x[bass.ds(t * P, P), :]).then_inc(x_in[k], 16)

            for t in range(NX):
                load(t, t)
                sp.sem_inc(y_st[t], 16)
            sp.dma_start(wl[:], logits_w).then_inc(w_in, 16)
            sp.dma_start(rs[:], scale).then_inc(w_in, 16)
            sp.dma_start(esc[:], expert_scale.partition_broadcast(P)).then_inc(w_in, 16)

            def step(t, k, i, last):
                sp.wait_ge(y_rdy, t + 1)
                if not last:
                    load(t + NX, k)
                sp.dma_start(yn[bass.ds(t * P, P), :], yb[:, k, :]).then_inc(y_st[k], 16)

            looped(sp, NT, NX, step)
            for n in range(FIRST):
                if n >= 2:
                    sp.wait_ge(wlo_rdy, n - 1)
                sp.dma_start(box["raw"][:, n % 2, :], w_experts[n // WPIECES, :, n % WPIECES, :]).then_inc(raw_in[n % 2], 16)
            for k in range(NX):
                sp.wait_ge(y_st[k], 16 * (NT // NX + 1))

        @block.gpsimd
        def _(pool):
            pool.iota(iota_e[:], [[1, E]], base=0, channel_multiplier=0, allow_small_or_imprecise_dtypes=True).then_inc(iotas, 1)
            pool.iota(iota_e8[:], [[1, E]], base=E, channel_multiplier=0, allow_small_or_imprecise_dtypes=True).then_inc(iotas, 1)
            pool.iota(levels[:], [[0, E], [P, LEVELS]], base=0, channel_multiplier=0, allow_small_or_imprecise_dtypes=True).then_inc(iotas, 1)
            pool.iota(iota_tile[:], [[1, SLOT_TILES]], base=0, channel_multiplier=0, allow_small_or_imprecise_dtypes=True).then_inc(iotas, 1)
            pool.iota(iota_row[:], [[1, P]], base=0, channel_multiplier=0, allow_small_or_imprecise_dtypes=True).then_inc(iotas, 1)
            pool.iota(token[:], [[0, TOPK], [P, NT]], base=0, channel_multiplier=1, allow_small_or_imprecise_dtypes=True).then_inc(iotas, 1)
            pool.iota(number[:], [[0, 1]], base=0, channel_multiplier=1, allow_small_or_imprecise_dtypes=True).then_inc(iotas, 1)
            pool.iota(number1[:], [[0, 1]], base=1, channel_multiplier=1, allow_small_or_imprecise_dtypes=True).then_inc(iotas, 1)
            for e in range(E):
                pool.memset(flip[:, e:e + 1], 0.0 if e == E - 1 else (-1.0) ** e).then_inc(iotas, 1)
                pool.memset(upto[:, e:e + 1], 0.0 if e == E - 1 else 1.0).then_inc(iotas, 1)
                pool.memset(follow[:, e:e + 1], e + 2.0 if e + 2 < E else 0.0).then_inc(iotas, 1)
            for n in range(FIRST):
                pool.wait_ge(whi_rdy, n + 1)
                cut = slice(n * WPIECE, (n + 1) * WPIECE)
                pool.tensor_tensor(box["lo"][:, cut], box["raw"][:, n % 2, :], box["hi"][:, cut].bitcast(F32), ALU.subtract).then_inc(wlo_rdy, 1)

        @block.scalar
        def _(act):
            def deviation(t, k):
                act.wait_ge(mv_rdy, t + 1)
                act.activation(sd[:, bass.ds(t, 1)], mv[:, k % 2, 1:2], ACT.Sqrt, bias=const["eps"][:]).then_inc(sd_rdy, 1)

            def step(t, k, i, last):
                if not (last and k == NX - 1):
                    deviation(t + 1, k + 1)
                act.wait_ge(tr_rdy, t + 1)
                act.activation(yT[:, k % 2, :], tr[:, k % 2, :], ACT.Copy).then_inc(yT_rdy, 1)
                if not (isinstance(t, int) and t == 0):
                    keep(t - 1, (k - 1) % 2)

            def keep(t, k):
                act.wait_ge(lgT_rdy, t + 1)
                act.activation(lgT[0:E, bass.ds(t, 1), :], lgT_ps[k].unsqueeze(1), ACT.Copy).then_inc(lgT_kept, 1)

            deviation(0, 0)
            looped(act, NT, NX, step, head=True)
            keep(NT - 1, (NT - 1) % 2)
            act.wait_ge(step_done, 3)
            act.activation(small["msd"][:], small["ms"][:], ACT.Sqrt).then_inc(msd_rdy, 1)
            act.wait_ge(gap_rdy, 1)
            act.activation(small["egap"][:], small["gap"][:], ACT.Exp).then_inc(egap_rdy, 1)
            for n in range(FIRST):
                act.wait_ge(raw_in[n % 2], 16 * (n // 2 + 1))
                act.activation(box["hi"][:, n * WPIECE:(n + 1) * WPIECE], box["raw"][:, n % 2, :], ACT.Copy).then_inc(whi_rdy, 1)

        @block.tensor
        def _(pe):
            pe.sem_inc(yT_rdy, 4)
            pe.sem_inc(lgT_kept, 2)
            pe.wait_ge(wr_rdy, DC)

            def turn(t, k):
                pe.wait_ge(y_rdy, t + 1)
                pe.wait_ge(yT_rdy, t + 3)
                for c in range(DC):
                    ins = pe.transpose(tr[:, k % 2, c * P:(c + 1) * P], yb[:, k % NX, c * P:(c + 1) * P], const["ident"][:])
                ins.then_inc(tr_rdy, 1)

            turn(0, 0)
            turn(1, 1)

            def step(t, k, i, last):
                pe.wait_ge(yT_rdy, t + 5)
                pe.wait_ge(lgT_kept, t + 1)
                for c in range(DC):
                    ins = pe.matmul(lgT_ps[k % 2], wr[:, c, :], yT[:, k % 2, c * P:(c + 1) * P],
                                    start=(c == 0), stop=(c == DC - 1), skip_group_check=True)
                ins.then_inc(lgT_rdy, 1)
                if not (last and k >= NX - 2):
                    turn(t + 2, k + 2)

            looped(pe, NT, NX, step)
            pe.wait_ge(lgT_kept, NT + 2)
            for t in range(NT):
                ins = pe.transpose(lg_ps[:, t, :], lgT[0:E, t, :], const["ident"][0:E, 0:E])
            ins.then_inc(lg_rdy, 1)
            pe.wait_ge(both_rdy, 1)
            pe.matmul(pre_ps[:], const["before"][:], wide["both"][:], start=True, stop=True)
            pe.matmul(tot_ps[:], const["ones"][:], wide["both"][:], start=True, stop=True).then_inc(counted, 1)
            for q in range(TOPK * NT):
                if q % HOT == 0:
                    pe.wait_ge(hot_rdy, q // HOT + 1)
                ins = pe.matmul(rows_ps[:], in_row[:, q, :], in_tile[:, q, :], start=(q == 0), stop=(q == TOPK * NT - 1))
            ins.then_inc(rows_rdy, 1)
            pe.wait_ge(tab_rdy, 4)
            for c in range(5):
                ins = pe.matmul(tab_ps[:, c, :], tabf[0:SLOT_TILES, c:c + 1], const["ident"][0:SLOT_TILES, 0:SLOT_TILES], start=True, stop=True, skip_group_check=True)
            ins.then_inc(tab_rdy, 1)

        @block.vector
        def _(dve):
            steps = [0]

            def then(ins):
                steps[0] += 1
                ins.then_inc(step_done, 1)
                dve.wait_ge(step_done, steps[0])

            dve.wait_ge(w_in, 48)
            for c in range(DC):
                dve.tensor_scalar(wr[:, c, :], wl[:, c, :], rs[:, c:c + 1], float(D) ** -0.5, ALU.mult, ALU.mult).then_inc(wr_rdy, 1)

            def stats(t, k, i):
                dve.wait_ge(x_in[k], 16 * (i + 1))
                dve.bn_stats(bn[:, k % 2, :], xb[:, k, :]).then_inc(bn_rdy, 1)

            def moments(t, k):
                dve.bn_aggr(mv[:, k % 2, :], bn[:, k % 2, :]).then_inc(mv_rdy, 1)

            def keep_variance(t, k):
                dve.wait_ge(mv_rdy, t + 1)
                dve.tensor_copy(var[:, bass.ds(t, 1)], mv[:, k % 2, 1:2])

            stats(0, 0, 0)
            dve.wait_ge(bn_rdy, 1)
            moments(0, 0)
            keep_variance(0, 0)

            def step(t, k, i, last):
                ahead = not (last and k == NX - 1)
                kn = (k + 1) % NX
                if ahead:
                    stats(t + 1, kn, i + (1 if kn == 0 else 0))
                    dve.wait_ge(bn_rdy, t + 2)
                dve.wait_ge(sd_rdy, t + 1)
                dve.reciprocal(rstd[:, bass.ds(t, 1)], sd[:, bass.ds(t, 1)]).then_inc(rstd_rdy, 1)
                if ahead:
                    moments(t + 1, kn)
                dve.wait_ge(rstd_rdy, t + 1)
                dve.wait_ge(y_st[k], 16 * (i + 1))
                dve.wait_ge(yT_rdy, t + 1)
                dve.tensor_scalar(yb[:, k, :], xb[:, k, :], mv[:, k % 2, 0:1], rstd[:, bass.ds(t, 1)],
                                  ALU.subtract, ALU.mult).then_inc(y_rdy, 1)
                if ahead:
                    keep_variance(t + 1, kn)

            looped(dve, NT, NX, step)
            then(dve.tensor_tensor(small["ms"][:], rstd[:], rstd[:], ALU.mult))
            then(dve.tensor_tensor(small["ms"][:], small["ms"][:], var[:], ALU.mult))
            then(dve.tensor_scalar(small["ms"][:], small["ms"][:], RMS_EPS, None, ALU.add))
            dve.wait_ge(msd_rdy, 1)
            then(dve.reciprocal(small["rr"][:], small["msd"][:]))
            dve.wait_ge(lg_rdy, 1)
            dve.wait_ge(iotas, 8 + 3 * E)
            lg = wide["lg"]
            then(dve.tensor_tensor(lg[:], lg_ps[:], spread(small["rr"][:], E), ALU.mult))

            def best(values, top, at, onehot):
                then(dve.tensor_reduce(top[:], values[:], AX.X, ALU.max))
                then(dve.tensor_tensor(wide["eq"][:], values[:], spread(top[:], E), ALU.is_equal))
                then(dve.tensor_scalar(wide["cand"][:], wide["eq"][:], -float(E), None, ALU.mult))
                then(dve.tensor_tensor(wide["cand"][:], wide["cand"][:], spread(iota_e8[:], NT, 1), ALU.add))
                then(dve.tensor_reduce(at[:], wide["cand"][:], AX.X, ALU.min))
                then(dve.tensor_tensor(onehot[:], spread(at[:], E), spread(iota_e[:], NT, 1), ALU.is_equal))

            best(lg, small["top1"], small["at1"], wide["oh1"])
            then(dve.scalar_tensor_tensor(wide["left"][:], wide["oh1"][:], -3e38, lg[:], ALU.mult, ALU.add))
            best(wide["left"], small["top2"], small["at2"], wide["oh2"])
            dve.tensor_tensor(small["gap"][:], small["top2"][:], small["top1"][:], ALU.subtract).then_inc(gap_rdy, 1)
            dve.tensor_tensor(wide["both"][:], wide["oh1"][:], wide["oh2"][:], ALU.add).then_inc(both_rdy, 1)
            dve.wait_ge(egap_rdy, 1)
            then(dve.tensor_scalar(small["den"][:], small["egap"][:], 1.0, None, ALU.add))
            then(dve.reciprocal(small["w1"][:], small["den"][:]))
            then(dve.tensor_tensor(small["w2"][:], small["w1"][:], small["egap"][:], ALU.mult))
            for k, (oh, s, w) in enumerate((("oh1", "s1", "w1"), ("oh2", "s2", "w2"))):
                then(dve.tensor_tensor(wide["tmp"][:], wide[oh][:], spread(esc[:], NT, 1), ALU.mult))
                then(dve.tensor_reduce(small[s][:], wide["tmp"][:], AX.X, ALU.add))
                then(dve.scalar_tensor_tensor(plan["weight"][:, k, :], small[s][:], 0.5, small[w][:], ALU.mult, ALU.mult))
            dve.wait_ge(counted, 1)
            then(dve.tensor_copy(wide["tot"][:], tot_ps[:]))
            now, nxt = wide["tot"], wide["sumA"]
            for sh in (1, 2, 4, 8, 16):
                then(dve.tensor_copy(nxt[:, 0:sh, :], now[:, 0:sh, :]))
                then(dve.tensor_tensor(nxt[:, sh:NT, :], now[:, sh:NT, :], now[:, 0:NT - sh, :], ALU.add))
                now, nxt = nxt, (wide["sumB"] if nxt is wide["sumA"] else wide["sumA"])
            then(dve.tensor_tensor(over[:], spread(now[:, NT - 1, :], LEVELS), levels[:], ALU.is_gt))
            then(dve.tensor_reduce(tiles[:], over[:], AX.X, ALU.add))
            then(dve.tensor_scalar(tiles[:], tiles[:], 1.0, None, ALU.max))
            end, nend = tiles, endA
            for sh in (1, 2, 4):
                then(dve.tensor_copy(nend[:, 0:sh], end[:, 0:sh]))
                then(dve.tensor_tensor(nend[:, sh:E], end[:, sh:E], end[:, 0:E - sh], ALU.add))
                end, nend = nend, (endB if nend is endA else endA)
            then(dve.tensor_tensor(base[:], end[:], tiles[:], ALU.subtract))
            then(dve.tensor_scalar(base[:], base[:], float(P), None, ALU.mult))
            then(dve.tensor_tensor(wide["pos"][:], now[:], wide["tot"][:], ALU.subtract))
            then(dve.tensor_tensor(wide["pos"][:], wide["pos"][:], pre_ps[:], ALU.add))
            then(dve.tensor_tensor(wide["pos"][:], wide["pos"][:], spread(base[:], NT, 1), ALU.add))
            for k, oh in enumerate(("oh1", "oh2")):
                then(dve.tensor_tensor(wide["tmp2"][:], wide[oh][:], wide["pos"][:], ALU.mult))
                then(dve.tensor_reduce(slotf[:, k * NT:(k + 1) * NT], wide["tmp2"][:], AX.X, ALU.add))
            dve.tensor_copy(plan["slot"][:].rearrange("p k t -> p (k t)"), slotf[:])
            then(dve.tensor_scalar(tilef[:], slotf[:], 1.0 / P, -(P - 1) / (2.0 * P), ALU.mult, ALU.add))
            then(dve.tensor_scalar(tilef[:], tilef[:], 1.5 * 2 ** 23, None, ALU.add))
            then(dve.tensor_scalar(tilef[:], tilef[:], -1.5 * 2 ** 23, None, ALU.add))
            then(dve.scalar_tensor_tensor(rowf[:], tilef[:], -float(P), slotf[:], ALU.mult, ALU.add))
            for n in range(TOPK * NT // HOT):
                q = slice(n * HOT, (n + 1) * HOT)
                dve.tensor_tensor(in_tile[:, q, :], spread(tilef[:, q], SLOT_TILES), spread(iota_tile[:], HOT, 1), ALU.is_equal).then_inc(eq_rdy, 1)
                dve.tensor_tensor(in_row[:, q, :], spread(rowf[:, q], P), spread(iota_row[:], HOT, 1), ALU.is_equal).then_inc(eq_rdy, 1)
                dve.wait_ge(eq_rdy, 2 * (n + 1))
                dve.tensor_tensor(in_tile[:, q, :], in_tile[:, q, :].bitcast(F32), spread(token[:, q], SLOT_TILES), ALU.mult).then_inc(hot_rdy, 1)
            dve.tensor_copy(plan["used"][:], end[0:1, E - 1:E])
            own, past = end[0:SLOT_TILES, :], tmp_e[0:SLOT_TILES, :]
            for column, compare, weigh in ((0, ALU.is_le, upto), (1, ALU.is_le, flip), (2, ALU.is_equal, follow)):
                shift = number if compare == ALU.is_le else number1
                then(dve.tensor_scalar(past, own, shift[0:SLOT_TILES, :], None, compare))
                then(dve.tensor_tensor(past, past, weigh[0:SLOT_TILES, :], ALU.mult))
                then(dve.tensor_reduce(tabf[0:SLOT_TILES, column:column + 1], past, AX.X, ALU.add))
            tab = [tabf[0:SLOT_TILES, c:c + 1] for c in range(5)]
            dve.tensor_scalar(tab[0], tab[0], 1.0, None, ALU.add).then_inc(tab_rdy, 1)
            dve.tensor_scalar(tab[1], tab[1], float(WPIECES * WPIECE), None, ALU.mult).then_inc(tab_rdy, 1)
            dve.tensor_scalar(tab[3], tab[2], 1.0, float(E - 1), ALU.add, ALU.min).then_inc(tab_rdy, 1)
            dve.tensor_scalar(tab[4], tab[2], -2.0, 0.0, ALU.add, ALU.max).then_inc(tab_rdy, 1)
            dve.wait_ge(tab_rdy, 5)
            dve.tensor_copy(plan["tile"][:], tab_ps[:, 0:2, :])
            dve.memset(plan["next"][:, :, 0:LAG], 0)
            for row, column in enumerate((2, 3, 1, 4)):
                dve.tensor_copy(plan["next"][:, row, LAG:], tab_ps[:, column, :])
            dve.wait_ge(rows_rdy, 1)
            dve.tensor_copy(plan["rows"][:], rows_ps[:])


def expert_stage(nc, stage, const, yn, ys, w_experts, box, plan):
    with ExitStack() as ctx:
        mem = Memory(nc, ctx, stage)
        w_hi, w_lo, raw = box["hi"], box["lo"], box["raw"]
        AHEAD = 4
        xb = mem.sb("xb", [P, AHEAD * D])
        rows = mem.sb("rows", [P, AHEAD], U32)
        x_hi = mem.sb("x_hi", [P, 2, D], F32R)
        x_lo = mem.sb("x_lo", [P, 2, D], F32R)
        gl = mem.sb("gl", [P, 2, H])
        ac = mem.sb("ac", [P, 2, H])
        a_hi = mem.sb("a_hi", [P, 2, H], F32R)
        a_lo = mem.sb("a_lo", [P, 2, H], F32R)
        ob = mem.sb("ob", [P, 2, D])
        tr = mem.ps("tr", [P, 2, D])
        gu = mem.ps("gu", [P, 2, H])
        at = mem.ps("at", [P, 2, H])
        dn = mem.ps("dn", [P, 2, D])

        raw_in, w_rdy, hi_w = mem.sems("raw_in", 2), mem.sem("w_rdy"), mem.sem("hi_w")
        rows_rdy, x_in, st = mem.sem("rows_rdy"), mem.sems("x_in", AHEAD), mem.sems("st", 2)
        tr_rdy, xhi_rdy, xlo_rdy, gu_rdy, gl_rdy, ac_rdy, at_rdy, ahi_rdy, alo_rdy, dn_rdy, ob_rdy = (
            mem.sem(n) for n in ("tr_rdy", "xhi_rdy", "xlo_rdy", "gu_rdy", "gl_rdy", "ac_rdy", "at_rdy", "ahi_rdy",
                                 "alo_rdy", "dn_rdy", "ob_rdy"))
        block = ctx.enter_context(nc.Block())
        NTL = SLOT_TILES
        FULL = T * TOPK // P

        @block.gpsimd
        def _(pool):
            def follower(j):
                return pool.value_load(plan["next"][0:1, 0, bass.ds(j, 1)], min_val=0, max_val=E - 1)

            def gather(j, m, before=None):
                pool.tensor_copy(rows[:, m:m + 1], plan["rows"][:, bass.ds(j, 1)]).then_inc(rows_rdy, 1)
                pool.wait_ge(rows_rdy, j + 1)
                loaded = before() if before else None
                pool.indirect_dma_start(
                    xb[:, m * D:(m + 1) * D], None, yn, bass.IndirectOffsetOnAxis(ap=rows[:, m:m + 1], axis=0),
                ).then_inc(x_in[m], 16)
                return loaded

            def load(e, n):
                pool.dma_start(raw[:, n % 2, :], w_experts[bass.ds(e, 1), :, n, :].rearrange("a p m -> (a p) m")).then_inc(raw_in[n % 2], 16)

            def refill(j, e):
                with pool.If(e > 0):
                    off = pool.value_load(plan["next"][0:1, 2, bass.ds(j, 1)], min_val=0, max_val=WPIECES * WPIECE)
                    after = pool.value_load(plan["next"][0:1, 1, bass.ds(j, 1)], min_val=0, max_val=E - 1)
                    read = pool.value_load(plan["next"][0:1, 3, bass.ds(j, 1)], min_val=0, max_val=E - 3)
                    pool.wait_ge(dn_rdy, j + 3 - LAG)
                    for n in range(WPIECES):
                        pool.wait_ge(raw_in[n % 2], read * (16 * WPIECES // 2) + 16 * (n // 2 + 1))
                        part = bass.ds(off + n * WPIECE, WPIECE)
                        pool.tensor_tensor(w_hi[:, part], raw[:, n % 2, :], const["ones"][:, 0:1].to_broadcast([P, WPIECE]), ALU.mult).then_inc(hi_w, 1)
                        pool.wait_ge(hi_w, read * WPIECES + (n + 1))
                        pool.tensor_tensor(w_lo[:, part], raw[:, n % 2, :], w_hi[:, part].bitcast(F32), ALU.subtract).then_inc(w_rdy, 1)
                        pool.wait_ge(w_rdy, e * WPIECES + (n + 1))
                        if n + 2 < WPIECES:
                            load(e, n + 2)
                        else:
                            load(after, n + 2 - WPIECES)

            pool.sem_inc(w_rdy, 2 * WPIECES)
            for j in range(AHEAD):
                gather(j, j)
            for n in range(2):
                load(2, n)
            with pool.Fori(0, NTL // AHEAD - 1) as i:
                for m in range(AHEAD):
                    pool.wait_ge(tr_rdy, i * AHEAD + (m + 1))
                    j = i * AHEAD + m
                    refill(j, gather(j + AHEAD, m, lambda: follower(j)))
            with pool.Fori(NTL - AHEAD, NTL + LAG) as j:
                refill(j, follower(j))
            for s in range(2):
                pool.wait_ge(raw_in[s], 16 * ((E - 2) * WPIECES // 2 + 1))

        @block.sync
        def _(sp):
            sp.sem_inc(st[0], 16)
            sp.sem_inc(st[1], 16)

            def step(j, k, i, last):
                sp.wait_ge(ob_rdy, j + 1)
                sp.dma_start(ys[bass.ds(j * P, P), :], ob[:, k, :]).then_inc(st[k], 16)

            looped(sp, NTL, 2, step)
            for k in range(2):
                sp.wait_ge(st[k], 16 * (NTL // 2 + 1))

        @block.tensor
        def _(pe):
            used = pe.value_load(plan["used"][0:1, 0:1], min_val=FULL, max_val=NTL)

            def where_used(j, matmuls, done):
                if isinstance(j, int) and j >= FULL:
                    with pe.If(used > j):
                        matmuls()
                    with pe.Else():
                        pe.sem_inc(done, 1)
                else:
                    matmuls()

            def turn_rows(j, m, i):
                k = m % 2
                pe.wait_ge(x_in[m], 16 * (i + 1))
                pe.wait_ge(xlo_rdy, j + 1)
                for c in range(DC):
                    ins = pe.transpose(tr[:, k, c * P:(c + 1) * P], xb[:, m * D + c * P:m * D + (c + 1) * P], const["ident"][:])
                ins.then_inc(tr_rdy, 1)

            def up(j, k):
                need = pe.value_load(plan["tile"][0:1, 0, bass.ds(j, 1)], min_val=1, max_val=E)
                off = pe.value_load(plan["tile"][0:1, 1, bass.ds(j, 1)], min_val=0, max_val=WPIECES * WPIECE)
                pe.wait_ge(w_rdy, need * WPIECES)
                pe.wait_ge(xlo_rdy, j + 3)
                pe.wait_ge(ac_rdy, j + 1)

                def matmuls():
                    for c in range(DC):
                        xh, xl = x_hi[:, k, c * P:(c + 1) * P], x_lo[:, k, c * P:(c + 1) * P]
                        for n, (a, w) in enumerate(((xh, w_hi), (xh, w_lo), (xl, w_hi))):
                            for q in range(2):
                                ins = pe.matmul(gu[:, q, :], a, w[:, bass.ds(off + (c * WPIECE + q * H), H)],
                                                start=(c == 0 and n == 0), stop=(c == DC - 1 and n == 2))
                    ins.then_inc(gu_rdy, 1)

                where_used(j, matmuls, gu_rdy)

            def turn_act(j, k):
                pe.wait_ge(ac_rdy, j + 2)
                pe.wait_ge(alo_rdy, j + 1)
                for c in range(DC):
                    ins = pe.transpose(at[:, k, c * P:(c + 1) * P], ac[:, k, c * P:(c + 1) * P], const["ident"][:])
                ins.then_inc(at_rdy, 1)

            def down(j, k):
                off = pe.value_load(plan["tile"][0:1, 1, bass.ds(j, 1)], min_val=0, max_val=WPIECES * WPIECE)
                pe.wait_ge(alo_rdy, j + 3)

                def matmuls():
                    for c in range(DC):
                        ah, al = a_hi[:, k, c * P:(c + 1) * P], a_lo[:, k, c * P:(c + 1) * P]
                        for n, (a, w) in enumerate(((ah, w_hi), (ah, w_lo), (al, w_hi))):
                            ins = pe.matmul(dn[:, k, :], a, w[:, bass.ds(off + (DC * WPIECE + c * D), D)],
                                            start=(c == 0 and n == 0), stop=(c == DC - 1 and n == 2))
                    ins.then_inc(dn_rdy, 1)

                where_used(j, matmuls, dn_rdy)

            pe.sem_inc(xlo_rdy, 2)
            pe.sem_inc(alo_rdy, 2)
            pe.sem_inc(ac_rdy, 1)
            pe.sem_inc(dn_rdy, 2)
            turn_rows(0, 0, 0)
            up(0, 0)
            turn_rows(1, 1, 0)
            def step(j, m, i):
                turn_act(j - 1, 1 - m % 2)
                up(j, m % 2)
                turn_rows(j + 1, (m + 1) % AHEAD, i + (m + 1) // AHEAD)
                down(j - 1, 1 - m % 2)

            ROUNDS = (FULL - 1) // AHEAD
            with pe.Fori(0, ROUNDS) as i:
                for m in range(AHEAD):
                    step(i * AHEAD + (m + 1), (m + 1) % AHEAD, i + (m + 1) // AHEAD)
            for j in range(ROUNDS * AHEAD + 1, NTL - 1):
                step(j, j % AHEAD, j // AHEAD)
            j = NTL - 1
            turn_act(j - 1, 0)
            up(j, 1)
            down(j - 1, 0)
            turn_act(j, 1)
            down(j, 1)

        @block.scalar
        def _(act):
            def x_part(j, k):
                act.wait_ge(tr_rdy, j + 1)
                act.activation(x_hi[:, k, :], tr[:, k, :], ACT.Copy).then_inc(xhi_rdy, 1)

            def gelu(j, k):
                act.wait_ge(gu_rdy, j + 1)
                act.activation(gl[:, k, :], gu[:, 0, :], ACT.Gelu_apprx_tanh).then_inc(gl_rdy, 1)

            def a_part(j, k):
                act.wait_ge(at_rdy, j + 1)
                act.activation(a_hi[:, k, :], at[:, k, :], ACT.Copy).then_inc(ahi_rdy, 1)

            def out(j, k, i):
                act.wait_ge(dn_rdy, j + 3)
                act.wait_ge(st[k], 16 * (i + 1))
                act.activation(ob[:, k, :], dn[:, k, :], ACT.Copy).then_inc(ob_rdy, 1)

            x_part(0, 0)
            gelu(0, 0)
            x_part(1, 1)
            with act.Fori(0, NTL // 2 - 1) as i:
                for k in range(2):
                    j = i * 2 + k + 1
                    a_part(j - 1, k)
                    gelu(j, 1 - k)
                    x_part(j + 1, k)
                    out(j - 1, k, i)
            j = NTL - 1
            a_part(j - 1, 0)
            gelu(j, 1)
            out(j - 1, 0, NTL // 2 - 1)
            a_part(j, 1)
            out(j, 1, NTL // 2 - 1)

        @block.vector
        def _(dve):
            def x_part(j, k):
                dve.wait_ge(xhi_rdy, j + 1)
                dve.tensor_tensor(x_lo[:, k, :], tr[:, k, :], x_hi[:, k, :].bitcast(F32), ALU.subtract).then_inc(xlo_rdy, 1)

            def gate(j, k):
                dve.wait_ge(gl_rdy, j + 1)
                dve.tensor_tensor(ac[:, k, :], gu[:, 1, :], gl[:, k, :], ALU.mult).then_inc(ac_rdy, 1)

            def a_part(j, k):
                dve.wait_ge(ahi_rdy, j + 1)
                dve.tensor_tensor(a_lo[:, k, :], at[:, k, :], a_hi[:, k, :].bitcast(F32), ALU.subtract).then_inc(alo_rdy, 1)

            x_part(0, 0)
            gate(0, 0)
            x_part(1, 1)
            with dve.Fori(0, NTL // 2 - 1) as i:
                for k in range(2):
                    j = i * 2 + k + 1
                    a_part(j - 1, k)
                    gate(j, 1 - k)
                    x_part(j + 1, k)
            j = NTL - 1
            a_part(j - 1, 0)
            gate(j, 1)
            a_part(j, 1)


class Front:

    def __init__(self, mem, const, x, nx, ny, joined=None, x_new=None, ng=2):
        self.const, self.x, self.nx, self.ny, self.joined, self.x_to, self.ng = const, x, nx, ny, joined, x_new, ng
        self.xb = mem.sb("xb", [P, nx, D])
        self.yb = mem.sb("yb", [P, ny, D])
        self.bn = mem.sb("bn", [P, 2, 6])
        self.mv = mem.sb("mv", [P, 2, 2])
        self.sd = mem.sb("sd", [P, 2])
        self.rstd = mem.sb("rstd", [P, 2])
        self.tr = mem.ps("tr", [P, 2, D])
        self.x_in = mem.sems("x_in", nx)
        (self.bn_rdy, self.mv_rdy, self.sd_rdy, self.rstd_rdy, self.y_rdy, self.tr_rdy, self.hi_rdy, self.lo_rdy) = (
            mem.sem(n) for n in ("bn_rdy", "mv_rdy", "sd_rdy", "rstd_rdy", "y_rdy", "tr_rdy", "hi_rdy", "lo_rdy"))
        if joined:
            self.gb = mem.sb("gb", [P, ng, TOPK, D])
            self.g_in = mem.sems("g_in", ng)
            self.x_st = mem.sems("x_st", nx)
            self.one_rdy, self.x_rdy = mem.sem("one_rdy"), mem.sem("x_rdy")

    def load(self, sp, t, k):
        sp.dma_start(self.xb[:, k, :], self.x[bass.ds(t * P, P), :]).then_inc(self.x_in[k], 16)

    def sp_tile(self, sp, t, k, i, ahead):
        if self.joined:
            sp.wait_ge(self.x_rdy, t + 1)
            sp.dma_start(self.x_to[bass.ds(t * P, P), :], self.xb[:, k, :]).then_inc(self.x_st[k], 16)
        if ahead:
            sp.wait_ge(self.y_rdy, t + 1)
            if self.joined:
                sp.wait_ge(self.x_st[k], 16 * (i + 1))
            self.load(sp, t + self.nx, k)

    def sp_end(self, sp):
        if self.joined:
            for k in range(self.nx):
                sp.wait_ge(self.x_st[k], 16 * (NT // self.nx))

    def gather(self, pool, begin=0, end=NT):
        ys, plan = self.joined
        for t in range(begin, end):
            if t >= self.ng:
                pool.wait_ge(self.x_rdy, t - self.ng + 1)
            for k in range(TOPK):
                pool.indirect_dma_start(
                    self.gb[:, t % self.ng, k, :], None, ys, bass.IndirectOffsetOnAxis(ap=plan["slot"][:, k, t:t + 1], axis=0),
                ).then_inc(self.g_in[t % self.ng], 16)

    def stats(self, dve, t, k, i, g):
        kg = k % self.ng
        xk = self.xb[:, k, :]
        dve.wait_ge(self.x_in[k], 16 * (i + 1))
        if self.joined:
            w = self.joined[1]["weight"]
            dve.wait_ge(self.g_in[kg], 16 * TOPK * (g + 1))
            dve.scalar_tensor_tensor(xk, self.gb[:, kg, 0, :], w[:, 0, bass.ds(t, 1)], xk, ALU.mult, ALU.add).then_inc(self.one_rdy, 1)
            dve.wait_ge(self.one_rdy, t + 1)
            dve.scalar_tensor_tensor(xk, self.gb[:, kg, 1, :], w[:, 1, bass.ds(t, 1)], xk, ALU.mult, ALU.add).then_inc(self.x_rdy, 1)
            dve.wait_ge(self.x_rdy, t + 1)
        dve.bn_stats(self.bn[:, k % 2, :], xk).then_inc(self.bn_rdy, 1)

    def moments(self, dve, k):
        dve.bn_aggr(self.mv[:, k % 2, :], self.bn[:, k % 2, :]).then_inc(self.mv_rdy, 1)

    def first(self, dve):
        self.stats(dve, 0, 0, 0, 0)
        dve.wait_ge(self.bn_rdy, 1)
        self.moments(dve, 0)

    def resume(self, dve, t, k):
        self.stats(dve, t, k, 0, t // self.ng)
        dve.wait_ge(self.bn_rdy, t + 1)
        self.moments(dve, k)

    def normalise(self, dve, t, k, i, ky, ahead):
        kn = (k + 1) % self.nx
        if ahead:
            n = i + (1 if kn == 0 else 0)
            g = i * (self.nx // self.ng) + (k + 1) // self.ng
            self.stats(dve, t + 1, kn, n, g)
            dve.wait_ge(self.bn_rdy, t + 2)
        dve.wait_ge(self.sd_rdy, t + 1)
        dve.reciprocal(self.rstd[:, k % 2:k % 2 + 1], self.sd[:, k % 2:k % 2 + 1]).then_inc(self.rstd_rdy, 1)
        if ahead:
            self.moments(dve, kn)
        dve.wait_ge(self.rstd_rdy, t + 1)
        dve.tensor_scalar(self.yb[:, ky, :], self.xb[:, k, :], self.mv[:, k % 2, 0:1], self.rstd[:, k % 2:k % 2 + 1],
                          ALU.subtract, ALU.mult).then_inc(self.y_rdy, 1)

    def deviation(self, act, t, k):
        act.wait_ge(self.mv_rdy, t + 1)
        act.activation(self.sd[:, k % 2:k % 2 + 1], self.mv[:, k % 2, 1:2], ACT.Sqrt, bias=self.const["eps"][:]).then_inc(self.sd_rdy, 1)

    def free(self, pe):
        pe.sem_inc(self.lo_rdy, 2)

    def turn(self, pe, t, k, ky):
        pe.wait_ge(self.y_rdy, t + 1)
        pe.wait_ge(self.lo_rdy, t + 1)
        for c in range(DC):
            ins = pe.transpose(self.tr[:, k % 2, c * P:(c + 1) * P], self.yb[:, ky, c * P:(c + 1) * P], self.const["ident"][:])
        ins.then_inc(self.tr_rdy, 1)

    def hi(self, act, t, k, to):
        act.wait_ge(self.tr_rdy, t + 1)
        act.activation(to, self.tr[:, k % 2, :].rearrange("p (c m) -> p c m", c=DC), ACT.Copy).then_inc(self.hi_rdy, 1)

    def lo(self, dve, t, k, to, hi):
        dve.wait_ge(self.hi_rdy, t + 1)
        dve.tensor_tensor(to, self.tr[:, k % 2, :].rearrange("p (c m) -> p c m", c=DC), hi.bitcast(F32), ALU.subtract).then_inc(self.lo_rdy, 1)


def products(parts_a, parts_b):
    (ah, al), (bh, bl) = parts_a, parts_b
    return ((ah, bh), (ah, bl), (al, bh))


GA = 4
QW = GA * P


def projection_stage(nc, stage, const, x, x_new, joined, q_w, k_w, v_w, q_parts, kst, v):
    with ExitStack() as ctx:
        mem = Memory(nc, ctx, stage)
        f = Front(mem, const, x, GA, GA, joined, x_new, GA)
        y_hi = mem.sb("y_hi", [P, 2, DC, QW], F32R)
        y_lo = mem.sb("y_lo", [P, 2, DC, QW], F32R)
        NQ = HEADS * HD
        raw = {"q": mem.sb("q_raw", [P, DC, NQ]), "k": mem.sb("k_raw", [P, DC, 3 * HD]), "v": mem.sb("v_raw", [P, DC, HD])}
        w_hi = {n: mem.sb(f"{n}_whi", list(r.shape), F32R) for n, r in raw.items()}
        w_lo = {n: mem.sb(f"{n}_wlo", list(r.shape), F32R) for n, r in raw.items()}
        q_hi = mem.sb("q_hi", [P, 2, QW], F32R)
        q_lo = mem.sb("q_lo", [P, 2, QW], F32R)
        q_ps = mem.ps("q", [P, 2, QW])
        k_ps = mem.ps("k", [P, QW])
        v_ps = mem.ps("v", [P, GA, HD])
        w_in, whi_rdy, wlo_rdy, ones_rdy = (mem.sem(n) for n in ("w_in", "whi_rdy", "wlo_rdy", "ones_rdy"))
        q_rdy, qhi_rdy, qlo_rdy, k_rdy, khi_rdy, klo_rdy, v_rdy, v_kept = (
            mem.sem(n) for n in ("q_rdy", "qhi_rdy", "qlo_rdy", "k_rdy", "khi_rdy", "klo_rdy", "v_rdy", "v_kept"))
        q_st = mem.sems("q_st", 2)
        block = ctx.enter_context(nc.Block())
        NG = NT // GA
        QC = NQ // P

        def parts(g2):
            return (y_hi[:, g2], y_lo[:, g2])

        def tile_of(buf, g2, j):
            return buf[:, g2, :, j * P:(j + 1) * P]

        def exists(g):
            return not isinstance(g, int) or g < NG

        def groups(eng, step):
            with eng.Fori(0, NG // 2 - 2) as i:
                for g2 in range(2):
                    step(i * 2 + g2, g2)
            for g in range(NG - 4, NG):
                step(g, g % 2)

        @block.sync
        def _(sp):
            for s in range(2):
                sp.sem_inc(q_st[s], 32)
            for t in range(4):
                f.load(sp, t, t)
            sp.dma_start(raw["q"][:], q_w).then_inc(w_in, 16)
            for n in range(3):
                sp.dma_start(raw["k"][:, :, n * HD:(n + 1) * HD], k_w).then_inc(w_in, 16)
            sp.dma_start(raw["v"][:], v_w).then_inc(w_in, 16)

            def query(g, m):
                s = m % 2
                sp.wait_ge(qlo_rdy, g * QC + m + 3)
                for n, part in enumerate((q_hi, q_lo)):
                    sp.dma_start(q_parts[n, m * P:(m + 1) * P, bass.ds(g * QW, QW)], part[:, s, :].bitcast(F32)).then_inc(q_st[s], 16)

            for g in range(2):
                for j in range(GA):
                    f.sp_tile(sp, g * GA + j, j, g, True)

            def step(g, g2):
                for m in range(QC):
                    query(g, m)
                    if exists(g + 2):
                        f.sp_tile(sp, (g + 2) * GA + m, m, g + 2, exists(g + 3))

            groups(sp, step)
            f.sp_end(sp)
            for s in range(2):
                sp.wait_ge(q_st[s], 32 * (NG * QC // 2 + 1))

        @block.gpsimd
        def _(pool):
            f.gather(pool, 0, GA)
            pool.memset(kst[96:98, :].bitcast(F32), 1.0).then_inc(ones_rdy, 1)
            f.gather(pool, GA)
            pool.wait_ge(ones_rdy, 1)

        @block.tensor
        def _(pe):
            f.free(pe)
            pe.sem_inc(qlo_rdy, 2)
            pe.sem_inc(klo_rdy, 1)
            pe.sem_inc(v_kept, 1)

            def main(g, g2):
                yp = parts(g2)
                pe.wait_ge(f.lo_rdy, (g + 1) * GA + 2)
                pe.wait_ge(klo_rdy, g + 1)
                for c in range(DC):
                    for n, (a, b) in enumerate(products((w_hi["k"][:, c, :], w_lo["k"][:, c, :]), (yp[0][:, c, :], yp[1][:, c, :]))):
                        ins = pe.matmul(k_ps[0:3 * HD, :], a, b, start=(c == 0 and n == 0), stop=(c == DC - 1 and n == 2))
                ins.then_inc(k_rdy, 1)
                for m in range(QC):
                    pe.wait_ge(qlo_rdy, g * QC + m + 1)
                    for c in range(DC):
                        wq = (w_hi["q"][:, c, m * P:(m + 1) * P], w_lo["q"][:, c, m * P:(m + 1) * P])
                        for n, (a, b) in enumerate(products(wq, (yp[0][:, c, :], yp[1][:, c, :]))):
                            ins = pe.matmul(q_ps[:, m % 2, :], a, b, start=(c == 0 and n == 0), stop=(c == DC - 1 and n == 2))
                    ins.then_inc(q_rdy, 1)
                    if exists(g + 1):
                        f.turn(pe, (g + 1) * GA + m, m, m)
                pe.wait_ge(v_kept, g + 1)
                for j in range(GA):
                    for c in range(DC):
                        yt = (tile_of(y_hi, g2, j)[:, c, :], tile_of(y_lo, g2, j)[:, c, :])
                        for n, (a, b) in enumerate(products(yt, (w_hi["v"][:, c, :], w_lo["v"][:, c, :]))):
                            ins = pe.matmul(v_ps[:, j, :], a, b, start=(c == 0 and n == 0), stop=(c == DC - 1 and n == 2))
                ins.then_inc(v_rdy, 1)

            for j in range(GA):
                f.turn(pe, j, j, j)
            pe.wait_ge(wlo_rdy, 3)
            groups(pe, main)

        @block.scalar
        def _(act):
            f.deviation(act, 0, 0)
            act.wait_ge(w_in, 80)
            for n in ("k", "q", "v"):
                act.activation(w_hi[n][:], raw[n][:], ACT.Copy).then_inc(whi_rdy, 1)

            def front(g):
                for j in range(GA):
                    f.deviation(act, g * GA + j + 1, (j + 1) % GA)

            def main(g, m):
                if m == 0:
                    act.wait_ge(k_rdy, g + 1)
                    act.activation(kst[0:3 * HD, bass.ds(g * QW, QW)], k_ps[0:3 * HD, :], ACT.Copy).then_inc(khi_rdy, 1)
                s = m % 2
                act.wait_ge(q_rdy, g * QC + m + 1)
                act.wait_ge(q_st[s], 32 * (g * (QC // 2) + m // 2 + 1))
                act.activation(q_hi[:, s, :], q_ps[:, s, :], ACT.Copy).then_inc(qhi_rdy, 1)

            front(0)
            for j in range(GA):
                f.hi(act, j, j, tile_of(y_hi, 0, j))
            front(1)

            def step(g, g2):
                for m in range(QC):
                    main(g, m)
                    if exists(g + 1):
                        f.hi(act, (g + 1) * GA + m, m, tile_of(y_hi, 1 - g2, m))
                    t = (g + 2) * GA + m
                    if exists(g + 2) and not (isinstance(t, int) and t + 1 == NT):
                        f.deviation(act, t + 1, (m + 1) % GA)
                act.wait_ge(v_rdy, g + 1)
                act.activation(v[:, bass.ds(g * GA, GA), :], v_ps[:], ACT.Copy).then_inc(v_kept, 1)

            groups(act, step)

        @block.vector
        def _(dve):
            f.first(dve)

            def front(g, j):
                f.normalise(dve, g * GA + j, j, g, j, not (isinstance(g, int) and g * GA + j + 1 == NT))

            def low_part(g, g2, j):
                f.lo(dve, g * GA + j, j, tile_of(y_lo, g2, j), tile_of(y_hi, g2, j))

            def main(g, m):
                if m == 0:
                    dve.wait_ge(khi_rdy, g + 1)
                    kl = kst[HD:2 * HD, bass.ds(g * QW, QW)]
                    dve.tensor_tensor(kl, k_ps[HD:2 * HD, :], kl.bitcast(F32), ALU.subtract).then_inc(klo_rdy, 1)
                s = m % 2
                dve.wait_ge(qhi_rdy, g * QC + m + 1)
                dve.tensor_tensor(q_lo[:, s, :], q_ps[:, s, :], q_hi[:, s, :].bitcast(F32), ALU.subtract).then_inc(qlo_rdy, 1)

            for j in range(GA):
                front(0, j)
            for j in range(GA):
                low_part(0, 0, j)
            for n, name in enumerate(("k", "q", "v")):
                dve.wait_ge(whi_rdy, n + 1)
                dve.tensor_tensor(w_lo[name][:], raw[name][:], w_hi[name][:].bitcast(F32), ALU.subtract).then_inc(wlo_rdy, 1)
            for j in range(GA):
                front(1, j)

            def step(g, g2):
                for m in range(QC):
                    main(g, m)
                    if exists(g + 1):
                        low_part(g + 1, 1 - g2, m)
                    if exists(g + 2):
                        front(g + 2, m)

            groups(dve, step)


QT = S // P
HALF = HEADS // 2
UNITS = 2 * QT
OUT_AT = 7
TURN_AT = 11
KROWS = 3 * HD


def attention_stage(nc, stage, const, q_parts, kst, v, attn, o_w, w_hi, w_lo):
    with ExitStack() as ctx:
        mem = Memory(nc, ctx, stage)
        qst = mem.sb("qst", [P, 2, HEADS, P], F32R)
        pt = mem.sb("pt", [P, 4, HALF * P])
        pairs = mem.sb("pairs", [P, 4, 2, HALF * P])
        quads = mem.sb("quads", [P, 2, HALF * P])
        mx = mem.sb("mx", [P, HEADS, 2])
        neg = mem.sb("neg", [P, HALF])
        msplit = mem.sb("msplit", [P, 2, HALF], F32R)
        mT = mem.sb("mT", [2 * HALF, P])
        inv = mem.sb("inv", [P, 2 * P])
        raw = mem.sb("raw", [P, DC, D])
        sc = mem.ps("sc", [P, 2, 4 * P])
        am = mem.ps("am", [P, 2, 8 * P])
        pv = mem.ps("pv", [P, 2, 2, 2 * P])
        q_in = [mem.sems(f"q_in{k}_", 2) for k in range(2)]
        m_in = mem.sems("m_in", 2)
        w_in, whi_rdy = mem.sem("w_in"), mem.sem("whi_rdy")
        am_rdy, mx_rdy, neg_rdy, mhi_rdy, ms_rdy, mT_rdy, mT_kept, s_rdy, p_rdy, pv_rdy, pair_rdy, quad_rdy, half_rdy, sum_rdy, inv_rdy, o_rdy = (
            mem.sem(n) for n in ("am_rdy", "mx_rdy", "neg_rdy", "mhi_rdy", "ms_rdy", "mT_rdy", "mT_kept", "s_rdy",
                                 "p_rdy", "pv_rdy", "pair_rdy", "quad_rdy", "half_rdy", "sum_rdy", "inv_rdy", "o_rdy"))
        block = ctx.enter_context(nc.Block())
        N = B * QT
        QUADS = UNITS // 4

        def rounds(eng, step):
            for k in range(2):
                step(k, k, 0, 0, 0)
            for b in range(B):
                with eng.Fori(0 if b else 1, QT // 2 - 1) as i:
                    for k in range(2):
                        step(i * 2 + (k + b * QT), k, i + b * (QT // 2), b, b)
                for k in range(2):
                    n = (b + 1) * QT - 2 + k
                    step(n, k, n // 2, b, b if k == 0 else (b + 1 if b + 1 < B else None))

        def lagging(do, n, q, size=UNITS):
            if q >= 0:
                do(n, q)
            elif not is_first(n):
                do(n - 1, q + size)

        def is_first(n):
            return isinstance(n, int) and n == 0

        @block.sync
        def _(sp):
            def load(n, k, h):
                for r, part in enumerate((0, 0, 1)):
                    src = q_parts[part, h * HALF * HD:(h + 1) * HALF * HD, bass.ds(n * P, P)].rearrange("(h d) q -> d h q", d=HD)
                    sp.dma_start(qst[r * HD:(r + 1) * HD, k, h * HALF:(h + 1) * HALF, :].bitcast(F32), src).then_inc(q_in[k][h], 16)

            def maxima(n, k, h):
                sp.wait_ge(mT_kept, n * 2 + (h + 1))
                for part in range(2):
                    row = KROWS + part
                    sp.dma_start(qst[row:row + 1, k, h * HALF:(h + 1) * HALF, :].bitcast(F32),
                                 mT[part * HALF:(part + 1) * HALF, :]).then_inc(m_in[h], 16)

            for n in range(2):
                for h in range(2):
                    load(n, n, h)
            for c in range(DC):
                sp.dma_start(raw[:, c, :], o_w[:, c, :]).then_inc(w_in, 16)
            maxima(0, 0, 0)

            def step(n, k, i, b, nb):
                more = not (isinstance(n, int) and n + 2 >= N)
                maxima(n, k, 1)
                sp.wait_ge(s_rdy, n * (2 * UNITS) + 2 * QT)
                if more:
                    load(n + 2, k, 0)
                if nb is not None:
                    maxima(n + 1, 1 - k, 0)
                sp.wait_ge(s_rdy, n * (2 * UNITS) + 2 * UNITS)
                if more:
                    load(n + 2, k, 1)

            rounds(sp, step)

        @block.tensor
        def _(pe):
            pe.sem_inc(mx_rdy, 2)
            pe.sem_inc(p_rdy, 2)
            pe.sem_inc(o_rdy, 2)

            def score(n, k, b, u, g):
                h, kt = divmod(u, QT)
                if kt == 0 and g == 0:
                    pe.wait_ge(m_in[h], n * 32 + 32)
                pe.wait_ge(p_rdy, n * (2 * UNITS) + (2 * u + g + 1))
                hh = h * HALF + g * 4
                pe.matmul(sc[:, g, :], kst[0:KROWS + 2, b * S + kt * P:b * S + (kt + 1) * P], qst[0:KROWS + 2, k, hh:hh + 4, :],
                          start=True, stop=True).then_inc(s_rdy, 1)

            def maxi(n, k, i, b, u, g):
                hd, kh = divmod(u, 2)
                if g == 0:
                    if u % QT == 0:
                        pe.wait_ge(q_in[k][u // QT], i * 48 + 48)
                    pe.wait_ge(mx_rdy, n * UNITS + (u + 1))
                o = b * S + kh * (S // 2) + g * 4 * P
                ins = pe.matmul(am[:, u % 2, g * 4 * P:(g + 1) * 4 * P], qst[0:KROWS, k, hd, :], kst[0:KROWS, o:o + 4 * P], start=True, stop=True)
                if g:
                    ins.then_inc(am_rdy, 1)

            def turn(n, h):
                pe.wait_ge(ms_rdy, n * 2 + (h + 1))
                pe.wait_ge(o_rdy, n * 2 + (h + 1))
                pe.transpose(pv[0:2 * HALF, h, 0, 0:P], msplit[:].rearrange("p s h -> p (s h)").bitcast(F32),
                             const["ident"][:]).then_inc(mT_rdy, 1)

            def values(n, b, u):
                h, kt = divmod(u, QT)
                if kt == 0:
                    pe.wait_ge(o_rdy, n * 2 + (h + 1))
                    pe.wait_ge(mT_kept, n * 2 + (h + 1))
                pe.wait_ge(p_rdy, n * (2 * UNITS) + (2 * u + 4))
                for j in range(4):
                    ins = pe.matmul(pv[HD * j:HD * (j + 1), h, 0, :], v[:, b * QT + kt, :], pt[:, u % 4, 2 * P * j:2 * P * (j + 1)],
                                    start=(kt == 0), stop=(kt == QT - 1), skip_group_check=True)
                ins.then_inc(pv_rdy, 1)

            def sums(n, q):
                h, part = divmod(q, QUADS // 2)
                pe.wait_ge(quad_rdy, n * (2 * QUADS) + (2 * q + 10))
                pe.wait_ge(half_rdy, n * QUADS + (q + 5))
                for j in range(4):
                    ins = pe.matmul(pv[HD * j:HD * (j + 1), h, 1, :], const["ones"][:, 0:HD], quads[:, q % 2, 2 * P * j:2 * P * (j + 1)],
                                    start=False, stop=(part == QUADS // 2 - 1), skip_group_check=True)
                ins.then_inc(sum_rdy, 1)

            for u in range(UNITS):
                for g in range(2):
                    maxi(0, 0, 0, 0, u, g)
                if u == QT + TURN_AT:
                    turn(0, 0)
            for g in range(2):
                score(0, 0, 0, 0, g)

            def step(n, k, i, b, nb):
                for u in range(UNITS):
                    if u == TURN_AT:
                        turn(n, 1)
                    if u == QT + TURN_AT and nb is not None:
                        turn(n + 1, 0)
                    for g in range(2):
                        if nb is not None:
                            maxi(n + 1, 1 - k, i + k, nb, u, g)
                        if u + 1 < UNITS:
                            score(n, k, b, u + 1, g)
                        elif nb is not None:
                            score(n + 1, 1 - k, nb, 0, g)
                    values(n, b, u)
                    if u % 4 == 0:
                        lagging(sums, n, u // 4 - 2, QUADS)

            rounds(pe, step)
            sums(N - 1, QUADS - 2)
            sums(N - 1, QUADS - 1)

        @block.scalar
        def _(act):
            act.sem_inc(pv_rdy, 4)
            act.sem_inc(pair_rdy, 2)
            act.wait_ge(w_in, 16 * DC)
            for c in range(DC):
                act.activation(w_hi[:, c, :], raw[:, c, :], ACT.Copy).then_inc(whi_rdy, 1)

            def step(n, k, i, b, nb):
                for u in range(UNITS):
                    for g in range(2):
                        act.wait_ge(s_rdy, n * (2 * UNITS) + (2 * u + g + 1))
                        if g == 0:
                            act.wait_ge(pv_rdy, n * UNITS + (u + 1))
                            if u % 2 == 0:
                                act.wait_ge(pair_rdy, n * (UNITS // 2) + (u // 2 + 1))
                        act.activation(pt[:, u % 4, g * 4 * P:(g + 1) * 4 * P], sc[:, g, :], ACT.Exp, scale=HD ** -0.5).then_inc(p_rdy, 1)

            rounds(act, step)

        @block.gpsimd
        def _(pool):
            pool.sem_inc(half_rdy, 4)
            for c in range(DC):
                pool.wait_ge(whi_rdy, c + 1)
                pool.tensor_tensor(w_lo[:, c, :], raw[:, c, :], w_hi[:, c, :].bitcast(F32), ALU.subtract)

            def step(n, k, i, b, nb):
                for p in range(UNITS // 2):
                    q = p // 2
                    if p % 2 == 0:
                        pool.wait_ge(quad_rdy, n * (2 * QUADS) + (2 * q + 2))
                        pool.wait_ge(half_rdy, n * QUADS + (q + 1))
                    pool.wait_ge(p_rdy, n * (2 * UNITS) + (4 * p + 6))
                    pool.tensor_tensor(pairs[:, q % 4, p % 2, :], pt[:, 2 * p % 4, :], pt[:, (2 * p + 1) % 4, :], ALU.add).then_inc(pair_rdy, 1)
                    if p % 2:
                        pool.wait_ge(pair_rdy, n * (UNITS // 2) + (p + 3))
                        pool.wait_ge(sum_rdy, n * QUADS + (q + 1))
                        pool.tensor_tensor(quads[:, q % 2, 4 * P:], pairs[:, q % 4, 0, 4 * P:], pairs[:, q % 4, 1, 4 * P:], ALU.add).then_inc(half_rdy, 1)

            rounds(pool, step)

        @block.vector
        def _(dve):
            dve.sem_inc(mT_rdy, 1)
            dve.sem_inc(quad_rdy, 8)
            dve.sem_inc(sum_rdy, 2)

            def maxi(n, u):
                dve.wait_ge(am_rdy, n * UNITS + (u + 1))
                dve.tensor_reduce(mx[:, u // 2, u % 2:u % 2 + 1], am[:, u % 2, :], AX.X, ALU.max).then_inc(mx_rdy, 1)

            def split(n, h):
                dve.wait_ge(mx_rdy, n * UNITS + (QT * (h + 1) + 2))
                dve.tensor_reduce(neg[:], mx[:, h * HALF:(h + 1) * HALF, :], AX.X, ALU.max, negate=True).then_inc(neg_rdy, 1)
                dve.wait_ge(neg_rdy, n * 2 + (h + 1))
                dve.wait_ge(mT_rdy, n * 2 + (h + 1))
                dve.tensor_copy(msplit[:, 0, :], neg[:]).then_inc(mhi_rdy, 1)
                dve.wait_ge(mhi_rdy, n * 2 + (h + 1))
                dve.tensor_tensor(msplit[:, 1, :], neg[:], msplit[:, 0, :].bitcast(F32), ALU.subtract).then_inc(ms_rdy, 1)

            def keep(n, h, first=False):
                dve.wait_ge(mT_rdy, n * 2 + (h + 2))
                if not first:
                    dve.wait_ge(m_in[1 - h], n * 32 + (32 if h else 0))
                dve.tensor_copy(mT[:], pv[0:2 * HALF, h, 0, 0:P]).then_inc(mT_kept, 1)

            def quad(n, piece):
                q, r = divmod(piece, 4)
                if r > 1:
                    return
                if r == 0:
                    dve.wait_ge(pair_rdy, n * (UNITS // 2) + (2 * q + 4))
                    dve.wait_ge(sum_rdy, n * QUADS + (q + 1))
                cut = slice(2 * P * r, 2 * P * (r + 1))
                dve.tensor_tensor(quads[:, q % 2, cut], pairs[:, q % 4, 0, cut], pairs[:, q % 4, 1, cut], ALU.add).then_inc(quad_rdy, 1)

            def shares(n, h):
                dve.wait_ge(sum_rdy, n * QUADS + (QUADS // 2 * (h + 1) + 2))
                dve.reciprocal(inv[:], pv[:, h, 1, :]).then_inc(inv_rdy, 1)

            def output(n, h):
                dve.wait_ge(inv_rdy, n * 2 + (h + 1))
                dve.tensor_tensor(attn[:, bass.ds(n, 1), h, :], pv[:, h, 0, :].unsqueeze(1), inv[:].unsqueeze(1), ALU.mult).then_inc(o_rdy, 1)

            for u in range(UNITS):
                maxi(0, u)
                if u == QT - 1:
                    split(0, 0)
                if u == QT + TURN_AT + 1:
                    keep(0, 0, True)
            split(0, 1)

            def step(n, k, i, b, nb):
                for u in range(UNITS):
                    if u == TURN_AT:
                        keep(n, 1)
                    if nb is not None:
                        maxi(n + 1, u)
                        if u == QT - 1:
                            split(n + 1, 0)
                        if u == QT + TURN_AT:
                            keep(n + 1, 0)
                    for m, h, at in ((n - 1, 1, OUT_AT), (n, 0, QT + OUT_AT)):
                        if u in (at, at + 1) and not (h and is_first(n)):
                            (output if u > at else shares)(m, h)
                    lagging(quad, n, u - 5)
                if nb is not None:
                    split(n + 1, 1)

            rounds(dve, step)
            for piece in range(UNITS - 5, UNITS):
                quad(N - 1, piece)
            shares(N - 1, 1)
            output(N - 1, 1)


def output_stage(nc, stage, const, attn, w_hi, w_lo, x, x_new):
    with ExitStack() as ctx:
        mem = Memory(nc, ctx, stage)
        NX = 4
        a_hi = mem.sb("a_hi", [P, 2, D], F32R)
        a_lo = mem.sb("a_lo", [P, 2, D], F32R)
        xb = mem.sb("xb", [P, NX, D])
        ob = mem.sb("ob", [P, 2, D])
        pr = mem.ps("pr", [P, 2, D])
        x_in, st = mem.sems("x_in", NX), mem.sems("st", 2)
        hi_rdy, lo_rdy, pr_rdy, ob_rdy = (mem.sem(n) for n in ("hi_rdy", "lo_rdy", "pr_rdy", "ob_rdy"))
        block = ctx.enter_context(nc.Block())

        def rows(t):
            return attn[:, bass.ds(t, 1)].rearrange("p a h m -> p a (h m)")

        @block.sync
        def _(sp):
            def load(t, k):
                sp.dma_start(xb[:, k, :], x[bass.ds(t * P, P), :]).then_inc(x_in[k], 16)

            for k in range(2):
                sp.sem_inc(st[k], 16)
            for t in range(NX):
                load(t, t)

            def step(t, k, i, last):
                sp.wait_ge(ob_rdy, t + 3)
                sp.dma_start(x_new[bass.ds(t * P, P), :], ob[:, k % 2, :]).then_inc(st[k % 2], 16)
                if not last:
                    load(t + NX, k)

            looped(sp, NT, NX, step)
            for k in range(2):
                sp.wait_ge(st[k], 16 * (NT // 2 + 1))

        @block.scalar
        def _(act):
            act.sem_inc(pr_rdy, 2)

            def step(t, k, i, last):
                act.wait_ge(pr_rdy, t + 1)
                act.activation(a_hi[:, k % 2, :].unsqueeze(1), rows(t), ACT.Copy).then_inc(hi_rdy, 1)

            looped(act, NT, NX, step)

        @block.vector
        def _(dve):
            def low_part(t, k):
                dve.wait_ge(hi_rdy, t + 1)
                dve.tensor_tensor(a_lo[:, k % 2, :].unsqueeze(1), rows(t), a_hi[:, k % 2, :].bitcast(F32).unsqueeze(1), ALU.subtract).then_inc(lo_rdy, 1)

            low_part(0, 0)

            def step(t, k, i, last):
                if not (last and k == NX - 1):
                    low_part(t + 1, k + 1)
                dve.wait_ge(pr_rdy, t + 3)
                dve.wait_ge(x_in[k], i * 16 + 16)
                dve.wait_ge(st[k % 2], i * (16 * NX // 2) + (k // 2 * 16 + 16))
                dve.tensor_tensor(ob[:, k % 2, :], pr[:, k % 2, :], xb[:, k, :], ALU.add).then_inc(ob_rdy, 1)

            looped(dve, NT, NX, step)

        @block.tensor
        def _(pe):
            pe.sem_inc(ob_rdy, 2)

            def step(t, k, i, last):
                pe.wait_ge(lo_rdy, t + 1)
                pe.wait_ge(ob_rdy, t + 1)
                for c in range(DC):
                    cut = slice(c * P, (c + 1) * P)
                    for n, (a, b) in enumerate(products((a_hi[:, k % 2, cut], a_lo[:, k % 2, cut]), (w_hi[:, c, :], w_lo[:, c, :]))):
                        ins = pe.matmul(pr[:, k % 2, :], a, b, start=(c == 0 and n == 0), stop=(c == DC - 1 and n == 2))
                ins.then_inc(pr_rdy, 1)

            looped(pe, NT, NX, step)


GF = 2
FW = GF * P


def ffn_stage(nc, stage, const, x, x_new, joined, w_gate, w_up, w_down, gate_s, up_s, down_s, x_out):
    with ExitStack() as ctx:
        mem = Memory(nc, ctx, stage)
        f = Front(mem, const, x, 2 * GF, GF, joined, x_new)
        PIECE = D
        wg_hi, wg_lo = mem.sb("wg_hi", [P, DC, INTER], F32R), mem.sb("wg_lo", [P, DC, INTER], F32R)
        wu_hi, wu_lo = mem.sb("wu_hi", [P, DC, INTER], F32R), mem.sb("wu_lo", [P, DC, INTER], F32R)
        wd_hi, wd_lo = mem.sb("wd_hi", [P, IC, D], F32R), mem.sb("wd_lo", [P, IC, D], F32R)
        y_hi, y_lo = mem.sb("y_hi", [P, 2, DC, FW], F32R), mem.sb("y_lo", [P, 2, DC, FW], F32R)
        h_hi, h_lo = mem.sb("h_hi", [P, IC, FW], F32R), mem.sb("h_lo", [P, IC, FW], F32R)
        sg, hf = mem.sb("sg", [P, 2, FW]), mem.sb("hf", [P, 2, FW])
        rb, ob = mem.sb("rb", [P, GF, D]), mem.sb("ob", [P, GF, D])
        gs, us, ds_ = mem.sb("gs", [P, IC]), mem.sb("us", [P, IC]), mem.sb("ds", [P, D])
        diff, total, flag = mem.sb("diff", [P, 3 * DC * INTER // PIECE]), mem.sb("total", [P, 1]), mem.sb("flag", [1, 1], I32)
        gu = mem.ps("gu", [P, 2, 2, FW])
        dn = mem.ps("dn", [P, GF, D])
        raw_in, whi_rdy = mem.sems("raw_in", 3 * GF + 2), mem.sems("whi_rdy", 3)
        s_in, wlo_rdy, ds_rdy, cmp_rdy, diff_rdy, flag_rdy = (
            mem.sem(n) for n in ("s_in", "wlo_rdy", "ds_rdy", "cmp_rdy", "diff_rdy", "flag_rdy"))
        r_in, st = mem.sems("r_in", GF), mem.sems("st", GF)
        gu_rdy, sg_rdy, h_rdy, hhi_rdy, hlo_rdy, dn_rdy, o_half, o_rdy = (
            mem.sem(n) for n in ("gu_rdy", "sg_rdy", "h_rdy", "hhi_rdy", "hlo_rdy", "dn_rdy", "o_half", "o_rdy"))
        block = ctx.enter_context(nc.Block())
        NG = NT // GF
        res = x_new if joined else x

        raws = [t[:, j, :] for t in (rb, ob, f.xb[:, GF:2 * GF, :]) for j in range(GF)]
        raws += [t[:].rearrange("p k n -> p (k n)") for t in (sg, hf)]
        NR = len(raws)
        pieces = []
        for mats in ((w_gate, wg_hi[:], wg_lo[:]), (w_up, wu_hi[:], wu_lo[:]), (w_down, wd_hi[:], wd_lo[:])):
            flat = [t.rearrange("p a b -> p (a b)") for t in mats]
            for o in range(0, DC * INTER, PIECE):
                pieces.append([t[:, o:o + PIECE] for t in flat])

        def tile_of(buf, g2, j):
            return buf[:, g2, :, j * P:(j + 1) * P]

        def groups(eng, step):
            with eng.Fori(0, NG // 2 - 2) as i:
                for g2 in range(2):
                    step(i * 2 + g2, g2, i)
            for g in range(NG - 4, NG):
                step(g, g % 2, g // 2)

        def exists(g):
            return not isinstance(g, int) or g < NG

        @block.sync
        def _(sp):
            for j in range(GF):
                sp.sem_inc(st[j], 16)
            for t in range(GF):
                f.load(sp, t, t)
            for to, src in ((gs, gate_s), (us, up_s), (ds_, down_s.partition_broadcast(P))):
                sp.dma_start(to[:], src).then_inc(s_in, 16)
            for n, (src, hi, lo) in enumerate(pieces):
                if n >= NR:
                    sp.wait_ge(cmp_rdy, n - NR + 1)
                sp.dma_start(raws[n % NR], src).then_inc(raw_in[n % NR], 16)
            sp.wait_ge(cmp_rdy, len(pieces))
            for t in range(GF, 2 * GF):
                f.load(sp, t, t)

            def tiles(g, g2, i):
                for j in range(GF):
                    f.sp_tile(sp, g * GF + j, g2 * GF + j, i, exists(g + 2))

            tiles(0, 0, 0)
            tiles(1, 1, 0)

            def step(g, g2, i):
                for j in range(GF):
                    sp.wait_ge(o_rdy, g * GF + (j + 1))
                    if joined:
                        sp.wait_ge(f.x_st[g2 * GF + j], i * 16 + 16)
                    sp.dma_start(rb[:, j, :], res[bass.ds((g * GF + j) * P, P), :]).then_inc(r_in[j], 16)
                if exists(g + 2):
                    tiles(g + 2, g2, i + 1)
                for j in range(GF):
                    sp.wait_ge(o_rdy, g * GF + (j + 3))
                    sp.dma_start(x_out[bass.ds((g * GF + j) * P, P), :], ob[:, j, :]).then_inc(st[j], 16)

            groups(sp, step)
            f.sp_end(sp)
            for j in range(GF):
                sp.wait_ge(st[j], 16 * (NG + 1))

        @block.gpsimd
        def _(pool):
            if joined:
                f.gather(pool, 0, GF)
            for n in range(0, len(pieces), 3):
                hi = pieces[n][1]
                pool.wait_ge(raw_in[n % NR], 16 * (n // NR + 1))
                pool.tensor_scalar(hi, raws[n % NR], 1.0, None, ALU.mult).then_inc(whi_rdy[0], 1)
            if joined:
                f.gather(pool, GF)

        @block.tensor
        def _(pe):
            f.free(pe)
            pe.sem_inc(h_rdy, 2)
            pe.sem_inc(o_rdy, 2)
            pe.sem_inc(hlo_rdy, 2)

            def turn(g, g2):
                for j in range(GF):
                    f.turn(pe, g * GF + j, j, j)

            turn(0, 0)
            pe.wait_ge(diff_rdy, 2)
            pe.matmul(dn[0:1, 0, 0:1], const["ones"][:, 0:1], total[:], start=True, stop=True).then_inc(diff_rdy, 1)
            pe.wait_ge(flag_rdy, 1)
            some_low = pe.value_load(flag[0:1, 0:1], min_val=0, max_val=1)
            pe.wait_ge(wlo_rdy, len(pieces))

            def passes(a, b, low):
                return [(x, y) for x, y, is_low in zip(*zip(*products(a, b)), (False, True, False)) if low or not is_low]

            def step(g, g2, i, low):
                pe.wait_ge(f.lo_rdy, g * GF + (GF + 2))
                for m in range(IC):
                    k = (g2 * IC + m) % 2
                    pe.wait_ge(h_rdy, g * IC + (m + 1))
                    for q, (hi, lo) in enumerate(((wg_hi, wg_lo), (wu_hi, wu_lo))):
                        for c in range(DC):
                            w = (hi[:, c, m * P:(m + 1) * P], lo[:, c, m * P:(m + 1) * P])
                            ab = passes((y_hi[:, g2, c, :], y_lo[:, g2, c, :]), w, low)
                            for n, (y, w) in enumerate(ab):
                                ins = pe.matmul(gu[:, k, q, :], w, y, start=(c == 0 and n == 0), stop=(c == DC - 1 and n == len(ab) - 1))
                    ins.then_inc(gu_rdy, 1)
                if exists(g + 1):
                    turn(g + 1, 1 - g2)
                for j in range(GF):
                    pe.wait_ge(o_rdy, g * GF + (j + 1))
                    for m in range(IC):
                        if j == 0:
                            pe.wait_ge(hlo_rdy, g * IC + (m + 3))
                        hp = (h_hi[:, m, j * P:(j + 1) * P], h_lo[:, m, j * P:(j + 1) * P])
                        ab = passes(hp, (wd_hi[:, m, :], wd_lo[:, m, :]), low)
                        for n, (a, b) in enumerate(ab):
                            ins = pe.matmul(dn[:, j, :], a, b, start=(m == 0 and n == 0), stop=(m == IC - 1 and n == len(ab) - 1))
                    ins.then_inc(dn_rdy, 1)

            with pe.If(some_low == 0):
                groups(pe, lambda g, g2, i: step(g, g2, i, False))
            with pe.Else():
                groups(pe, lambda g, g2, i: step(g, g2, i, True))

        @block.scalar
        def _(act):
            def front(g, g2):
                for j in range(GF):
                    if not (isinstance(g, int) and g * GF + j + 1 >= NT):
                        f.deviation(act, g * GF + (j + 1), (g2 * GF + j + 1) % 4)

            def group_hi(g, g2):
                for j in range(GF):
                    f.hi(act, g * GF + j, j, tile_of(y_hi, g2, j))

            for t in range(GF):
                f.deviation(act, t, t)
            group_hi(0, 0)

            def magnitudes(n):
                lo = pieces[n][2]
                act.wait_ge(wlo_rdy, n + 1)
                act.activation(raws[n % NR], lo.bitcast(F32), ACT.Abs, accum_out=diff[:, n:n + 1]).then_inc(cmp_rdy, 1)

            def high(n):
                act.wait_ge(raw_in[n % NR], 16 * (n // NR + 1))
                act.activation(pieces[n][1], raws[n % NR], ACT.Copy).then_inc(whi_rdy[1], 1)

            high(1)
            for n in range(1, len(pieces)):
                if n % 3 == 1 and n + 3 < len(pieces):
                    high(n + 3)
                magnitudes(n - 1)
            magnitudes(len(pieces) - 1)
            f.deviation(act, GF, GF)
            front(1, 1)
            act.wait_ge(s_in, 48)

            def part(g, g2, m):
                act.wait_ge(h_rdy, g * IC + (m + 3))
                act.activation(h_hi[:, m, :], hf[:, (g2 * IC + m) % 2, :], ACT.Copy).then_inc(hhi_rdy, 1)

            def step(g, g2, i):
                for m in range(IC):
                    k = (g2 * IC + m) % 2
                    act.wait_ge(gu_rdy, g * IC + (m + 1))
                    act.activation(sg[:, k, :], gu[:, k, 0, :], ACT.Silu, scale=gs[:, m:m + 1]).then_inc(sg_rdy, 1)
                    if m:
                        part(g, g2, m - 1)
                part(g, g2, IC - 1)
                if exists(g + 1):
                    group_hi(g + 1, 1 - g2)
                if exists(g + 2):
                    front(g + 2, g2)

            groups(act, step)

        @block.vector
        def _(dve):
            f.first(dve)

            def front(g, g2, i):
                for j in range(GF):
                    f.normalise(dve, g * GF + j, g2 * GF + j, i, j, not (isinstance(g, int) and g * GF + j + 1 >= NT))

            def group_lo(g, g2):
                for j in range(GF):
                    f.lo(dve, g * GF + j, j, tile_of(y_lo, g2, j), tile_of(y_hi, g2, j))

            for j in range(GF):
                f.normalise(dve, j, j, 0, j, j + 1 < GF)
            for n, (src, hi, lo) in enumerate(pieces):
                if n % 3 == 2:
                    dve.wait_ge(raw_in[n % NR], 16 * (n // NR + 1))
                    dve.tensor_copy(hi, raws[n % NR]).then_inc(whi_rdy[2], 1)
                dve.wait_ge(whi_rdy[n % 3], n // 3 + 1)
                dve.tensor_tensor(lo, raws[n % NR], hi.bitcast(F32), ALU.subtract).then_inc(wlo_rdy, 1)
            dve.wait_ge(cmp_rdy, len(pieces))
            dve.tensor_reduce(total[:], diff[:, 0:len(pieces)], AX.X, ALU.add).then_inc(diff_rdy, 1)
            dve.wait_ge(diff_rdy, 1)
            dve.tensor_scalar(total[:], total[:], 0.0, None, ALU.not_equal).then_inc(diff_rdy, 1)
            dve.wait_ge(diff_rdy, 3)
            dve.tensor_scalar(flag[:], dn[0:1, 0, 0:1], 1.0, None, ALU.min).then_inc(flag_rdy, 1)
            f.resume(dve, GF, GF)
            dve.wait_ge(s_in, 48)
            dve.tensor_scalar(ds_[:], ds_[:], 0.5, None, ALU.mult).then_inc(ds_rdy, 1)
            dve.wait_ge(ds_rdy, 1)
            group_lo(0, 0)
            front(1, 1, 0)

            def part(g, g2, m):
                dve.wait_ge(hhi_rdy, g * IC + (m + 1))
                dve.tensor_tensor(h_lo[:, m, :], hf[:, (g2 * IC + m) % 2, :], h_hi[:, m, :].bitcast(F32), ALU.subtract).then_inc(hlo_rdy, 1)

            def step(g, g2, i):
                for m in range(IC):
                    k = (g2 * IC + m) % 2
                    dve.wait_ge(sg_rdy, g * IC + (m + 1))
                    dve.wait_ge(hlo_rdy, g * IC + (m + 1))
                    dve.scalar_tensor_tensor(hf[:, k, :], gu[:, k, 1, :], us[:, m:m + 1], sg[:, k, :], ALU.mult, ALU.mult).then_inc(h_rdy, 1)
                    if m:
                        part(g, g2, m - 1)
                part(g, g2, IC - 1)
                if exists(g + 1):
                    group_lo(g + 1, 1 - g2)
                if exists(g + 2):
                    front(g + 2, g2, i + 1)
                for j in range(GF):
                    dve.wait_ge(dn_rdy, g * GF + (j + 1))
                    dve.wait_ge(st[j], i * 32 + (g2 * 16 + 16))
                    dve.tensor_tensor(ob[:, j, :], dn[:, j, :], ds_[:], ALU.mult).then_inc(o_half, 1)
                    dve.wait_ge(o_half, g * GF + (j + 1))
                    dve.wait_ge(r_in[j], i * 32 + (g2 * 16 + 16))
                    dve.tensor_tensor(ob[:, j, :], ob[:, j, :], rb[:, j, :], ALU.add).then_inc(o_rdy, 1)

            groups(dve, step)


def keyvalue_stage(nc, stage, const, x, w_kv, w_qT, w_out, b_kv, b_q, b_out, gamma, beta, angles, x_out):
    with ExitStack() as ctx:
        mem = Memory(nc, ctx, stage)
        NB = QT
        xb, yb, y2 = mem.sb("xb", [P, 2, D]), mem.sb("yb", [P, 2, D]), mem.sb("y2", [P, 2, D])
        xy = mem.sb("xy", [P, NB, D])
        yT = mem.sb("yT", [P, NB, D])
        bn, mv = mem.sb("bn", [P, 6]), mem.sb("mv", [P, 2])
        sd, rstd = mem.sb("sd", [P, 1]), mem.sb("rstd", [P, 1])
        bn2, mv2 = mem.sb("bn2", [P, 6]), mem.sb("mv2", [P, 2])
        sd2, rstd2 = mem.sb("sd2", [P, 1]), mem.sb("rstd2", [P, 1])
        pause = mem.sb("pause", [P, 1])
        t_hi, t_lo = mem.sb("t_hi", [P, 2, D], F32R), mem.sb("t_lo", [P, 2, D], F32R)
        raw = mem.sb("raw", [P, DC, 2 * D])
        wk_hi, wk_lo = mem.sb("wk_hi", [P, DC, 2 * D], F32R), mem.sb("wk_lo", [P, DC, 2 * D], F32R)
        wq, wo = mem.sb("wq", [P, DC, D]), mem.sb("wo", [P, DC, D])
        aw, m_raw = raw[:, :, 0:D], raw[:, :, D:2 * D]
        m_hi, m_lo = mem.sb("m_hi", [P, DC, D], F32R), mem.sb("m_lo", [P, DC, D], F32R)
        gam, bet, bq = mem.sb("gam", [P, DC]), mem.sb("bet", [P, DC]), mem.sb("bq", [P, DC])
        bet_w, bq_w = mem.sb("bet_w", [P, DC, P]), mem.sb("bq_w", [P, DC, P])
        borow = mem.sb("borow", [1, D])
        bkv, bo = mem.sb("bkv", [P, 2, D]), mem.sb("bo", [P, D])
        cs = mem.sb("cs", [P, 2, 2, P])
        kv, kvc, kvs = mem.sb("kv", [P, 2, 2, D]), mem.sb("kvc", [P, 2, 2, ROT]), mem.sb("kvs", [P, 2, 2, ROT])
        brow = kv[0:1, 0].rearrange("p v d -> p (v d)")
        prod, junk = mem.sb("prod", [P, 2, D]), mem.ps("junk", [P, D])
        sq, nrm, rn, rr = mem.sb("sq", [P, 2, 2]), mem.sb("nrm", [P, 2, 2]), mem.sb("rn", [P, 2, 2]), mem.sb("rr", [P, 2, 1])
        asum, afac = mem.sb("asum", [P, DC]), mem.sb("afac", [P, DC])
        ob = mem.sb("ob", [P, 2, D])
        tr = mem.ps("tr", [P, 2, D])
        kv_ps = mem.ps("kv", [P, 2, 2, D])
        a_ps = mem.ps("a", [P, 2, DC])
        names = ("w_in", "wo_in", "wide_rdy", "bk_rdy", "bk_kept", "whi_rdy", "wlo_rdy", "bn_rdy", "mv_rdy", "sd_rdy", "rs_rdy", "y_rdy",
                 "xy_rdy", "bn2_rdy", "mv2_rdy", "sd2_rdy", "rs2_rdy", "y2_rdy", "tr_rdy", "yT_rdy", "thi_rdy", "tlo_rdy",
                 "kv_rdy", "kv_kept", "cos_rdy", "sin_rdy", "rot_rdy", "sq_rdy", "nrm_rdy", "rn_rdy", "rr_rdy", "prod_rdy",
                 "a_rdy", "a_kept", "zero_rdy", "af_rdy", "aw_rdy", "m_rdy", "mraw_rdy", "mhi_rdy", "mlo_rdy", "b_rdy",
                 "b_kept", "ohi_rdy", "olo_rdy", "o_rdy", "o_half", "ob_rdy")
        sm = {n: mem.sem(n) for n in names}
        x_in, cs_in, o_st = (mem.sems(n, 2) for n in ("x_in", "cs_in", "o_st"))
        block = ctx.enter_context(nc.Block())

        def spans(eng, b, step):
            def one(s, k, n, head, last):
                step(s + b * NB, s, k, n + b * (NB // 2), head, last)

            for k in range(2):
                one(k, k, 0, True, False)
            with eng.Fori(1, NB // 2 - 1) as n:
                for k in range(2):
                    one(n * 2 + k, k, n, False, False)
            for k in range(2):
                one(NB - 2 + k, k, NB // 2 - 1, False, True)

        @block.sync
        def _(sp):
            def load(t, k):
                sp.dma_start(xb[:, k, :], x[bass.ds(t * P, P), :]).then_inc(x_in[k], 16)

            def load_angles(s, k):
                sp.dma_start(cs[:, k], angles[bass.ds(s * P, P), :, :]).then_inc(cs_in[k], 16)

            for k in range(2):
                sp.sem_inc(o_st[k], 16)
            load(0, 0)
            load(1, 1)
            for to, src in ((gam[:], gamma), (bet[:], beta), (bq[:], b_q), (brow, b_kv), (raw[:], w_kv)):
                sp.dma_start(to, src).then_inc(sm["w_in"], 16)
            for to, src in ((borow, b_out), (wq, w_qT), (wo, w_out)):
                sp.dma_start(to[:], src).then_inc(sm["wo_in"], 16)
            for b in range(B):
                for k in range(2):
                    load_angles(k, k)

                def first(t, s, k, i, head, last):
                    if not (last and b == B - 1):
                        sp.wait_ge(sm["xy_rdy"], t + 1)
                        load(t + 2, k)
                    if not (head and k == 0 or last and k == 1):
                        sp.wait_ge(sm["rot_rdy"], t * 2)
                        load_angles(s + 1, 1 - k)

                spans(sp, b, first)
                sp.wait_ge(sm["rot_rdy"], (b + 1) * NB * 2)

                def second(t, s, k, i, head, last):
                    sp.wait_ge(sm["ob_rdy"], t + 1)
                    sp.dma_start(x_out[bass.ds(t * P, P), :], ob[:, k, :]).then_inc(o_st[k], 16)

                spans(sp, b, second)
            for k in range(2):
                sp.wait_ge(o_st[k], 16 * (NT // 2 + 1))

        @block.tensor
        def _(pe):
            pe.sem_inc(sm["yT_rdy"], 2)
            pe.sem_inc(sm["kv_kept"], 2)
            pe.sem_inc(sm["a_kept"], 2)
            pe.sem_inc(sm["o_half"], 2)
            pe.wait_ge(sm["wide_rdy"], 2 * DC)
            pe.wait_ge(sm["w_in"], 80)
            for h in range(2):
                for c in range(DC):
                    pe.matmul(kv_ps[:, 0, h, :], bet_w[:, c, :], raw[:, c, h * D:(h + 1) * D], start=(c == 0), stop=False)
                ins = pe.matmul(kv_ps[:, 0, h, :], const["ones"][0:1, :], brow[:, h * D:(h + 1) * D], start=False, stop=True)
            ins.then_inc(sm["bk_rdy"], 1)

            def turn(t, k):
                pe.wait_ge(sm["y2_rdy"], t + 1)
                pe.wait_ge(sm["yT_rdy"], t + 1)
                for c in range(DC):
                    ins = pe.transpose(tr[:, k, c * P:(c + 1) * P], y2[:, k, c * P:(c + 1) * P], const["ident"][:])
                ins.then_inc(sm["tr_rdy"], 1)

            def keysvalues(t, k):
                pe.wait_ge(sm["tlo_rdy"], t + 1)
                pe.wait_ge(sm["kv_kept"], t + 1)
                for h in range(2):
                    for c in range(DC):
                        w = (wk_hi[:, c, h * D:(h + 1) * D], wk_lo[:, c, h * D:(h + 1) * D])
                        for n, (a, bb) in enumerate(products((t_hi[:, k, c * P:(c + 1) * P], t_lo[:, k, c * P:(c + 1) * P]), w)):
                            ins = pe.matmul(kv_ps[:, k, h, :], a, bb, start=(c == 0 and n == 0), stop=(c == DC - 1 and n == 2))
                ins.then_inc(sm["kv_rdy"], 1)

            def sums(t, k):
                pe.wait_ge(sm["prod_rdy"], t * 2 + 5)
                pe.wait_ge(sm["rr_rdy"], t + 1)
                pe.wait_ge(sm["a_kept"], t + 1)
                for c in range(DC):
                    ins = pe.matmul(a_ps[:, k, c:c + 1], prod[:, k, c * P:(c + 1) * P], rr[:, k, :], start=True, stop=True)
                ins.then_inc(sm["a_rdy"], 1)

            for b in range(B):
                if b:
                    pe.wait_ge(sm["o_half"], b * NB + 2)
                turn(b * NB, 0)
                if not b:
                    pe.wait_ge(sm["bk_kept"], 1)
                    pe.wait_ge(sm["wlo_rdy"], DC)
                keysvalues(b * NB, 0)
                turn(b * NB + 1, 1)

                def first(t, s, k, i, head, last):
                    if not last:
                        turn(t + 2, k)
                    if not (head and k == 0):
                        sums(t - 1, 1 - k)
                    if not (last and k == 1):
                        keysvalues(t + 1, 1 - k)

                spans(pe, b, first)
                sums((b + 1) * NB - 1, 1)
                pe.wait_ge(sm["wo_in"], 48)
                pe.wait_ge(sm["aw_rdy"], DC * (b + 1))
                pe.wait_ge(sm["kv_kept"], 2 + (b + 1) * NB)
                for m in range(DC):
                    for c in range(DC):
                        ins = pe.matmul(kv_ps[:, m // 2, m % 2, :], wq[:, c, m * P:(m + 1) * P], aw[:, c, :], start=(c == 0), stop=(c == DC - 1))
                    ins.then_inc(sm["m_rdy"], 1)
                for c in range(DC):
                    pe.matmul(tr[:, 0, :], bq_w[:, c, :], aw[:, c, :], start=(c == 0), stop=False)
                for m in range(DC):
                    pe.wait_ge(sm["mraw_rdy"], DC * b + m + 1)
                    pe.matmul(tr[:, 0, :], bet_w[:, m, :], m_raw[:, m, :], start=False, stop=False)
                pe.matmul(tr[:, 0, :], const["ones"][0:1, :], borow[:], start=False, stop=True).then_inc(sm["b_rdy"], 1)
                pe.wait_ge(sm["mlo_rdy"], DC * (b + 1))
                pe.wait_ge(sm["b_kept"], b + 1)

                def second(t, s, k, i, head, last):
                    pe.wait_ge(sm["olo_rdy"], t + 1)
                    pe.wait_ge(sm["o_half"], t + 1)
                    for c in range(DC):
                        for n, (a, bb) in enumerate(products((t_hi[:, k, c * P:(c + 1) * P], t_lo[:, k, c * P:(c + 1) * P]), (m_hi[:, c, :], m_lo[:, c, :]))):
                            ins = pe.matmul(tr[:, k, :], a, bb, start=(c == 0 and n == 0), stop=(c == DC - 1 and n == 2))
                    ins.then_inc(sm["o_rdy"], 1)

                spans(pe, b, second)

        @block.gpsimd
        def _(pool):
            pool.sem_inc(sm["prod_rdy"], 3)

            def total(t, s, k):
                pool.wait_ge(sm["y_rdy"], t + 1)
                pool.tensor_tensor(xy[:, bass.ds(s, 1), :], xb[:, k, :].unsqueeze(1), yb[:, k, :].unsqueeze(1), ALU.add).then_inc(sm["xy_rdy"], 1)

            for b in range(B):
                if b:
                    pool.wait_ge(sm["ob_rdy"], b * NB)
                total(b * NB, 0, 0)
                total(b * NB + 1, 1, 1)

                def first(t, s, k, i, head, last):
                    if not last:
                        total(t + 2, s + 2, k)
                    pool.wait_ge(sm["kv_kept"], t + 3)
                    pool.wait_ge(cs_in[k], i * 16 + 16)
                    pool.wait_ge(sm["prod_rdy"], t * 2 + 1)
                    pairs = kv[:, k, :, 0:ROT].rearrange("p v (d two) -> p v d two", two=2)
                    c_pairs = kvc[:, k].rearrange("p v (d two) -> p v d two", two=2)
                    s_pairs = kvs[:, k].rearrange("p v (d two) -> p v d two", two=2)
                    for e in range(2):
                        cosine, sine = (spread(cs[:, k, n, :], 2, 1) for n in range(2))
                        pool.tensor_tensor(c_pairs[:, :, :, e], pairs[:, :, :, e], cosine, ALU.mult).then_inc(sm["cos_rdy"], 1)
                        pool.tensor_tensor(s_pairs[:, :, :, e], pairs[:, :, :, 1 - e], sine, ALU.mult).then_inc(sm["sin_rdy"], 1)
                    pool.wait_ge(sm["cos_rdy"], t * 2 + 2)
                    pool.wait_ge(sm["sin_rdy"], t * 2 + 2)
                    pool.tensor_tensor(c_pairs[:, :, :, 0], c_pairs[:, :, :, 0], s_pairs[:, :, :, 0], ALU.subtract).then_inc(sm["rot_rdy"], 1)
                    pool.tensor_tensor(c_pairs[:, :, :, 1], c_pairs[:, :, :, 1], s_pairs[:, :, :, 1], ALU.add).then_inc(sm["rot_rdy"], 1)

                spans(pool, b, first)

        @block.scalar
        def _(act):
            def root(t):
                act.wait_ge(sm["mv_rdy"], t + 1)
                act.activation(sd[:], mv[:, 1:2], ACT.Sqrt, bias=const["eps"][:]).then_inc(sm["sd_rdy"], 1)

            def root2(t):
                act.wait_ge(sm["mv2_rdy"], t + 1)
                act.activation(sd2[:], mv2[:, 1:2], ACT.Sqrt, bias=const["eps"][:]).then_inc(sm["sd2_rdy"], 1)

            def parts(t, s, k):
                act.wait_ge(sm["tr_rdy"], t + 1)
                act.activation(t_hi[:, k, :], tr[:, k, :], ACT.Copy).then_inc(sm["thi_rdy"], 1)
                act.activation(yT[:, bass.ds(s, 1), :], tr[:, k, :].unsqueeze(1), ACT.Copy).then_inc(sm["yT_rdy"], 1)

            for b in range(B):
                root(b * NB)
                root2(b * NB)
                root(b * NB + 1)
                parts(b * NB, 0, 0)
                root2(b * NB + 1)

                def first(t, s, k, i, head, last):
                    if not last:
                        root(t + 2)
                        root2(t + 2)
                        if head and k == 0:
                            parts(t + 1, 1, 1)
                        parts(t + 2, s + 2, k)
                    act.wait_ge(sm["kv_kept"], t + 3)
                    for h in range(2):
                        act.activation(junk[:], kv[:, k, h, :], ACT.Square, accum_out=sq[:, k, h:h + 1]).then_inc(sm["sq_rdy"], 1)
                        act.wait_ge(sm["sq_rdy"], t * 2 + (h + 1))
                    act.activation(nrm[:, k, :], sq[:, k, :], ACT.Sqrt).then_inc(sm["nrm_rdy"], 1)

                spans(act, b, first)
                for m in range(DC):
                    act.wait_ge(sm["m_rdy"], b * DC + m + 1)
                    act.activation(m_raw[:, m, :], kv_ps[:, m // 2, m % 2, :], ACT.Copy).then_inc(sm["mraw_rdy"], 1)
                act.wait_ge(sm["yT_rdy"], (b + 1) * NB + 2)

                def second(t, s, k, i, head, last):
                    if head:
                        act.wait_ge(sm["kv_rdy"], (b + 1) * NB)
                    else:
                        act.wait_ge(sm["o_rdy"], t - 1)
                    act.activation(t_hi[:, k, :].unsqueeze(1), yT[:, bass.ds(s, 1), :], ACT.Copy).then_inc(sm["ohi_rdy"], 1)

                spans(act, b, second)

        @block.vector
        def _(dve):
            def aggregate(stats, out, done, signal, t):
                dve.wait_ge(sm[done], t + 1)
                dve.tensor_copy(pause[:], const["eps"][:])
                dve.bn_aggr(out[:], stats[:]).then_inc(sm[signal], 1)

            def stats(t, k, i):
                dve.wait_ge(x_in[k], i * 16 + 16)
                dve.bn_stats(bn[:], xb[:, k, :]).then_inc(sm["bn_rdy"], 1)
                aggregate(bn, mv, "bn_rdy", "mv_rdy", t)

            def norm(t, k):
                dve.wait_ge(sm["sd_rdy"], t + 1)
                dve.reciprocal(rstd[:], sd[:]).then_inc(sm["rs_rdy"], 1)
                dve.wait_ge(sm["rs_rdy"], t + 1)
                dve.tensor_scalar(yb[:, k, :], xb[:, k, :], mv[:, 0:1], rstd[:], ALU.subtract, ALU.mult).then_inc(sm["y_rdy"], 1)
                dve.wait_ge(sm["y_rdy"], t + 1)
                dve.bn_stats(bn2[:], yb[:, k, :]).then_inc(sm["bn2_rdy"], 1)
                aggregate(bn2, mv2, "bn2_rdy", "mv2_rdy", t)

            def norm2(t, k):
                dve.wait_ge(sm["sd2_rdy"], t + 1)
                dve.reciprocal(rstd2[:], sd2[:]).then_inc(sm["rs2_rdy"], 1)
                dve.wait_ge(sm["rs2_rdy"], t + 1)
                dve.tensor_scalar(y2[:, k, :], yb[:, k, :], mv2[:, 0:1], rstd2[:], ALU.subtract, ALU.mult).then_inc(sm["y2_rdy"], 1)

            def low_part(t, s, k):
                dve.wait_ge(sm["thi_rdy"], t + 1)
                dve.wait_ge(sm["yT_rdy"], t + 3)
                dve.tensor_tensor(t_lo[:, k, :].unsqueeze(1), yT[:, bass.ds(s, 1), :], t_hi[:, k, :].bitcast(F32).unsqueeze(1),
                                  ALU.subtract).then_inc(sm["tlo_rdy"], 1)

            def take_sums(t, k):
                dve.wait_ge(sm["a_rdy"], t + 1)
                dve.wait_ge(sm["a_kept"], t + 2)
                dve.tensor_tensor(asum[:], asum[:], a_ps[:, k, :], ALU.add).then_inc(sm["a_kept"], 1)

            def weights():
                dve.wait_ge(sm["w_in"], 80)
                for to, src in ((bet_w, bet), (bq_w, bq)):
                    for c in range(DC):
                        dve.tensor_scalar(to[:, c, :], const["ones"][:], src[:, c:c + 1], None, ALU.mult).then_inc(sm["wide_rdy"], 1)
                for c in range(DC):
                    dve.tensor_scalar(wk_hi[:, c, :], raw[:, c, :], gam[:, c:c + 1], None, ALU.mult).then_inc(sm["whi_rdy"], 1)
                for c in range(DC):
                    dve.wait_ge(sm["whi_rdy"], c + 1)
                    dve.scalar_tensor_tensor(wk_lo[:, c, :], raw[:, c, :], gam[:, c:c + 1], wk_hi[:, c, :].bitcast(F32), ALU.mult, ALU.subtract).then_inc(sm["wlo_rdy"], 1)
                dve.wait_ge(sm["bk_rdy"], 1)
                dve.tensor_copy(bkv[:], kv_ps[:, 0]).then_inc(sm["bk_kept"], 1)

            for b in range(B):
                dve.memset(asum[:], 0.0).then_inc(sm["zero_rdy"], 1)
                stats(b * NB, 0, b * (NB // 2))
                norm(b * NB, 0)
                norm2(b * NB, 0)
                stats(b * NB + 1, 1, b * (NB // 2))
                if b == 0:
                    weights()
                low_part(b * NB, 0, 0)
                norm(b * NB + 1, 1)
                norm2(b * NB + 1, 1)

                def factor(t, k, first):
                    if first:
                        dve.wait_ge(sm["zero_rdy"], b + 1)
                    else:
                        take_sums(t - 1, 1 - k)
                    dve.wait_ge(sm["nrm_rdy"], t + 1)
                    dve.reciprocal(rn[:, k, :], nrm[:, k, :]).then_inc(sm["rn_rdy"], 1)
                    dve.tensor_tensor(prod[:, k, ROT:D], kv[:, k, 0, ROT:D], kv[:, k, 1, ROT:D], ALU.mult).then_inc(sm["prod_rdy"], 1)
                    dve.wait_ge(sm["rn_rdy"], t + 1)
                    dve.tensor_tensor(rr[:, k, :], rn[:, k, 0:1], rn[:, k, 1:2], ALU.mult).then_inc(sm["rr_rdy"], 1)

                def rotated(t, k):
                    dve.wait_ge(sm["rot_rdy"], t * 2 + 2)
                    dve.tensor_tensor(prod[:, k, 0:ROT], kvc[:, k, 0, :], kvc[:, k, 1, :], ALU.mult).then_inc(sm["prod_rdy"], 1)

                def first(t, s, k, i, head, last):
                    started = not (head and k == 0)
                    if not last:
                        stats(t + 2, k, i + 1)
                    if not (last and k == 1) and started:
                        low_part(t + 1, s + 1, 1 - k)
                    if not last:
                        norm(t + 2, k)
                    if started:
                        factor(t - 1, 1 - k, head and k == 1)
                    if not last:
                        norm2(t + 2, k)
                    if started:
                        rotated(t - 1, 1 - k)
                    else:
                        low_part(t + 1, s + 1, 1 - k)
                    dve.wait_ge(sm["kv_rdy"], t + 1)
                    dve.tensor_tensor(kv[:, k], kv_ps[:, k], bkv[:], ALU.add).then_inc(sm["kv_kept"], 1)
                spans(dve, b, first)
                factor((b + 1) * NB - 1, 1, False)
                rotated((b + 1) * NB - 1, 1)
                take_sums((b + 1) * NB - 1, 1)
                dve.wait_ge(sm["a_kept"], (b + 1) * NB + 2)
                dve.tensor_scalar(afac[:], asum[:], 0.5, 0.5, ALU.mult, ALU.add).then_inc(sm["af_rdy"], 1)
                dve.wait_ge(sm["af_rdy"], b + 1)
                dve.wait_ge(sm["wo_in"], 48)
                for c in range(DC):
                    dve.tensor_scalar(aw[:, c, :], wo[:, c, :], afac[:, c:c + 1], None, ALU.mult).then_inc(sm["aw_rdy"], 1)
                for m in range(DC):
                    dve.wait_ge(sm["mraw_rdy"], b * DC + m + 1)
                    dve.tensor_scalar(m_hi[:, m, :], m_raw[:, m, :], gam[:, m:m + 1], None, ALU.mult).then_inc(sm["mhi_rdy"], 1)
                    dve.wait_ge(sm["mhi_rdy"], b * DC + m + 1)
                    dve.scalar_tensor_tensor(m_lo[:, m, :], m_raw[:, m, :], gam[:, m:m + 1], m_hi[:, m, :].bitcast(F32),
                                             ALU.mult, ALU.subtract).then_inc(sm["mlo_rdy"], 1)
                dve.wait_ge(sm["b_rdy"], b + 1)
                dve.tensor_copy(bo[:], tr[:, 0, :]).then_inc(sm["b_kept"], 1)
                dve.wait_ge(sm["b_kept"], b + 1)

                def part(t, s, k):
                    dve.wait_ge(sm["ohi_rdy"], t + 1)
                    dve.tensor_tensor(t_lo[:, k, :].unsqueeze(1), yT[:, bass.ds(s, 1), :], t_hi[:, k, :].bitcast(F32).unsqueeze(1),
                                      ALU.subtract).then_inc(sm["olo_rdy"], 1)

                part(b * NB, 0, 0)

                def second(t, s, k, i, head, last):
                    if not (last and k == 1):
                        part(t + 1, s + 1, 1 - k)
                    dve.wait_ge(sm["o_rdy"], t + 1)
                    dve.wait_ge(o_st[k], i * 16 + 16)
                    dve.tensor_tensor(ob[:, k, :], tr[:, k, :], bo[:], ALU.add).then_inc(sm["o_half"], 1)
                    dve.wait_ge(sm["o_half"], t + 3)
                    dve.tensor_tensor(ob[:, k, :].unsqueeze(1), ob[:, k, :].unsqueeze(1), xy[:, bass.ds(s, 1), :], ALU.add).then_inc(sm["ob_rdy"], 1)

                spans(dve, b, second)


def build(nc, a, out):
    def scratch(name, shape):
        return nc.dram_tensor(name, shape, F32, kind="Internal").ap()

    x = [a["x"]] + [scratch(f"x{n}", (T, D)) for n in range(1, 6)]
    yn, ys = scratch("yn", (T, D)), scratch("ys", (SLOTS, D))
    q_parts = scratch("q_parts", (2, HEADS * HD, T))
    with ExitStack() as ctx:
        mem = Memory(nc, ctx, "all")
        const = {"ident": mem.sb("ident", [P, P]), "before": mem.sb("before", [P, P]), "ones": mem.sb("ones", [P, P]), "eps": mem.sb("eps", [P, 1])}
        plan = {"slot": mem.sb("slot", [P, TOPK, NT], U32), "weight": mem.sb("weight", [P, TOPK, NT])}
        setup_stage(nc, const)

        def experts(n, src):
            with ExitStack() as weights:
                held = Memory(nc, weights, f"weights{n}")
                box = {"hi": held.sb("hi", [P, 2 * WPIECES * WPIECE], F32R), "lo": held.sb("lo", [P, 2 * WPIECES * WPIECE], F32R),
                       "raw": held.sb("raw", [P, 2, WPIECE])}
                tables = {"rows": held.sb("rows", [P, SLOT_TILES], U32), "tile": held.sb("tile", [1, 2, SLOT_TILES], I32),
                          "next": held.sb("next", [1, 4, LAG + SLOT_TILES], I32), "used": held.sb("used", [1, 1], I32), **plan}
                routing_stage(nc, f"route{n}", const, src, a["router_scale"], a["router_w"], a["expert_scale"], a["experts"], box, yn, tables)
                expert_stage(nc, f"expert{n}", const, yn, ys, a["experts"], box, tables)

        def ffn(n, src, joined_to, joined, to):
            ffn_stage(nc, f"ffn{n}", const, src, joined_to, joined, a["gate_w"], a["up_w"], a["down_w"], a["gate_s"], a["up_s"], a["down_s"], to)

        experts(0, x[0])
        with ExitStack() as attended:
            outputs = Memory(nc, attended, "attended")
            attn = outputs.sb("attn", [P, NT, 2, 2 * P])
            ow_hi, ow_lo = outputs.sb("ow_hi", [P, DC, D], F32R), outputs.sb("ow_lo", [P, DC, D], F32R)
            with ExitStack() as attention:
                held = Memory(nc, attention, "attention")
                kst, v = held.sb("kst", [P, T], F32R), held.sb("v", [P, NT, HD])
                projection_stage(nc, "project", const, x[0], x[1], (ys, plan), a["q_w"], a["k_w"], a["v_w"], q_parts, kst, v)
                attention_stage(nc, "attend", const, q_parts, kst, v, attn, a["o_w"], ow_hi, ow_lo)
            output_stage(nc, "output", const, attn, ow_hi, ow_lo, x[1], x[2])
        experts(1, x[2])
        ffn(0, x[2], x[3], (ys, plan), x[4])
        keyvalue_stage(nc, "keyvalue", const, x[4], a["kv_w"], a["qT_w"], a["out_w"], a["kv_b"], a["q_b"], a["out_b"],
                       a["gamma"], a["beta"], a["angles"], x[5])
        ffn(1, x[5], None, None, out)


def layout(np, i):
    def chunked(w):
        return w.reshape(w.shape[0] // P, P, -1).transpose(1, 0, 2)

    def column(v):
        return v.reshape(-1, P).T

    gate_up = i["L0_ffn_gating_einsum"].transpose(0, 3, 1, 2).reshape(E, DC, P, WPIECE).transpose(0, 2, 1, 3)
    down = i["L0_ffn_linear"].reshape(E, H // P // 2, 2, P, D).transpose(0, 3, 1, 2, 4).reshape(E, P, H // P // 2, WPIECE)
    w_in, b_in = i["L1_attn_W_in"], i["L1_attn_b_in"]
    inv_freq = np.float32(1.0) / np.float32(10000.0) ** (np.arange(0, ROT, 2, dtype=np.float32) / np.float32(ROT))
    turns = np.arange(S, dtype=np.float32)[:, None] * inv_freq[None, :]
    return {
        "x": i["L0_attn_x"].reshape(T, D),
        "router_scale": column(i["L0_ffn_router_scale"]), "router_w": chunked(i["L0_ffn_router_logits"]),
        "expert_scale": i["L0_ffn_per_expert_scale"], "experts": np.concatenate([gate_up, down], axis=2),
        "q_w": chunked(i["L0_attn_q_w"].T), "k_w": chunked(i["L0_attn_k_w"].T), "v_w": chunked(i["L0_attn_v_w"].T),
        "o_w": i["L0_attn_o_w"].T.reshape(2, HALF // 2, 2, HD, D).transpose(1, 3, 0, 2, 4).reshape(P, DC, D),
        "gate_w": chunked(i["L1_ffn_gate_w"].T), "up_w": chunked(i["L1_ffn_up_w"].T), "down_w": chunked(i["L1_ffn_down_w"].T),
        "gate_s": column(i["L1_ffn_gate_s"]), "up_s": column(i["L1_ffn_up_s"]), "down_s": i["L1_ffn_down_s"],
        "kv_w": chunked(w_in[:, D:]), "qT_w": chunked(w_in[:, :D].T), "out_w": chunked(i["L1_attn_W_out"]),
        "kv_b": b_in[None, D:], "q_b": column(b_in[:D]), "out_b": i["L1_attn_b_out"][None, :],
        "gamma": column(i["L1_attn_gamma"]), "beta": column(i["L1_attn_beta"]),
        "angles": np.stack([np.cos(turns), np.sin(turns)], axis=1),
    }


def kernel(**inputs):
    import numpy as np
    import concourse.bacc as bacc
    from concourse.bass_utils import run_bass_kernel_spmd

    nc = bacc.Bacc("TRN2", target_bir_lowering=False, num_devices=1)
    arrays = {n: np.ascontiguousarray(v) for n, v in layout(np, {n: np.asarray(v) for n, v in inputs.items()}).items()}
    drams = {n: nc.dram_tensor(f"{n}_dram", v.shape, mybir.dt.from_np(v.dtype), kind="ExternalInput").ap() for n, v in arrays.items()}
    out = nc.dram_tensor("out_dram", (T, D), F32, kind="ExternalOutput").ap()
    build(nc, drams, out)
    r = run_bass_kernel_spmd(nc, [{f"{n}_dram": v for n, v in arrays.items()}], core_ids=[0])
    return r.results[0]["out_dram"].reshape(B, S, D)
```
